# Optimizing a Trainium2 kernel written in Bass

```python
import numpy as np
import jax
import jax.numpy as jnp

def _softmax(x, axis=-1):
    return jax.nn.softmax(x, axis=axis)

def _gelu(x):
    return jax.nn.gelu(x, approximate=True)

def _silu(x):
    return jax.nn.silu(x)

def _sigmoid(x):
    return jax.nn.sigmoid(x)

def _layernorm(x, axis=-1, eps=1e-05):
    m = jnp.mean(x, axis=axis, keepdims=True)
    v = jnp.var(x, axis=axis, keepdims=True)
    return (x - m) / jnp.sqrt(v + eps)

def _scatter_add(tgt, idx, src, axis=0):
    return tgt.at[idx].add(src)

def _segment_sum(src, seg, n):
    return jax.ops.segment_sum(src, seg, n)
kernel_name = 'mk_gnn_resnorm_d4_gnn_r32_e0c849'

def setup_inputs(seed: int=0):
    np.random.seed(seed)
    _w = jnp.asarray

    def _rec_inputs():
        import jax
        import jax.numpy as jnp
        _gk = jax.random.key(seed)
        x = -8.776e-05 + 1 * jax.random.normal(jax.random.fold_in(_gk, 1), (625, 256), jnp.float32)
        _s = jax.random.randint(jax.random.fold_in(_gk, 2), (5000,), 0, 625, jnp.int32)
        _d = jax.random.randint(jax.random.fold_in(_gk, 3), (5000,), 0, 625, jnp.int32)
        _loop = jnp.arange(625, dtype=jnp.int32)
        src = jnp.concatenate([_s, _d, _loop])
        dst = jnp.concatenate([_d, _s, _loop])
        _o = jnp.argsort(dst, stable=True)
        src = src[_o]
        dst = dst[_o]
        edge_attr_256 = 5.93493e-05 + 1.00006 * jax.random.normal(jax.random.fold_in(_gk, 13), (10625, 256), jnp.float32)
        edge_attr_32 = 0.000268479 + 0.999861 * jax.random.normal(jax.random.fold_in(_gk, 14), (10625, 32), jnp.float32)
        return (x, src, dst, edge_attr_256, edge_attr_32)
    x, src, dst, edge_attr_256, edge_attr_32 = _rec_inputs()

    def _L0_gnn_setup():
        import jax, jax.numpy as jnp
        import numpy as np
        N_NODES = 625
        IN_FEATS = 256
        GCN_OUT = 256
        N_EDGES = 20000
        H_ENC = 10

        def lstm_unbatched(x, Wih, Whh, bih, bhh):
            H = Whh.shape[1]
            xW = x @ Wih.T + (bih + bhh)

            def step(carry, xt):
                h, c = carry
                gates = xt + h @ Whh.T
                i, f, g, o = jnp.split(gates, 4)
                c = jax.nn.sigmoid(f) * c + jax.nn.sigmoid(i) * jnp.tanh(g)
                h = jax.nn.sigmoid(o) * jnp.tanh(c)
                return ((h, c), h)
            init = (jnp.zeros((H,), x.dtype), jnp.zeros((H,), x.dtype))
            _, hs = jax.lax.scan(step, init, xW)
            return hs
        key = jax.random.key(seed)
        ks = jax.random.split(key, 16)

        def unif(k, shape, fan_in):
            b = 1.0 / np.sqrt(fan_in)
            return jax.random.uniform(k, shape, jnp.float32, -b, b)
        x = jax.random.normal(ks[0], (N_NODES, IN_FEATS), jnp.float32)
        src = jax.random.randint(ks[1], (N_EDGES,), 0, N_NODES, jnp.int64 if jax.config.jax_enable_x64 else jnp.int32)
        dst = jax.random.randint(ks[2], (N_EDGES,), 0, N_NODES, jnp.int64 if jax.config.jax_enable_x64 else jnp.int32)
        W_gcn = unif(ks[3], (GCN_OUT, IN_FEATS), IN_FEATS)
        b_gcn = unif(ks[4], (GCN_OUT,), IN_FEATS)
        Wih_e = unif(ks[5], (4 * H_ENC, GCN_OUT), H_ENC)
        Whh_e = unif(ks[6], (4 * H_ENC, H_ENC), H_ENC)
        bih_e = unif(ks[7], (4 * H_ENC,), H_ENC)
        bhh_e = unif(ks[8], (4 * H_ENC,), H_ENC)
        Wih_d = unif(ks[9], (4 * GCN_OUT, H_ENC), GCN_OUT)
        Whh_d = unif(ks[10], (4 * GCN_OUT, GCN_OUT), GCN_OUT)
        bih_d = unif(ks[11], (4 * GCN_OUT,), GCN_OUT)
        bhh_d = unif(ks[12], (4 * GCN_OUT,), GCN_OUT)
        return dict(x=x, src=src, dst=dst, W_gcn=W_gcn, b_gcn=b_gcn, Wih_e=Wih_e, Whh_e=Whh_e, bih_e=bih_e, bhh_e=bhh_e, Wih_d=Wih_d, Whh_d=Whh_d, bih_d=bih_d, bhh_d=bhh_d)
    _L0_gnn_all = _L0_gnn_setup()
    _L0_gnn_in = {k: v for k, v in _L0_gnn_all.items() if k in ('W_gcn', 'b_gcn', 'Wih_e', 'Whh_e', 'bih_e', 'bhh_e', 'Wih_d', 'Whh_d', 'bih_d', 'bhh_d')}
    del _L0_gnn_all

    def _L1_gnn_setup():
        import jax, jax.numpy as jnp
        import numpy as np
        N, E, D = (50000, 9375, 256)
        BN_EPS = 1e-05

        def _bn(z, gamma, beta, mean, var):
            return (z - mean) * jax.lax.rsqrt(var + BN_EPS) * gamma + beta
        key = jax.random.key(seed)
        ks = jax.random.split(key, 8)
        s = 1.0 / np.sqrt(D)
        return {'x': jax.random.normal(ks[0], (N, D), dtype=jnp.float32), 'edge_index': jax.random.randint(ks[1], (2, E), 0, N, dtype=jnp.int64), 'edge_attr': jax.random.normal(ks[2], (E, D), dtype=jnp.float32), 'W1': jax.random.normal(ks[3], (D, D), dtype=jnp.float32) * s, 'b1': jnp.zeros((D,), jnp.float32), 'W2': jax.random.normal(ks[4], (D, D), dtype=jnp.float32) * s, 'b2': jnp.zeros((D,), jnp.float32), 'bn1_gamma': jnp.ones((D,), jnp.float32), 'bn1_beta': jnp.zeros((D,), jnp.float32), 'bn1_mean': jnp.zeros((D,), jnp.float32), 'bn1_var': jnp.ones((D,), jnp.float32), 'bn2_gamma': jnp.ones((D,), jnp.float32), 'bn2_beta': jnp.zeros((D,), jnp.float32), 'bn2_mean': jnp.zeros((D,), jnp.float32), 'bn2_var': jnp.ones((D,), jnp.float32)}
    _L1_gnn_all = _L1_gnn_setup()
    _L1_gnn_in = {k: v for k, v in _L1_gnn_all.items() if k in ('W1', 'b1', 'W2', 'b2', 'bn1_gamma', 'bn1_beta', 'bn1_mean', 'bn1_var', 'bn2_gamma', 'bn2_beta', 'bn2_mean', 'bn2_var')}
    del _L1_gnn_all

    def _L2_gnn_setup():
        import jax, jax.numpy as jnp
        import numpy as np
        N, E = (50000, 25000)
        IN_DIM = 256
        OUT_DIM = 256
        H = 8
        D = OUT_DIM // H
        SCALE = D ** (-0.5)
        LN_EPS = 1e-05

        def _layernorm(x, g, b):
            mu = jnp.mean(x, axis=-1, keepdims=True)
            var = jnp.mean((x - mu) ** 2, axis=-1, keepdims=True)
            return (x - mu) * jax.lax.rsqrt(var + LN_EPS) * g + b
        key = jax.random.key(seed)
        ks = jax.random.split(key, 12)
        s = 1.0 / np.sqrt(IN_DIM)
        inp = {'x': jax.random.normal(ks[0], (N, IN_DIM), jnp.float32), 'edge_index': jax.random.randint(ks[1], (2, E), 0, N, jnp.int64), 'batch': jnp.zeros((N,), jnp.int64), 'Wq': jax.random.uniform(ks[2], (IN_DIM, OUT_DIM), jnp.float32, -s, s), 'Wk': jax.random.uniform(ks[3], (IN_DIM, OUT_DIM), jnp.float32, -s, s), 'Wv': jax.random.uniform(ks[4], (IN_DIM, OUT_DIM), jnp.float32, -s, s), 'Wo_w': jax.random.uniform(ks[5], (OUT_DIM, OUT_DIM), jnp.float32, -s, s), 'Wo_b': jnp.zeros((OUT_DIM,), jnp.float32), 'ln1_g': jnp.ones((OUT_DIM,), jnp.float32), 'ln1_b': jnp.zeros((OUT_DIM,), jnp.float32), 'ln2_g': jnp.ones((OUT_DIM,), jnp.float32), 'ln2_b': jnp.zeros((OUT_DIM,), jnp.float32), 'ffn_w1': jax.random.uniform(ks[6], (OUT_DIM, 2 * OUT_DIM), jnp.float32, -s, s), 'ffn_b1': jnp.zeros((2 * OUT_DIM,), jnp.float32), 'ffn_w2': jax.random.uniform(ks[7], (2 * OUT_DIM, OUT_DIM), jnp.float32, -s, s), 'ffn_b2': jnp.zeros((OUT_DIM,), jnp.float32)}
        return inp
    _L2_gnn_all = _L2_gnn_setup()
    _L2_gnn_in = {k: v for k, v in _L2_gnn_all.items() if k in ('Wq', 'Wk', 'Wv', 'Wo_w', 'Wo_b', 'ln1_g', 'ln1_b', 'ln2_g', 'ln2_b', 'ffn_w1', 'ffn_b1', 'ffn_w2', 'ffn_b2')}
    del _L2_gnn_all

    def _L3_gnn_setup():
        import jax, jax.numpy as jnp
        import numpy as np
        N, E, DIM, HEADS, EDIM, DFF = (625, 10000, 256, 8, 32, 1024)
        C = DIM // HEADS

        def _gatv2(x, src, dst, ea, Wl, Wr, We, att, b):
            n = x.shape[0]
            h, c = att.shape
            e = src.shape[0]
            cnt = jax.ops.segment_sum(jnp.ones((e,), x.dtype), dst, num_segments=n)
            loop_ea = jax.ops.segment_sum(ea, dst, num_segments=n) / jnp.maximum(cnt, 1.0)[:, None]
            loop = jnp.arange(n)
            s = jnp.concatenate([src, loop])
            d = jnp.concatenate([dst, loop])
            ea_all = jnp.concatenate([ea, loop_ea], axis=0)
            xl = (x @ Wl).reshape(n, h, c)
            xr = (x @ Wr).reshape(n, h, c)
            ee = (ea_all @ We).reshape(-1, h, c)
            z = jax.nn.leaky_relu(xl[s] + xr[d] + ee, 0.2)
            score = jnp.einsum('ehc,hc->eh', z, att)
            m = jax.ops.segment_max(score, d, num_segments=n)
            ex = jnp.exp(score - m[d])
            den = jax.ops.segment_sum(ex, d, num_segments=n)
            alpha = ex / den[d]
            out = jax.ops.segment_sum(alpha[:, :, None] * xl[s], d, num_segments=n)
            return out.reshape(n, h * c) + b

        def _bn(x, g, b, eps=1e-05):
            mu = x.mean(axis=0)
            var = ((x - mu) ** 2).mean(axis=0)
            return (x - mu) * jax.lax.rsqrt(var + eps) * g + b

        def _lrelu(x):
            return jax.nn.leaky_relu(x, 0.01)
        key = jax.random.key(seed)
        ks = jax.random.split(key, 16)
        sc = 0.05
        inp = {'nf': jax.random.normal(ks[0], (N, DIM), jnp.float32), 'ei': jax.random.randint(ks[1], (2, E), 0, N, dtype=jnp.int32), 'ew': jax.random.normal(ks[2], (E, EDIM), jnp.float32)}
        for i, pfx in enumerate(['g1', 'g2']):
            kk = jax.random.split(ks[3 + i], 5)
            inp[pfx + '_Wl'] = jax.random.normal(kk[0], (DIM, DIM), jnp.float32) * sc
            inp[pfx + '_Wr'] = jax.random.normal(kk[1], (DIM, DIM), jnp.float32) * sc
            inp[pfx + '_We'] = jax.random.normal(kk[2], (EDIM, DIM), jnp.float32) * sc
            inp[pfx + '_att'] = jax.random.normal(kk[3], (HEADS, C), jnp.float32) * sc
            inp[pfx + '_b'] = jnp.zeros((DIM,), jnp.float32)
        for i, pfx in enumerate(['n1', 'n2', 'n3']):
            inp[pfx + '_g'] = jnp.ones((DIM,), jnp.float32)
            inp[pfx + '_b'] = jnp.zeros((DIM,), jnp.float32)
        inp['ff_W1'] = jax.random.normal(ks[8], (DIM, DFF), jnp.float32) * sc
        inp['ff_b1'] = jnp.zeros((DFF,), jnp.float32)
        inp['ff_W2'] = jax.random.normal(ks[9], (DFF, DIM), jnp.float32) * sc
        inp['ff_b2'] = jnp.zeros((DIM,), jnp.float32)
        return inp
    _L3_gnn_all = _L3_gnn_setup()
    _L3_gnn_in = {k: v for k, v in _L3_gnn_all.items() if k in ('g1_Wl', 'g1_Wr', 'g1_We', 'g1_att', 'g1_b', 'g2_Wl', 'g2_Wr', 'g2_We', 'g2_att', 'g2_b', 'n1_g', 'n1_b', 'n2_g', 'n2_b', 'n3_g', 'n3_b', 'ff_W1', 'ff_b1', 'ff_W2', 'ff_b2')}
    del _L3_gnn_all
    return {'x': x, 'src': src, 'dst': dst, 'edge_attr_256': edge_attr_256, 'edge_attr_32': edge_attr_32, 'L0_gnn_W_gcn': _L0_gnn_in['W_gcn'], 'L0_gnn_b_gcn': _L0_gnn_in['b_gcn'], 'L0_gnn_Wih_e': _L0_gnn_in['Wih_e'], 'L0_gnn_Whh_e': _L0_gnn_in['Whh_e'], 'L0_gnn_bih_e': _L0_gnn_in['bih_e'], 'L0_gnn_bhh_e': _L0_gnn_in['bhh_e'], 'L0_gnn_Wih_d': _L0_gnn_in['Wih_d'], 'L0_gnn_Whh_d': _L0_gnn_in['Whh_d'], 'L0_gnn_bih_d': _L0_gnn_in['bih_d'], 'L0_gnn_bhh_d': _L0_gnn_in['bhh_d'], 'L1_gnn_W1': _L1_gnn_in['W1'], 'L1_gnn_b1': _L1_gnn_in['b1'], 'L1_gnn_W2': _L1_gnn_in['W2'], 'L1_gnn_b2': _L1_gnn_in['b2'], 'L1_gnn_bn1_gamma': _L1_gnn_in['bn1_gamma'], 'L1_gnn_bn1_beta': _L1_gnn_in['bn1_beta'], 'L1_gnn_bn1_mean': _L1_gnn_in['bn1_mean'], 'L1_gnn_bn1_var': _L1_gnn_in['bn1_var'], 'L1_gnn_bn2_gamma': _L1_gnn_in['bn2_gamma'], 'L1_gnn_bn2_beta': _L1_gnn_in['bn2_beta'], 'L1_gnn_bn2_mean': _L1_gnn_in['bn2_mean'], 'L1_gnn_bn2_var': _L1_gnn_in['bn2_var'], 'L2_gnn_Wq': _L2_gnn_in['Wq'], 'L2_gnn_Wk': _L2_gnn_in['Wk'], 'L2_gnn_Wv': _L2_gnn_in['Wv'], 'L2_gnn_Wo_w': _L2_gnn_in['Wo_w'], 'L2_gnn_Wo_b': _L2_gnn_in['Wo_b'], 'L2_gnn_ln1_g': _L2_gnn_in['ln1_g'], 'L2_gnn_ln1_b': _L2_gnn_in['ln1_b'], 'L2_gnn_ln2_g': _L2_gnn_in['ln2_g'], 'L2_gnn_ln2_b': _L2_gnn_in['ln2_b'], 'L2_gnn_ffn_w1': _L2_gnn_in['ffn_w1'], 'L2_gnn_ffn_b1': _L2_gnn_in['ffn_b1'], 'L2_gnn_ffn_w2': _L2_gnn_in['ffn_w2'], 'L2_gnn_ffn_b2': _L2_gnn_in['ffn_b2'], 'L3_gnn_g1_Wl': _L3_gnn_in['g1_Wl'], 'L3_gnn_g1_Wr': _L3_gnn_in['g1_Wr'], 'L3_gnn_g1_We': _L3_gnn_in['g1_We'], 'L3_gnn_g1_att': _L3_gnn_in['g1_att'], 'L3_gnn_g1_b': _L3_gnn_in['g1_b'], 'L3_gnn_g2_Wl': _L3_gnn_in['g2_Wl'], 'L3_gnn_g2_Wr': _L3_gnn_in['g2_Wr'], 'L3_gnn_g2_We': _L3_gnn_in['g2_We'], 'L3_gnn_g2_att': _L3_gnn_in['g2_att'], 'L3_gnn_g2_b': _L3_gnn_in['g2_b'], 'L3_gnn_n1_g': _L3_gnn_in['n1_g'], 'L3_gnn_n1_b': _L3_gnn_in['n1_b'], 'L3_gnn_n2_g': _L3_gnn_in['n2_g'], 'L3_gnn_n2_b': _L3_gnn_in['n2_b'], 'L3_gnn_n3_g': _L3_gnn_in['n3_g'], 'L3_gnn_n3_b': _L3_gnn_in['n3_b'], 'L3_gnn_ff_W1': _L3_gnn_in['ff_W1'], 'L3_gnn_ff_b1': _L3_gnn_in['ff_b1'], 'L3_gnn_ff_W2': _L3_gnn_in['ff_W2'], 'L3_gnn_ff_b2': _L3_gnn_in['ff_b2']}

def reference(x, src, dst, edge_attr_256, edge_attr_32, L0_gnn_W_gcn, L0_gnn_b_gcn, L0_gnn_Wih_e, L0_gnn_Whh_e, L0_gnn_bih_e, L0_gnn_bhh_e, L0_gnn_Wih_d, L0_gnn_Whh_d, L0_gnn_bih_d, L0_gnn_bhh_d, L1_gnn_W1, L1_gnn_b1, L1_gnn_W2, L1_gnn_b2, L1_gnn_bn1_gamma, L1_gnn_bn1_beta, L1_gnn_bn1_mean, L1_gnn_bn1_var, L1_gnn_bn2_gamma, L1_gnn_bn2_beta, L1_gnn_bn2_mean, L1_gnn_bn2_var, L2_gnn_Wq, L2_gnn_Wk, L2_gnn_Wv, L2_gnn_Wo_w, L2_gnn_Wo_b, L2_gnn_ln1_g, L2_gnn_ln1_b, L2_gnn_ln2_g, L2_gnn_ln2_b, L2_gnn_ffn_w1, L2_gnn_ffn_b1, L2_gnn_ffn_w2, L2_gnn_ffn_b2, L3_gnn_g1_Wl, L3_gnn_g1_Wr, L3_gnn_g1_We, L3_gnn_g1_att, L3_gnn_g1_b, L3_gnn_g2_Wl, L3_gnn_g2_Wr, L3_gnn_g2_We, L3_gnn_g2_att, L3_gnn_g2_b, L3_gnn_n1_g, L3_gnn_n1_b, L3_gnn_n2_g, L3_gnn_n2_b, L3_gnn_n3_g, L3_gnn_n3_b, L3_gnn_ff_W1, L3_gnn_ff_b1, L3_gnn_ff_W2, L3_gnn_ff_b2):
    import jax
    import jax.numpy as jnp

    def _L0_gnn_ref(x, src, dst, W_gcn, b_gcn, Wih_e, Whh_e, bih_e, bhh_e, Wih_d, Whh_d, bih_d, bhh_d):
        import jax, jax.numpy as jnp
        import numpy as np
        N_NODES = 625
        IN_FEATS = 256
        GCN_OUT = 256
        N_EDGES = 20000
        H_ENC = 10

        def lstm_unbatched(x, Wih, Whh, bih, bhh):
            H = Whh.shape[1]
            xW = x @ Wih.T + (bih + bhh)

            def step(carry, xt):
                h, c = carry
                gates = xt + h @ Whh.T
                i, f, g, o = jnp.split(gates, 4)
                c = jax.nn.sigmoid(f) * c + jax.nn.sigmoid(i) * jnp.tanh(g)
                h = jax.nn.sigmoid(o) * jnp.tanh(c)
                return ((h, c), h)
            init = (jnp.zeros((H,), x.dtype), jnp.zeros((H,), x.dtype))
            _, hs = jax.lax.scan(step, init, xW)
            return hs
        agg = jax.ops.segment_sum(x[src], dst, num_segments=N_NODES)
        h = jax.nn.relu(agg @ W_gcn.T + b_gcn)
        z = lstm_unbatched(h, Wih_e, Whh_e, bih_e, bhh_e)
        out = lstm_unbatched(z, Wih_d, Whh_d, bih_d, bhh_d)
        return out

    def _L1_gnn_ref(x, edge_index, edge_attr, W1, b1, W2, b2, bn1_gamma, bn1_beta, bn1_mean, bn1_var, bn2_gamma, bn2_beta, bn2_mean, bn2_var):
        import jax, jax.numpy as jnp
        import numpy as np
        N, E, D = (50000, 9375, 256)
        BN_EPS = 1e-05

        def _bn(z, gamma, beta, mean, var):
            return (z - mean) * jax.lax.rsqrt(var + BN_EPS) * gamma + beta
        src, dst = (edge_index[0], edge_index[1])
        msg = jax.nn.relu(x[src] + edge_attr)
        agg = jax.ops.segment_sum(msg, dst, num_segments=x.shape[0])
        conv_out = x + agg
        h = x + conv_out
        f = _bn(h, bn1_gamma, bn1_beta, bn1_mean, bn1_var)
        f = jax.nn.gelu(f @ W1.T + b1, approximate=False)
        f = f @ W2.T + b2
        return _bn(h + f, bn2_gamma, bn2_beta, bn2_mean, bn2_var)

    def _L2_gnn_ref(x, edge_index, batch, Wq, Wk, Wv, Wo_w, Wo_b, ln1_g, ln1_b, ln2_g, ln2_b, ffn_w1, ffn_b1, ffn_w2, ffn_b2):
        import jax, jax.numpy as jnp
        import numpy as np
        N, E = (50000, 25000)
        IN_DIM = 256
        OUT_DIM = 256
        H = 8
        D = OUT_DIM // H
        SCALE = D ** (-0.5)
        LN_EPS = 1e-05

        def _layernorm(x, g, b):
            mu = jnp.mean(x, axis=-1, keepdims=True)
            var = jnp.mean((x - mu) ** 2, axis=-1, keepdims=True)
            return (x - mu) * jax.lax.rsqrt(var + LN_EPS) * g + b
        n = x.shape[0]
        residual = x
        Q = (x @ Wq).reshape(n, H, D)
        K = (x @ Wk).reshape(n, H, D)
        V = (x @ Wv).reshape(n, H, D)
        src, dst = (edge_index[0], edge_index[1])
        scores = jnp.einsum('ehd,ehd->eh', Q[dst], K[src]) * SCALE
        attn_max = jnp.zeros((n, H), scores.dtype).at[dst].max(scores)
        w = jnp.exp(scores - attn_max[dst])
        attn_sum = jnp.zeros((n, H), w.dtype).at[dst].add(w)
        w = w / (attn_sum[dst] + 1e-08)
        msg = V[src] * w[:, :, None]
        out = jnp.zeros((n, H, D), msg.dtype).at[dst].add(msg)
        out = out.reshape(n, OUT_DIM) @ Wo_w + Wo_b
        out = _layernorm(residual + out, ln1_g, ln1_b)
        ffn = jax.nn.gelu(out @ ffn_w1 + ffn_b1, approximate=False) @ ffn_w2 + ffn_b2
        out = _layernorm(out + ffn, ln2_g, ln2_b)
        return out

    def _L3_gnn_ref(nf, ei, ew, g1_Wl, g1_Wr, g1_We, g1_att, g1_b, g2_Wl, g2_Wr, g2_We, g2_att, g2_b, n1_g, n1_b, n2_g, n2_b, n3_g, n3_b, ff_W1, ff_b1, ff_W2, ff_b2):
        import jax, jax.numpy as jnp
        import numpy as np
        N, E, DIM, HEADS, EDIM, DFF = (625, 10000, 256, 8, 32, 1024)
        C = DIM // HEADS

        def _gatv2(x, src, dst, ea, Wl, Wr, We, att, b):
            n = x.shape[0]
            h, c = att.shape
            e = src.shape[0]
            cnt = jax.ops.segment_sum(jnp.ones((e,), x.dtype), dst, num_segments=n)
            loop_ea = jax.ops.segment_sum(ea, dst, num_segments=n) / jnp.maximum(cnt, 1.0)[:, None]
            loop = jnp.arange(n)
            s = jnp.concatenate([src, loop])
            d = jnp.concatenate([dst, loop])
            ea_all = jnp.concatenate([ea, loop_ea], axis=0)
            xl = (x @ Wl).reshape(n, h, c)
            xr = (x @ Wr).reshape(n, h, c)
            ee = (ea_all @ We).reshape(-1, h, c)
            z = jax.nn.leaky_relu(xl[s] + xr[d] + ee, 0.2)
            score = jnp.einsum('ehc,hc->eh', z, att)
            m = jax.ops.segment_max(score, d, num_segments=n)
            ex = jnp.exp(score - m[d])
            den = jax.ops.segment_sum(ex, d, num_segments=n)
            alpha = ex / den[d]
            out = jax.ops.segment_sum(alpha[:, :, None] * xl[s], d, num_segments=n)
            return out.reshape(n, h * c) + b

        def _bn(x, g, b, eps=1e-05):
            mu = x.mean(axis=0)
            var = ((x - mu) ** 2).mean(axis=0)
            return (x - mu) * jax.lax.rsqrt(var + eps) * g + b

        def _lrelu(x):
            return jax.nn.leaky_relu(x, 0.01)
        src, dst = (ei[0], ei[1])
        h = nf + _lrelu(_bn(_gatv2(nf, src, dst, ew, g1_Wl, g1_Wr, g1_We, g1_att, g1_b), n1_g, n1_b))
        h = h + _lrelu(_bn(_gatv2(h, src, dst, ew, g2_Wl, g2_Wr, g2_We, g2_att, g2_b), n2_g, n2_b))
        ff = jax.nn.relu(h @ ff_W1 + ff_b1) @ ff_W2 + ff_b2
        h = h + _lrelu(_bn(ff, n3_g, n3_b))
        return h
    edge_index = jnp.stack([src, dst])
    batch0 = jnp.zeros((625,), jnp.int32)
    x = _layernorm(x + _L0_gnn_ref(x, src, dst, L0_gnn_W_gcn, L0_gnn_b_gcn, L0_gnn_Wih_e, L0_gnn_Whh_e, L0_gnn_bih_e, L0_gnn_bhh_e, L0_gnn_Wih_d, L0_gnn_Whh_d, L0_gnn_bih_d, L0_gnn_bhh_d), axis=-1)
    x = _layernorm(x + _L1_gnn_ref(x, edge_index, edge_attr_256, L1_gnn_W1, L1_gnn_b1, L1_gnn_W2, L1_gnn_b2, L1_gnn_bn1_gamma, L1_gnn_bn1_beta, L1_gnn_bn1_mean, L1_gnn_bn1_var, L1_gnn_bn2_gamma, L1_gnn_bn2_beta, L1_gnn_bn2_mean, L1_gnn_bn2_var), axis=-1)
    x = _layernorm(x + _L2_gnn_ref(x, edge_index, batch0, L2_gnn_Wq, L2_gnn_Wk, L2_gnn_Wv, L2_gnn_Wo_w, L2_gnn_Wo_b, L2_gnn_ln1_g, L2_gnn_ln1_b, L2_gnn_ln2_g, L2_gnn_ln2_b, L2_gnn_ffn_w1, L2_gnn_ffn_b1, L2_gnn_ffn_w2, L2_gnn_ffn_b2), axis=-1)
    x = _layernorm(x + _L3_gnn_ref(x, edge_index, edge_attr_32, L3_gnn_g1_Wl, L3_gnn_g1_Wr, L3_gnn_g1_We, L3_gnn_g1_att, L3_gnn_g1_b, L3_gnn_g2_Wl, L3_gnn_g2_Wr, L3_gnn_g2_We, L3_gnn_g2_att, L3_gnn_g2_b, L3_gnn_n1_g, L3_gnn_n1_b, L3_gnn_n2_g, L3_gnn_n2_b, L3_gnn_n3_g, L3_gnn_n3_b, L3_gnn_ff_W1, L3_gnn_ff_b1, L3_gnn_ff_W2, L3_gnn_ff_b2), axis=-1)
    return x

_drawn_inputs = setup_inputs


def setup_inputs(seed=0):
    import zlib

    import numpy as np

    out = dict(_drawn_inputs(seed))
    spreads = {'L1_gnn_b1': (0.0, 0.8),
     'L1_gnn_b2': (0.0, 0.675),
     'L1_gnn_bn1_gamma': (1.0, 0.2),
     'L1_gnn_bn1_beta': (0.0, 0.8),
     'L1_gnn_bn1_mean': (0.0, 0.8),
     'L1_gnn_bn1_var': (1.0, 0.2),
     'L1_gnn_bn2_gamma': (1.0, 0.2),
     'L1_gnn_bn2_beta': (0.0, 0.8),
     'L1_gnn_bn2_mean': (0.0, 0.74),
     'L1_gnn_bn2_var': (1.0, 0.2),
     'L2_gnn_Wo_b': (0.0, 0.1),
     'L2_gnn_ln1_g': (1.0, 0.2),
     'L2_gnn_ln1_b': (0.0, 0.1),
     'L2_gnn_ln2_g': (1.0, 0.2),
     'L2_gnn_ln2_b': (0.0, 0.1),
     'L2_gnn_ffn_b1': (0.0, 0.361),
     'L2_gnn_ffn_b2': (0.0, 0.1),
     'L3_gnn_g1_b': (0.0, 0.8),
     'L3_gnn_g2_b': (0.0, 0.8),
     'L3_gnn_n1_g': (1.0, 0.2),
     'L3_gnn_n1_b': (0.0, 0.1),
     'L3_gnn_n2_g': (1.0, 0.2),
     'L3_gnn_n2_b': (0.0, 0.1),
     'L3_gnn_n3_g': (1.0, 0.2),
     'L3_gnn_n3_b': (0.0, 0.1),
     'L3_gnn_ff_b1': (0.0, 0.359),
     'L3_gnn_ff_b2': (0.0, 0.8)}
    factors = {'L0_gnn_W_gcn': 5.746,
     'L0_gnn_b_gcn': 8.0,
     'L0_gnn_Wih_e': 2.908,
     'L0_gnn_Whh_e': 8.0,
     'L0_gnn_bih_e': 8.0,
     'L0_gnn_bhh_e': 8.0,
     'L0_gnn_Wih_d': 3.353,
     'L0_gnn_Whh_d': 4.31,
     'L2_gnn_Wq': 7.201,
     'L2_gnn_Wk': 6.977,
     'L3_gnn_g1_Wr': 3.609,
     'L3_gnn_g1_We': 3.181,
     'L3_gnn_g2_Wr': 3.948,
     'L3_gnn_g2_We': 4.13}
    for name, (base, spread) in spreads.items():
        noise = np.random.default_rng([zlib.crc32(name.encode()), seed]).standard_normal(out[name].shape)
        drawn = base * np.exp(spread * noise) if base else spread * noise
        out[name] = jnp.asarray(drawn.astype(out[name].dtype))
    for name, factor in factors.items():
        out[name] = (out[name] * factor).astype(out[name].dtype)
    return out
```

```python
from contextlib import ExitStack

import concourse.bass as bass
from concourse import mybir

F32 = mybir.dt.float32
F16 = mybir.dt.float16
BF16 = mybir.dt.bfloat16
I32 = mybir.dt.int32
ALU = mybir.AluOpType
ACT = mybir.ActivationFunctionType
AX = mybir.AxisListType.X

P = 128
N = 625
Q = 125
NC = N // Q
E = 10625
T = E // Q
F = 256
KF = F // P
EF = 32
HE = 10
HEADS, HD = 8, 32
EPS = 1e-5
PIECES = ((0, 512), (512, N))
U = 5

H_SCALE = 2.0 ** 8
W_SCALE = 2.0 ** 6
G_SCALE = H_SCALE * W_SCALE
XE_MAX = 60000.0
STEPS = 630
LAG = 2
KS = 106

VECS = ['L0_gnn_b_gcn', 'L1_gnn_b1', 'L1_gnn_b2', 'L1_gnn_bn1_gamma', 'L1_gnn_bn1_beta', 'L1_gnn_bn1_mean',
        'L1_gnn_bn1_var', 'L1_gnn_bn2_gamma', 'L1_gnn_bn2_beta', 'L1_gnn_bn2_mean', 'L1_gnn_bn2_var',
        'L2_gnn_Wo_b', 'L2_gnn_ln1_g', 'L2_gnn_ln1_b', 'L2_gnn_ln2_g', 'L2_gnn_ln2_b', 'L2_gnn_ffn_b1',
        'L2_gnn_ffn_b2', 'L3_gnn_g1_b', 'L3_gnn_g2_b', 'L3_gnn_n1_g', 'L3_gnn_n1_b', 'L3_gnn_n2_g',
        'L3_gnn_n2_b', 'L3_gnn_n3_g', 'L3_gnn_n3_b', 'L3_gnn_ff_b1', 'L3_gnn_ff_b2']
VEC_BLOCKS = {name: {'L2_gnn_ffn_b1': 4, 'L3_gnn_ff_b1': 8}.get(name, 2) for name in VECS}
VEC_AT = {name: sum(VEC_BLOCKS[v] for v in VECS[:i]) for i, name in enumerate(VECS)}
N_VEC = sum(VEC_BLOCKS.values())


class Memory:
    pass


class Phase:

    used = []

    def __init__(self, nc, name):
        self.nc, self.name, self.ctx = nc, f"{name}{nc.next_id()}", ExitStack()

    def __enter__(self):
        self.ctx.__enter__()
        return self

    def __exit__(self, *exc):
        return self.ctx.__exit__(*exc)

    def sb(self, name, shape, dt=F32):
        return self.ctx.enter_context(self.nc.sbuf_tensor(f"{self.name}_{name}", shape, dt))

    def ps(self, name, shape):
        return self.ctx.enter_context(self.nc.psum_tensor(f"{self.name}_{name}", shape, F32))

    def sem(self, name):
        handle = self.nc.alloc_semaphore(f"{self.name}_{name}")
        Phase.used.append(handle)
        return handle

    def block(self):
        return self.ctx.enter_context(self.nc.Block())


def recycle(nc):
    nc.all_engine_barrier()
    nc.clear_and_free_semaphores(list(Phase.used))
    nc.all_engine_barrier()
    Phase.used.clear()


def vec(mem, name):
    at = VEC_AT[name]
    return mem.vecs[:, at:at + VEC_BLOCKS[name]]


def load(nc, pairs):
    with Phase(nc, "load") as ph:
        loaded = ph.sem("loaded")
        block = ph.block()

        @block.sync
        def _(sp):
            for to, of in pairs[0::2]:
                sp.dma_start(to, of).then_inc(loaded, 16)
            sp.wait_ge(loaded, 16 * len(pairs))

        @block.scalar
        def _(act):
            for to, of in pairs[1::2]:
                act.dma_start(to, of).then_inc(loaded, 16)


def dense(nc, x, w, out, k_blocks, m_blocks, func, bias=None, scale=1.0):
    with Phase(nc, "dense") as ph:
        product = ph.ps("product", [P, 2, 1024])
        product_ready, evacuated = ph.sem("product_ready"), ph.sem("evacuated")
        block = ph.block()

        @block.tensor
        def _(pe):
            for m in range(m_blocks):
                if m >= 2:
                    pe.wait_ge(evacuated, m - 1)
                for a, b in PIECES:
                    for k in range(k_blocks):
                        last = pe.matmul(product[:, m % 2, a:b], w[:, k, m * P:(m + 1) * P], x[:, k, a:b],
                                         start=(k == 0), stop=(k == k_blocks - 1))
                last.then_inc(product_ready, 1)

        @block.scalar
        def _(act):
            for m in range(m_blocks):
                act.wait_ge(product_ready, m + 1)
                act.activation(out[:, m, 0:N], product[:, m % 2, 0:N], func, scale=scale,
                               bias=0.0 if bias is None else bias[:, m:m + 1]).then_inc(evacuated, 1)


def node_major(nc, x, w, out, cols):
    with Phase(nc, "nodes") as ph:
        product = ph.ps("product", [P, 2, 512])
        product_ready, evacuated = ph.sem("product_ready"), ph.sem("evacuated")
        block = ph.block()

        @block.tensor
        def _(pe):
            for c in range(NC):
                if c >= 2:
                    pe.wait_ge(evacuated, c - 1)
                for k in range(KF):
                    last = pe.matmul(product[0:Q, c % 2, 0:cols], x[:, k, c * Q:(c + 1) * Q], w[:, k, 0:cols],
                                     start=(k == 0), stop=(k == KF - 1))
                last.then_inc(product_ready, 1)

        @block.vector
        def _(dve):
            for c in range(NC):
                dve.wait_ge(product_ready, c + 1)
                dve.tensor_copy(out[:, c, 0:cols], product[0:Q, c % 2, 0:cols]).then_inc(evacuated, 1)


def layer_norm(nc, mem, x, out, gain=None, shift=None):
    with Phase(nc, "ln") as ph:
        mean, var = ph.ps("mean", [P, 1024]), ph.ps("var", [P, 1024])
        centred, squares = ph.sb("centred", [P, KF, N]), ph.sb("squares", [P, KF, N])
        rstd = ph.sb("rstd", [P, N])
        mean_ready, centred_ready, squares_ready = ph.sem("mean_ready"), ph.sem("centred_ready"), ph.sem("squares_ready")
        var_ready, std_ready, rstd_ready, normed = ph.sem("var_ready"), ph.sem("std_ready"), ph.sem("rstd_ready"), ph.sem("normed")
        block = ph.block()

        @block.tensor
        def _(pe):
            for a, b in PIECES:
                for k in range(KF):
                    last = pe.matmul(mean[:, a:b], mem.averager[:], x[:, k, a:b], start=(k == 0), stop=(k == KF - 1))
            last.then_inc(mean_ready, 1)
            pe.wait_ge(squares_ready, KF)
            for a, b in PIECES:
                for k in range(KF):
                    last = pe.matmul(var[:, a:b], mem.averager[:], squares[:, k, a:b], start=(k == 0), stop=(k == KF - 1))
            last.then_inc(var_ready, 1)

        @block.scalar
        def _(act):
            for k in range(KF):
                act.wait_ge(centred_ready, k + 1)
                act.activation(squares[:, k, :], centred[:, k, :], ACT.Square).then_inc(squares_ready, 1)
            act.wait_ge(var_ready, 1)
            act.activation(rstd[:], var[:, 0:N], ACT.Sqrt, bias=mem.eps[:, 0:1]).then_inc(std_ready, 1)

        @block.vector
        def _(dve):
            dve.wait_ge(mean_ready, 1)
            for k in range(KF):
                dve.tensor_tensor(centred[:, k, :], x[:, k, :], mean[:, 0:N], ALU.subtract).then_inc(centred_ready, 1)
            dve.wait_ge(std_ready, 1)
            dve.reciprocal(rstd[:], rstd[:]).then_inc(rstd_ready, 1)
            dve.wait_ge(rstd_ready, 1)
            dve.wait_ge(centred_ready, KF)
            for k in range(KF):
                dve.tensor_tensor(out[:, k, :], centred[:, k, :], rstd[:], ALU.mult).then_inc(normed, 1)
            if gain is not None:
                for k in range(KF):
                    dve.wait_ge(normed, k + 1)
                    dve.tensor_scalar(out[:, k, :], out[:, k, :], gain[:, k:k + 1], shift[:, k:k + 1], ALU.mult, ALU.add)


def setup(nc, mem, d):
    load(nc, [(mem.src[:], d["src"]), (mem.dst[:], d["dst"]), (mem.averager[:], d["averager"]), (mem.vecs[:], d["vecs"]),
              (mem.x[:], d["x"])])
    with Phase(nc, "count") as ph:
        node_i = ph.sb("node_i", [P, N], I32)
        node = ph.sb("node", [P, N], F16)
        src_f, dst_f = ph.sb("src_f", [P, T]), ph.sb("dst_f", [P, T])
        src_hot = ph.sb("src_hot", [P, U, N], F16)
        low = [ph.ps(f"low{c}", [P, 512]) for c in range(NC)]
        high = ph.ps("high", [P, 2, 512])
        REST = N - 512
        iota_ready, node_ready, index_ready = ph.sem("iota_ready"), ph.sem("node_ready"), ph.sem("index_ready")
        hot_ready, counted, zeroed = ph.sem("hot_ready"), ph.sem("counted"), ph.sem("zeroed")
        block = ph.block()

        def rest(c):
            return high[0:Q, c // 4, (c % 4) * REST:(c % 4 + 1) * REST]

        @block.gpsimd
        def _(pool):
            pool.iota(node_i[:], pattern=[[1, N]], base=0, channel_multiplier=0).then_inc(iota_ready, 1)

        @block.vector
        def _(dve):
            dve.memset(mem.eps[:], EPS)
            for c in range(NC):
                dve.memset(low[c][:], 0.0).then_inc(zeroed, 1)
            dve.memset(high[:], 0.0).then_inc(zeroed, 1)
            dve.tensor_copy(src_f[0:Q, :], mem.src[:]).then_inc(index_ready, 1)
            dve.tensor_copy(dst_f[0:Q, :], mem.dst[:]).then_inc(index_ready, 1)
            dve.wait_ge(iota_ready, 1)
            dve.tensor_copy(node[:], node_i[:]).then_inc(node_ready, 1)
            dve.wait_ge(node_ready, 1)
            dve.wait_ge(index_ready, 2)
            with dve.Fori(0, T // U) as i:
                t = i * U
                for u in range(U):
                    dve.wait_ge(counted, t + u + 1)
                    dve.tensor_scalar(src_hot[0:Q, u, :], node[0:Q, :], src_f[0:Q, bass.ds(t + u, 1)], None,
                                      ALU.is_equal)
                    dve.tensor_scalar(mem.dst_hot[:, bass.ds(t * N + u * N, N)], node[0:Q, :],
                                      dst_f[0:Q, bass.ds(t + u, 1)], None, ALU.is_equal).then_inc(hot_ready, 1)

        @block.tensor
        def _(pe):
            pe.sem_inc(counted, U)
            pe.wait_ge(zeroed, NC + 1)
            with pe.Fori(0, T // U) as i:
                t = i * U
                for u in range(U):
                    pe.wait_ge(hot_ready, t + u + 1)
                    for c in range(NC):
                        rows = src_hot[0:Q, u, c * Q:(c + 1) * Q]
                        pe.matmul(low[c][0:Q, :], rows, mem.dst_hot[:, bass.ds(t * N + u * N, 512)],
                                  start=False, stop=False, skip_group_check=True)
                        last = pe.matmul(rest(c), rows, mem.dst_hot[:, bass.ds(t * N + (u * N + 512), REST)],
                                         start=False, stop=False, skip_group_check=True)
                    last.then_inc(counted, 1)

        @block.scalar
        def _(act):
            act.wait_ge(counted, T + U)
            for c in range(NC):
                act.activation(mem.counts[:, c, 0:512], low[c][0:Q, :], ACT.Copy)
                act.activation(mem.counts[:, c, 512:N], rest(c), ACT.Copy)


def edge_sums(nc, mem, d, agg):
    with Phase(nc, "sums") as ph:
        rows = ph.sb("rows", [Q, U, F])
        index = ph.sb("index", [Q, U], I32)
        index_ready, gathers = ph.sem("index_ready"), ph.sem("gathers")
        prev_row, dst_row = ph.sb("prev_row", [P, U * Q], I32), ph.sb("dst_row", [P, U * Q], I32)
        keep = ph.sb("keep", [P, U * Q])
        last = ph.sb("last", [Q, T])
        next_dst = ph.sb("next_dst", [Q, T], I32)
        sums = ph.sb("sums", [P, U, KF, Q])
        masked, remainder = ph.sb("masked", [Q, 3, F]), ph.sb("remainder", [Q, 3, F])
        parts = ph.sb("parts", [Q, 3, 3, F], BF16)
        identity = ph.sb("identity", [P, P])
        turned, back = ph.ps("turned", [P, 2, 512]), ph.ps("back", [P, 2, 512])
        low, high = ph.ps("low", [P, KF, 512]), ph.ps("high", [P, 512])
        REST = N - 512
        slot = (0, 1, 0, 1, 2)
        load(nc, [(next_dst[:], d["dst_next"]), (identity[:], d["identity"][:, 0, 0:P])])
        zeroed, last_ready, rows_loaded, keep_ready, keep_used = (ph.sem(n) for n in (
            "zeroed", "last_ready", "rows_loaded", "keep_ready", "keep_used"))
        gathered = [ph.sem(f"gathered{u}") for u in range(U)]
        turned_ready, summed, back_ready, masked_ready = (ph.sem(n) for n in ("turned_ready", "summed", "back_ready", "masked_ready"))
        hi_ready, rest_ready, mid_ready, parts_ready, added = (ph.sem(n) for n in ("hi_ready", "rest_ready", "mid_ready", "parts_ready", "added"))
        block = ph.block()

        def piece(buf, u, k, width):
            at = (slot[u] % 2) * KF * width + k * width
            return buf[:, slot[u] // 2, at:at + width]

        @block.sync
        def _(sp):
            with sp.Fori(0, T // U) as i:
                sp.wait_ge(keep_used, i + 1)
                for to, of in ((dst_row, d["dst_row"]), (prev_row, d["prev_row"])):
                    sp.dma_start(to[:], of[:, bass.ds(i * (U * Q), U * Q)].partition_broadcast(P)).then_inc(rows_loaded, 16)

        @block.gpsimd
        def _(pool):
            with pool.Fori(0, T // U) as i:
                t = i * U
                for u in range(U):
                    pool.wait_ge(turned_ready, t + u + 1)
                    pool.tensor_copy(index[:, u:u + 1], mem.src[:, bass.ds(t + u, 1)]).then_inc(index_ready, 1)
                    pool.wait_ge(index_ready, t + u + 1)
                    pool.sem_inc(gathers, 1)
                    pool.indirect_dma_start(rows[:, u, :], None, d["x_table"],
                                            bass.IndirectOffsetOnAxis(ap=index[:, u:u + 1], axis=0)
                                            ).then_inc(gathered[u], 16)

        @block.tensor
        def _(pe):
            pe.sem_inc(turned_ready, U)
            pe.wait_ge(zeroed, 3)
            with pe.Fori(0, T // U) as i:
                t = i * U
                for u in range(U):
                    pe.wait_ge(gathered[u], i * 16 + 16)
                    pe.wait_ge(summed, t + u + 1)
                    for k in range(KF):
                        ins = pe.transpose(piece(turned, u, k, Q), rows[:, u, k * P:(k + 1) * P], identity[0:Q, 0:Q])
                    ins.then_inc(turned_ready, 1)
                    pe.wait_ge(summed, t + u + 3)
                    pe.wait_ge(masked_ready, t + u + 1)
                    for k in range(KF):
                        ins = pe.transpose(piece(back, u, k, P)[0:Q, :], sums[:, u, k, :], identity[:])
                    ins.then_inc(back_ready, 1)
                    pe.wait_ge(parts_ready, t + u + 1)
                    for part in range(3):
                        for k in range(KF):
                            w = parts[:, slot[u], part, k * P:(k + 1) * P]
                            pe.matmul(low[:, k, :], w, mem.dst_hot[:, bass.ds((t + u) * N, 512)],
                                      start=False, stop=False, skip_group_check=True)
                            ins = pe.matmul(high[:, k * REST:(k + 1) * REST], w, mem.dst_hot[:, bass.ds((t + u) * N + 512, REST)],
                                            start=False, stop=False, skip_group_check=True)
                    ins.then_inc(added, 1)

        @block.vector
        def _(dve):
            dve.memset(low[:], 0.0).then_inc(zeroed, 1)
            dve.memset(high[:], 0.0).then_inc(zeroed, 1)
            dve.memset(sums[:, U - 1, :, :], 0.0).then_inc(zeroed, 1)
            dve.tensor_tensor(last[:], mem.dst[:], next_dst[:], ALU.not_equal).then_inc(last_ready, 1)
            dve.sem_inc(keep_used, 1)
            dve.sem_inc(summed, 2)
            dve.sem_inc(added, 2)
            dve.wait_ge(zeroed, 3)
            with dve.Fori(0, T // U) as i:
                t = i * U
                dve.wait_ge(rows_loaded, i * 32 + 32)
                dve.tensor_tensor(keep[:], dst_row[:], prev_row[:], ALU.is_equal).then_inc(keep_used, 1)
                dve.wait_ge(keep_used, i + 2)
                for u in range(U):
                    n = t + u + 1
                    dve.wait_ge(turned_ready, t + u + (U + 1))
                    dve.wait_ge(summed, t + u + 2)
                    for k in range(KF):
                        ins = dve.tensor_tensor_scan(sums[:, u, k, :], keep[:, u * Q:(u + 1) * Q], piece(turned, u, k, Q),
                                                     sums[:, (u - 1) % U, k, Q - 1:Q], ALU.mult, ALU.add)
                    ins.then_inc(summed, 1)
                    dve.wait_ge(hi_ready, n)
                    dve.tensor_tensor(remainder[:, slot[u], :], masked[:, slot[u], :], parts[:, slot[u], 0, :],
                                      ALU.subtract).then_inc(rest_ready, 1)
                    dve.wait_ge(mid_ready, n)
                    dve.tensor_tensor(parts[:, slot[u], 2, :], remainder[:, slot[u], :], parts[:, slot[u], 1, :],
                                      ALU.subtract).then_inc(parts_ready, 1)

        @block.scalar
        def _(act):
            act.wait_ge(last_ready, 1)
            act.sem_inc(masked_ready, 2)
            with act.Fori(0, T // U) as i:
                t = i * U
                for u in range(U):
                    n = t + u + 1
                    act.wait_ge(back_ready, n)
                    act.wait_ge(added, n)
                    both = back[0:Q, slot[u] // 2, (slot[u] % 2) * F:(slot[u] % 2 + 1) * F]
                    act.activation(masked[:, slot[u], :], both, ACT.Copy, scale=last[:, bass.ds(t + u, 1)]).then_inc(masked_ready, 1)
                    act.wait_ge(masked_ready, t + u + 3)
                    act.activation(parts[:, slot[u], 0, :], masked[:, slot[u], :], ACT.Copy).then_inc(hi_ready, 1)
                    act.wait_ge(rest_ready, n)
                    act.activation(parts[:, slot[u], 1, :], remainder[:, slot[u], :], ACT.Copy).then_inc(mid_ready, 1)
            act.wait_ge(added, T + 2)
            act.activation(agg[:, :, 0:512], low[:], ACT.Copy)
            act.activation(agg[:, :, 512:N], high[:, 0:KF * REST].rearrange("p (k n) -> p k n", k=KF), ACT.Copy)


def gcn_input(nc, mem, d):
    with Phase(nc, "gcn") as g:
        w_gcn, w_enc = g.sb("w_gcn", [P, KF, F]), g.sb("w_enc", [P, KF, P])
        b_enc = g.sb("b_enc", [P, 2])
        agg, hid = g.sb("agg", [P, KF, N]), g.sb("hid", [P, KF, N])
        xe = g.sb("xe", [P, N])
        load(nc, [(w_gcn[:], d["w_gcn"]), (w_enc[:], d["w_enc"]), (b_enc[:], d["b_enc"])])
        edge_sums(nc, mem, d, agg)
        dense(nc, agg, w_gcn, hid, KF, KF, ACT.Relu, vec(mem, 'L0_gnn_b_gcn'))
        with Phase(nc, "xe") as ph:
            product = ph.ps("product", [P, 1024])
            product_ready, bias_ready, xe_ready, hi_ready = (ph.sem(n) for n in ("product_ready", "bias_ready", "xe_ready", "hi_ready"))
            cleared = ph.sem("cleared")
            block = ph.block()

            @block.tensor
            def _(pe):
                for a, b in PIECES:
                    for k in range(KF):
                        last = pe.matmul(product[:, a:b], w_enc[:, k, :], hid[:, k, a:b], start=(k == 0), stop=(k == KF - 1))
                last.then_inc(product_ready, 1)

            @block.vector
            def _(dve):
                dve.tensor_tensor(b_enc[:, 0:1], b_enc[:, 0:1], b_enc[:, 1:2], ALU.add).then_inc(bias_ready, 1)
                dve.memset(mem.xe_parts[:], 0.0).then_inc(cleared, 1)
                dve.wait_ge(cleared, 1)
                dve.memset(mem.xe_parts[96:P, 1:, 0:1], H_SCALE).then_inc(cleared, 1)
                dve.wait_ge(product_ready, 1)
                dve.wait_ge(bias_ready, 1)
                dve.tensor_scalar(xe[:], product[:, 0:N], b_enc[:, 0:1], XE_MAX, ALU.add, ALU.min).then_inc(xe_ready, 1)
                dve.wait_ge(xe_ready, 1)
                dve.tensor_scalar(xe[:], xe[:], -XE_MAX, None, ALU.max).then_inc(xe_ready, 1)
                dve.wait_ge(xe_ready, 2)
                dve.wait_ge(cleared, 2)
                rows = slice(64, 64 + 4 * HE)
                dve.tensor_copy(mem.xe_parts[rows, 0:N, 0], xe[rows, :]).then_inc(hi_ready, 1)
                dve.wait_ge(hi_ready, 1)
                dve.tensor_tensor(mem.xe_parts[rows, 0:N, 1], xe[rows, :], mem.xe_parts[rows, 0:N, 0], ALU.subtract)


def lstm_weights(nc, d, rec_parts, in_parts):
    with Phase(nc, "weights") as g:
        w_rec, w_in, w_in2 = g.sb("w_rec", [P, KF, 4 * F]), g.sb("w_in", [P, 12, P]), g.sb("w_in2", [P, 12, P])
        part = g.sb("part", [P, 12, P], F16)
        part2 = g.sb("part2", [P, 12, P], F16)
        rows = g.sb("rows", [P, 2])
        load(nc, [(w_rec[:], d["w_rec"]), (w_in[:], d["w_in"]), (w_in2[:], d["w_in2"]), (rows[:], d["part_rows"])])
        with Phase(nc, "parts") as ph:
            scaled, hi_ready, lo_ready = ph.sem("scaled"), ph.sem("hi_ready"), ph.sem("lo_ready")
            block = ph.block()

            @block.vector
            def _(dve):
                dve.tensor_tensor(w_in[:], w_in[:], w_in2[:], ALU.add).then_inc(scaled, 1)
                dve.wait_ge(scaled, 1)
                for lo, hi, s in ((0, 2, W_SCALE), (2, 3, 2 * W_SCALE), (3, 4, W_SCALE)):
                    dve.tensor_scalar(w_rec[:, :, lo * F:hi * F], w_rec[:, :, lo * F:hi * F], s, None, ALU.mult).then_inc(scaled, 1)
                    dve.tensor_scalar(w_in[:, 3 * lo:3 * hi, :], w_in[:, 3 * lo:3 * hi, :], s, None, ALU.mult).then_inc(scaled, 1)
                dve.wait_ge(scaled, 7)
                dve.tensor_copy(rec_parts[:, :, 0, :], w_rec[:]).then_inc(hi_ready, 1)
                dve.tensor_copy(part[:], w_in[:]).then_inc(hi_ready, 1)
                dve.wait_ge(hi_ready, 2)
                dve.tensor_tensor(rec_parts[:, :, 1, :], w_rec[:], rec_parts[:, :, 0, :], ALU.subtract)
                dve.tensor_tensor(part2[:], w_in[:], part[:], ALU.subtract).then_inc(lo_ready, 1)
                dve.wait_ge(lo_ready, 1)
                dve.tensor_scalar(part2[:], part2[:], rows[:, 1:2], None, ALU.mult).then_inc(lo_ready, 1)
                dve.wait_ge(lo_ready, 2)
                dve.scalar_tensor_tensor(out=in_parts[:].rearrange("p g m -> p (g m)"), in0=part[:].rearrange("p g m -> p (g m)"),
                                         scalar=rows[:, 0:1], in1=part2[:].rearrange("p g m -> p (g m)"),
                                         op0=ALU.mult, op1=ALU.add)


def lstms(nc, mem, d):
    with Phase(nc, "lstm") as ph:
        w_rec, w_in = ph.sb("w_rec", [P, KF, 2, 4 * F], F16), ph.sb("w_in", [P, 12, P], F16)
        lstm_weights(nc, d, w_rec, w_in)
        inputs = ph.sb("inputs", [P, U, 2], F16)
        h_parts = ph.sb("h_parts", [P, KF, 2], F16)
        gates = ph.sb("gates", [P, 9])
        gates_o = ph.sb("gates_o", [P, 3])
        act_ifg_c = ph.sb("act_ifg_c", [P, 12])
        act_o, o_scaled = ph.sb("act_o", [P, 3]), ph.sb("o_scaled", [P, 3])
        terms, tanh_c = ph.sb("terms", [P, 6]), ph.sb("tanh_c", [P, 3])
        h_ring = ph.sb("h_ring", [P, U, 3])
        ps_ifg = ph.ps("ps_ifg", [P, 3, 512])
        ps_o = ph.ps("ps_o", [P, 3, 512])
        cleared, ifg_ready, o_ready, sums_ready, o_sums_ready = (ph.sem(n) for n in (
            "cleared", "ifg_ready", "o_ready", "sums_ready", "o_sums_ready"))
        ifg_acted, o_acted, terms_ready, cell_ready, o_scaled_ready = (ph.sem(n) for n in (
            "ifg_acted", "o_acted", "terms_ready", "cell_ready", "o_scaled_ready"))
        tanh_c_ready, h32_ready, h_hi_ready, h_ready, z_hi_ready = (ph.sem(n) for n in (
            "tanh_c_ready", "h32_ready", "h_hi_ready", "h_ready", "z_hi_ready"))
        z_ready, h_kept, xe_filled = (ph.sem(n) for n in (
            "z_ready", "h_kept", "xe_filled"))
        bank = (0, 1, 0, 1, 2)
        block = ph.block()

        @block.tensor
        def _(pe):
            pe.wait_ge(cleared, 4)
            with pe.Fori(0, STEPS // U) as i:
                t = i * U
                for u in range(U):
                    ifg, o = ps_ifg[:, bank[u], :], ps_o[:, bank[u], :]

                    def column(gate, j):
                        c = 3 * (gate % 3) + j if gate < 3 else j
                        return (ifg if gate < 3 else o)[:, 2 * c:2 * c + 2]

                    for gate in range(4):
                        for j in range(KF):
                            pe.matmul(column(gate, j), w_in[0:KS, 3 * gate + j, :], inputs[0:KS, (u - 1) % U, :],
                                      start=(gate in (0, 3) and j == 0), stop=False, skip_group_check=True)
                    pe.wait_ge(h_ready, t + u + 1)
                    for part_of in (range(3), range(3, 4)):
                        for gate in part_of:
                            for j in range(KF):
                                for k in range(KF):
                                    for part in range(2):
                                        m = gate * F + j * P
                                        pe.matmul(column(gate, j), w_rec[:, k, part, m:m + P], h_parts[:, k, :],
                                                  start=False, stop=False, skip_group_check=True)
                        if part_of[0] == 0:
                            pe.wait_ge(z_ready, t + u + 1)
                            pe.wait_ge(xe_filled, t + u + 1)
                        for gate in part_of:
                            last = pe.matmul(column(gate, 2), w_in[0:KS, 3 * gate + 2, :], inputs[0:KS, u, :],
                                             start=False, stop=False, skip_group_check=True)
                        last.then_inc(ifg_ready if part_of[0] == 0 else o_ready, 1)

        @block.scalar
        def _(act):
            with act.Fori(0, STEPS // U) as i:
                t = i * U
                for u in range(U):
                    act.wait_ge(sums_ready, t + u + 1)
                    act.activation(act_ifg_c[:, 0:9], gates[:], ACT.Tanh, scale=0.5 / G_SCALE).then_inc(ifg_acted, 1)
                    act.wait_ge(o_sums_ready, t + u + 1)
                    act.activation(act_o[:], gates_o[:], ACT.Tanh, scale=0.5 / G_SCALE).then_inc(o_acted, 1)
                    act.wait_ge(cell_ready, t + u + 1)
                    act.activation(tanh_c[:], act_ifg_c[:, 9:12], ACT.Tanh, scale=0.5).then_inc(tanh_c_ready, 1)

        @block.vector
        def _(dve):
            dve.memset(inputs[:], 0.0).then_inc(cleared, 1)
            dve.memset(h_parts[:], 0.0).then_inc(cleared, 1)
            dve.memset(act_ifg_c[:, 9:12], 0.0).then_inc(cleared, 1)
            dve.wait_ge(cleared, 3)
            dve.tensor_copy(inputs[64:KS, 0:U - 1, :], mem.xe_parts[64:KS, 0:U - 1, :]).then_inc(cleared, 1)
            dve.sem_inc(h_ready, 1)
            dve.sem_inc(z_ready, 1)
            dve.sem_inc(xe_filled, U - 1)
            dve.sem_inc(h_kept, U)
            with dve.Fori(0, STEPS // U) as i:
                t = i * U
                for u in range(U):
                    n = t + u + 1
                    dve.wait_ge(ifg_ready, n)
                    dve.tensor_reduce(gates[:], ps_ifg[:, bank[u], 0:18].rearrange("p (g two) -> p g two", two=2), AX,
                                      ALU.add).then_inc(sums_ready, 1)
                    dve.wait_ge(o_ready, n)
                    dve.tensor_reduce(gates_o[:], ps_o[:, bank[u], 0:6].rearrange("p (g two) -> p g two", two=2), AX,
                                      ALU.add).then_inc(o_sums_ready, 1)
                    dve.wait_ge(ifg_acted, n)
                    dve.scalar_tensor_tensor(out=terms[:], in0=act_ifg_c[:, 0:6], scalar=1.0, in1=act_ifg_c[:, 6:12],
                                             op0=ALU.add, op1=ALU.mult).then_inc(terms_ready, 1)
                    dve.wait_ge(terms_ready, n)
                    dve.scalar_tensor_tensor(out=act_ifg_c[:, 9:12], in0=terms[:, 3:6], scalar=0.5, in1=terms[:, 0:3],
                                             op0=ALU.mult, op1=ALU.add).then_inc(cell_ready, 1)
                    dve.wait_ge(o_acted, n)
                    dve.tensor_scalar(o_scaled[:], act_o[:], 1.0, H_SCALE / 2, ALU.add, ALU.mult).then_inc(o_scaled_ready, 1)
                    dve.wait_ge(o_scaled_ready, n)
                    dve.wait_ge(h_kept, n)
                    dve.wait_ge(tanh_c_ready, n)
                    dve.tensor_tensor(h_parts[:, :, 0], o_scaled[:, 0:2], tanh_c[:, 0:2], ALU.mult).then_inc(h_hi_ready, 1)
                    dve.tensor_tensor(h_ring[:, u, :], o_scaled[:], tanh_c[:], ALU.mult).then_inc(h32_ready, 1)
                    dve.wait_ge(h32_ready, n)
                    dve.wait_ge(h_hi_ready, n)
                    dve.tensor_tensor(h_parts[:, :, 1], h_ring[:, u, 0:2], h_parts[:, :, 0], ALU.subtract).then_inc(h_ready, 1)
                    z_hi, z_lo = inputs[0:64, (u + 1) % U, 0:1], inputs[0:64, (u + 1) % U, 1:2]
                    dve.tensor_copy(z_hi, h_ring[0:64, u, 2:3]).then_inc(z_hi_ready, 1)
                    dve.wait_ge(z_hi_ready, n)
                    dve.tensor_tensor(z_lo, h_ring[0:64, u, 2:3], z_hi, ALU.subtract).then_inc(z_ready, 1)

        @block.gpsimd
        def _(pool):
            pool.wait_ge(cleared, 4)
            with pool.Fori(0, STEPS // U) as i:
                t = i * U
                for u in range(U):
                    pool.wait_ge(h32_ready, t + u + 1)
                    pool.wait_ge(xe_filled, t + (u + U - 1))
                    pool.tensor_copy(mem.h_all[:, :, bass.ds(t + u, 1)], h_ring[:, u, 0:2].rearrange("p (k one) -> p k one", one=1)).then_inc(h_kept, 1)
                    pool.wait_ge(o_ready, t + u + 1)
                    pool.wait_ge(h_kept, t + (u + U + 1))
                    pool.tensor_copy(inputs[64:KS, (u - 1) % U, :],
                                     mem.xe_parts[64:KS, bass.ds(t + (u + U - 1), 1), :].rearrange("p one two -> p (one two)")).then_inc(xe_filled, 1)


def residual_scaled(nc, x, y, out, scale, at=0):
    with Phase(nc, "res") as ph:
        block = ph.block()

        @block.vector
        def _(dve):
            for k in range(KF):
                dve.scalar_tensor_tensor(out=out[:, k, :], in0=y[:, k, at:at + N], scalar=scale, in1=x[:, k, :],
                                         op0=ALU.mult, op1=ALU.add)


def add_into(nc, out, x, y):
    with Phase(nc, "add") as ph:
        block = ph.block()

        @block.vector
        def _(dve):
            dve.tensor_tensor(out[:], x[:], y[:], ALU.add)


def write_table(nc, nodes, table):
    with Phase(nc, "table") as ph:
        stored = ph.sem("stored")
        block = ph.block()

        @block.sync
        def _(sp):
            sp.dma_start(table.rearrange("(c p) f -> p c f", p=Q), nodes[:]).then_inc(stored, 16)
            sp.wait_ge(stored, 16)


def batch_norm_fixed(nc, mem, x, out, pfx):
    mean, var, gamma, beta = (vec(mem, pfx + n) for n in ("_mean", "_var", "_gamma", "_beta"))
    with Phase(nc, "bn") as ph:
        scale = ph.sb("scale", [P, KF])
        std_ready, scale_ready, scaled = ph.sem("std_ready"), ph.sem("scale_ready"), ph.sem("scaled")
        block = ph.block()

        @block.scalar
        def _(act):
            act.activation(scale[:], var, ACT.Sqrt, bias=mem.eps[:, 0:1]).then_inc(std_ready, 1)

        @block.vector
        def _(dve):
            dve.wait_ge(std_ready, 1)
            dve.reciprocal(scale[:], scale[:]).then_inc(scale_ready, 1)
            dve.wait_ge(scale_ready, 1)
            dve.tensor_tensor(scale[:], scale[:], gamma, ALU.mult).then_inc(scale_ready, 1)
            dve.wait_ge(scale_ready, 2)
            for k in range(KF):
                dve.tensor_scalar(out[:, k, :], x[:, k, :], mean[:, k:k + 1], scale[:, k:k + 1], ALU.subtract,
                                  ALU.mult).then_inc(scaled, 1)
            for k in range(KF):
                dve.wait_ge(scaled, k + 1)
                dve.tensor_scalar(out[:, k, :], out[:, k, :], beta[:, k:k + 1], None, ALU.add)


def gin_messages(nc, mem, d, agg):
    with Phase(nc, "gin") as ph:
        rows, attr = ph.sb("rows", [Q, U, F]), ph.sb("attr", [Q, U, F])
        index = ph.sb("index", [Q, U], I32)
        message, parts = ph.sb("message", [Q, U, F]), ph.sb("parts", [Q, U, 2, F], F16)
        low, high = ph.ps("low", [P, KF, 512]), ph.ps("high", [P, 512])
        REST = N - 512
        zeroed, index_ready, message_ready, hi_ready, parts_ready, added = (ph.sem(n) for n in (
            "zeroed", "index_ready", "message_ready", "hi_ready", "parts_ready", "added"))
        gathers = ph.sem("gathers")
        gathered = [ph.sem(f"gathered{u}") for u in range(U)]
        loaded = [ph.sem(f"loaded{u}") for u in range(U)]
        block = ph.block()

        @block.sync
        def _(sp):
            with sp.Fori(0, T // U) as i:
                t = i * U
                for u in range(U):
                    sp.wait_ge(message_ready, t + u + 1)
                    sp.dma_start(attr[:, u, :], d["edge_attr"][:, bass.ds((t + u) * F, F)]).then_inc(loaded[u], 16)

        @block.gpsimd
        def _(pool):
            with pool.Fori(0, T // U) as i:
                t = i * U
                for u in range(U):
                    pool.wait_ge(message_ready, t + u + 1)
                    pool.tensor_copy(index[:, u:u + 1], mem.src[:, bass.ds(t + u, 1)]).then_inc(index_ready, 1)
                    pool.wait_ge(index_ready, t + u + 1)
                    pool.sem_inc(gathers, 1)
                    pool.indirect_dma_start(rows[:, u, :], None, mem.table,
                                            bass.IndirectOffsetOnAxis(ap=index[:, u:u + 1], axis=0)).then_inc(gathered[u], 16)

        @block.vector
        def _(dve):
            dve.memset(low[:], 0.0).then_inc(zeroed, 1)
            dve.memset(high[:], 0.0).then_inc(zeroed, 1)
            dve.sem_inc(message_ready, U)
            dve.sem_inc(added, U)
            with dve.Fori(0, T // U) as i:
                t = i * U
                for u in range(U):
                    dve.wait_ge(gathered[u], i * 16 + 16)
                    dve.wait_ge(loaded[u], i * 16 + 16)
                    dve.wait_ge(added, t + u + 1)
                    dve.tensor_tensor(message[:, u, :], rows[:, u, :], attr[:, u, :], ALU.add).then_inc(message_ready, 1)
                    dve.wait_ge(hi_ready, t + u + 1)
                    dve.scalar_tensor_tensor(out=parts[:, u, 1, :], in0=message[:, u, :], scalar=0.0, in1=parts[:, u, 0, :],
                                             op0=ALU.max, op1=ALU.subtract).then_inc(parts_ready, 1)

        @block.scalar
        def _(act):
            with act.Fori(0, T // U) as i:
                t = i * U
                for u in range(U):
                    act.wait_ge(message_ready, t + u + (U + 1))
                    act.activation(parts[:, u, 0, :], message[:, u, :], ACT.Relu).then_inc(hi_ready, 1)
            act.wait_ge(added, T + U)
            act.activation(agg[:, :, 0:512], low[:], ACT.Copy)
            act.activation(agg[:, :, 512:N], high[:, 0:KF * REST].rearrange("p (k n) -> p k n", k=KF), ACT.Copy)

        @block.tensor
        def _(pe):
            pe.wait_ge(zeroed, 2)
            with pe.Fori(0, T // U) as i:
                t = i * U
                for u in range(U):
                    pe.wait_ge(parts_ready, t + u + 1)
                    for part in range(2):
                        for k in range(KF):
                            w = parts[:, u, part, k * P:(k + 1) * P]
                            pe.matmul(low[:, k, :], w, mem.dst_hot[:, bass.ds((t + u) * N, 512)],
                                      start=False, stop=False, skip_group_check=True)
                            ins = pe.matmul(high[:, k * REST:(k + 1) * REST], w, mem.dst_hot[:, bass.ds((t + u) * N + 512, REST)],
                                            start=False, stop=False, skip_group_check=True)
                    ins.then_inc(added, 1)


def layer_gin(nc, mem, d):
    with Phase(nc, "l1") as g:
        identity, w1, w2 = (g.sb(n, [P, KF, F]) for n in ("identity", "w1", "w2"))
        nodes = g.sb("nodes", [Q, NC, F])
        agg, f, f2 = (g.sb(n, [P, KF, N]) for n in ("agg", "f", "f2"))
        load(nc, [(identity[:], d["identity"]), (w1[:], d["gin_w1"]), (w2[:], d["gin_w2"])])
        node_major(nc, mem.x, identity, nodes, F)
        write_table(nc, nodes, mem.table)
        gin_messages(nc, mem, d, agg)
        residual_scaled(nc, agg, mem.x, agg, 2.0)
        batch_norm_fixed(nc, mem, agg, f, 'L1_gnn_bn1')
        dense(nc, f, w1, f2, KF, KF, ACT.Gelu, vec(mem, 'L1_gnn_b1'))
        dense(nc, f2, w2, f, KF, KF, ACT.Identity, vec(mem, 'L1_gnn_b2'))
        add_into(nc, agg, agg, f)
        batch_norm_fixed(nc, mem, agg, agg, 'L1_gnn_bn2')
        add_into(nc, mem.x, mem.x, agg)
    layer_norm(nc, mem, mem.x, mem.x)


def attention(nc, mem, d, q, k_, v, out):
    NEG = -1e30
    with Phase(nc, "att") as g:
        v_ones = g.sb("v_ones", [Q, NC, HEADS, 2 * HD])
        no_edge = g.sb("no_edge", [Q, NC, N])
        top = g.sb("top", [Q, NC, HEADS])
        top_rows = g.sb("top_rows", [P, N])
        minus_head = g.sb("minus_head", [P, HEADS, Q])
        identity = g.sb("identity", [P, P])
        load(nc, [(minus_head[:], d["minus_head"]), (identity[:], d["identity"][:, 0, 0:P])])
        with Phase(nc, "mask") as ph:
            turned = ph.ps("turned", [P, 2, 1024])
            turned_ready, evacuated = ph.sem("turned_ready"), ph.sem("evacuated")
            block = ph.block()

            @block.tensor
            def _(pe):
                for c in range(NC):
                    if c >= 2:
                        pe.wait_ge(evacuated, c - 1)
                    for s in range(NC):
                        at = (512 if s == NC - 1 else 0) + (0 if s == NC - 1 else s * Q)
                        ins = pe.transpose(turned[0:Q, c % 2, at:at + Q], mem.counts[:, s, c * Q:(c + 1) * Q], identity[0:Q, 0:Q])
                    ins.then_inc(turned_ready, 1)

            @block.vector
            def _(dve):
                dve.memset(v_ones[:, :, :, HD:2 * HD], 1.0)
                for c in range(NC):
                    dve.tensor_copy(v_ones[:, c, :, 0:HD], v[:, c, :].rearrange("p (h e) -> p h e", h=HEADS))
                for c in range(NC):
                    dve.wait_ge(turned_ready, c + 1)
                    for a, b, at in ((0, 4 * Q, 0), (4 * Q, N, 512)):
                        ins = dve.tensor_scalar(no_edge[:, c, a:b], turned[0:Q, c % 2, at:at + b - a], 0.0, NEG,
                                                ALU.is_equal, ALU.mult)
                    ins.then_inc(evacuated, 1)
        with Phase(nc, "top") as ph:
            scores = ph.ps("scores", [P, 3, 1024])
            rows = ph.ps("rows", [HEADS, 1024])
            scratch = ph.sb("scratch", [Q, 2, N])
            scores_ready, reduced, rows_ready = ph.sem("scores_ready"), ph.sem("reduced"), ph.sem("rows_ready")
            block = ph.block()

            @block.tensor
            def _(pe):
                n = 0
                for c in range(NC):
                    for h in range(HEADS):
                        if n >= 3:
                            pe.wait_ge(reduced, n - 2)
                        p = slice(HD * (h % 4), HD * (h % 4) + HD)
                        for a, b in PIECES:
                            ins = pe.matmul(scores[0:Q, n % 3, a:b], q[p, h // 4, c * Q:(c + 1) * Q], k_[p, h // 4, a:b],
                                            start=True, stop=True)
                        ins.then_inc(scores_ready, 1)
                        n += 1
                pe.wait_ge(reduced, n)
                for c in range(NC):
                    at = 512 if c == NC - 1 else c * Q
                    ins = pe.transpose(rows[:, at:at + Q], top[:, c, :], identity[0:Q, 0:Q])
                ins.then_inc(rows_ready, 1)

            @block.vector
            def _(dve):
                n = 0
                for c in range(NC):
                    for h in range(HEADS):
                        dve.wait_ge(scores_ready, n + 1)
                        if n >= 2:
                            dve.wait_ge(reduced, n - 1)
                        dve.tensor_tensor_reduce(out=scratch[:, n % 2, :], in0=scores[0:Q, n % 3, 0:N], in1=no_edge[:, c, :],
                                                 scale=1.0, scalar=0.0, op0=ALU.add, op1=ALU.max,
                                                 accum_out=top[:, c, h:h + 1]).then_inc(reduced, 1)
                        n += 1
                dve.wait_ge(rows_ready, 1)
                for j in range(0, P, HD):
                    dve.tensor_copy(top_rows[j:j + HEADS, 0:4 * Q], rows[:, 0:4 * Q])
                    dve.tensor_copy(top_rows[j:j + HEADS, 4 * Q:N], rows[:, 512:512 + Q])
        with Phase(nc, "mix") as ph:
            scores = ph.ps("scores", [P, 2, 1024])
            mixed = ph.ps("mixed", [2 * HD, 2, 1024])
            low, weight = ph.sb("low", [Q, 2, N]), ph.sb("weight", [Q, 2, N])
            inverse = ph.sb("inverse", [HD, N])
            scores_ready, low_ready, exp_ready, weight_ready, mixed_ready, head_done = (ph.sem(n) for n in (
                "scores_ready", "low_ready", "exp_ready", "weight_ready", "mixed_ready", "head_done"))
            inverse_ready = ph.sem("inverse_ready")
            block = ph.block()
            todo = [(h, s) for h in range(HEADS) for s in range(NC)]
            rows_of = lambda h: slice(HD * (h % 4), HD * (h % 4) + HEADS)

            @block.tensor
            def _(pe):
                def mix(n):
                    h, s = todo[n]
                    pe.wait_ge(weight_ready, n + 1)
                    if s == 0 and h >= 2:
                        pe.wait_ge(head_done, h - 1)
                    for a, b in PIECES:
                        ins = pe.matmul(mixed[:, h % 2, a:b], v_ones[:, s, h, :], weight[:, n % 2, a:b],
                                        start=(s == 0), stop=(s == NC - 1))
                    ins.then_inc(mixed_ready, 1)

                for n, (h, s) in enumerate(todo):
                    if n >= 2:
                        pe.wait_ge(low_ready, n - 1)
                    p = slice(HD * (h % 4), HD * (h % 4) + HD)
                    for a, b in PIECES:
                        pe.matmul(scores[0:Q, n % 2, a:b], k_[p, h // 4, s * Q:(s + 1) * Q], q[p, h // 4, a:b],
                                  start=True, stop=False)
                        ins = pe.matmul(scores[0:Q, n % 2, a:b], minus_head[rows_of(h), h, :], top_rows[rows_of(h), a:b],
                                        start=False, stop=True)
                    ins.then_inc(scores_ready, 1)
                    if n >= 1:
                        mix(n - 1)
                mix(len(todo) - 1)

            @block.scalar
            def _(act):
                for n in range(len(todo)):
                    act.wait_ge(low_ready, n + 1)
                    act.activation(low[:, n % 2, :], low[:, n % 2, :], ACT.Exp).then_inc(exp_ready, 1)

            @block.vector
            def _(dve):
                def finish(h):
                    dve.wait_ge(mixed_ready, NC * (h + 1))
                    dve.wait_ge(head_done, h)
                    dve.tensor_scalar(inverse[:], mixed[HD:2 * HD, h % 2, 0:N], 1e-8, None, ALU.add).then_inc(inverse_ready, 1)
                    dve.wait_ge(inverse_ready, 2 * h + 1)
                    dve.reciprocal(inverse[:], inverse[:]).then_inc(inverse_ready, 1)
                    dve.wait_ge(inverse_ready, 2 * h + 2)
                    dve.tensor_tensor(out[HD * (h % 4):HD * (h % 4) + HD, h // 4, :], mixed[0:HD, h % 2, 0:N], inverse[:],
                                      ALU.mult).then_inc(head_done, 1)

                for n, (h, s) in enumerate(todo):
                    dve.wait_ge(scores_ready, n + 1)
                    if n >= 2:
                        dve.wait_ge(weight_ready, n - 1)
                    dve.tensor_scalar(low[:, n % 2, :], scores[0:Q, n % 2, 0:N], 0.0, None, ALU.min).then_inc(low_ready, 1)
                    dve.wait_ge(exp_ready, n + 1)
                    if n >= 2:
                        dve.wait_ge(mixed_ready, n - 1)
                    dve.tensor_tensor(weight[:, n % 2, :], low[:, n % 2, :], mem.counts[:, s, :], ALU.mult).then_inc(weight_ready, 1)
                    if s == 1 and h >= 1:
                        finish(h - 1)
                finish(HEADS - 1)


def layer_attention(nc, mem, d):
    with Phase(nc, "l2") as g:
        wo = g.sb("wo", [P, KF, F])
        mixed, y = g.sb("mixed", [P, KF, N]), g.sb("y", [P, KF, N])
        with Phase(nc, "qkv") as g2:
            wq, wk, wv = (g2.sb(n, [P, KF, F]) for n in ("wq", "wk", "wv"))
            q, k_ = g2.sb("q", [P, KF, N]), g2.sb("k", [P, KF, N])
            v = g2.sb("v", [Q, NC, F])
            load(nc, [(wq[:], d["att_wq"]), (wk[:], d["att_wk"]), (wv[:], d["att_wv"]), (wo[:], d["att_wo"])])
            dense(nc, mem.x, wq, q, KF, KF, ACT.Identity, scale=HD ** -0.5)
            dense(nc, mem.x, wk, k_, KF, KF, ACT.Identity)
            node_major(nc, mem.x, wv, v, F)
            attention(nc, mem, d, q, k_, v, mixed)
        dense(nc, mixed, wo, y, KF, KF, ACT.Identity, vec(mem, 'L2_gnn_Wo_b'))
        add_into(nc, y, mem.x, y)
        layer_norm(nc, mem, y, y, vec(mem, 'L2_gnn_ln1_g'), vec(mem, 'L2_gnn_ln1_b'))
        with Phase(nc, "ffn") as g2:
            w1, w2 = g2.sb("w1", [P, KF, 2 * F]), g2.sb("w2", [P, 2 * KF, F])
            hidden = g2.sb("hidden", [P, 2 * KF, N])
            load(nc, [(w1[:], d["att_w1"]), (w2[:], d["att_w2"])])
            dense(nc, y, w1, hidden, KF, 2 * KF, ACT.Gelu, vec(mem, 'L2_gnn_ffn_b1'))
            dense(nc, hidden, w2, mixed, 2 * KF, KF, ACT.Identity, vec(mem, 'L2_gnn_ffn_b2'))
        add_into(nc, y, y, mixed)
        layer_norm(nc, mem, y, y, vec(mem, 'L2_gnn_ln2_g'), vec(mem, 'L2_gnn_ln2_b'))
        add_into(nc, mem.x, mem.x, y)
    layer_norm(nc, mem, mem.x, mem.x)


def loop_attributes(nc, mem, d, loop_ea):
    with Phase(nc, "loops") as ph:
        attr = ph.sb("attr", [Q, U, EF])
        parts = ph.sb("parts", [Q, U, 2, 2 * EF], F16)
        total = ph.ps("total", [2 * EF, 1024])
        inverse = ph.sb("inverse", [EF, N])
        zeroed, loaded, attr_used, hi_ready, parts_ready, added, inverse_ready = (ph.sem(n) for n in (
            "zeroed", "loaded", "attr_used", "hi_ready", "parts_ready", "added", "inverse_ready"))
        block = ph.block()

        @block.sync
        def _(sp):
            with sp.Fori(0, T // U) as i:
                sp.wait_ge(attr_used, i + 1)
                sp.dma_start(attr[:], d["small_attr"][:, bass.ds(i * (U * EF), U * EF)].rearrange("p (u f) -> p u f", u=U)
                             ).then_inc(loaded, 16)

        @block.vector
        def _(dve):
            dve.memset(total[:], 0.0).then_inc(zeroed, 1)
            dve.memset(parts[:, :, 0, EF:], 1.0).then_inc(zeroed, 1)
            dve.memset(parts[:, :, 1, EF:], 0.0).then_inc(zeroed, 1)
            dve.sem_inc(attr_used, 1)
            dve.sem_inc(added, 1)
            with dve.Fori(0, T // U) as i:
                dve.wait_ge(loaded, i * 16 + 16)
                dve.wait_ge(added, i + 1)
                dve.tensor_copy(parts[:, :, 0, 0:EF], attr[:]).then_inc(hi_ready, 1)
                dve.wait_ge(hi_ready, i + 1)
                dve.tensor_tensor(parts[:, :, 1, 0:EF], attr[:], parts[:, :, 0, 0:EF], ALU.subtract).then_inc(parts_ready, 1)
                dve.wait_ge(parts_ready, i + 1)
                dve.sem_inc(attr_used, 1)
            dve.wait_ge(added, T // U + 1)
            dve.tensor_scalar(inverse[:], total[EF:2 * EF, 0:N], 1.0, None, ALU.max).then_inc(inverse_ready, 1)
            dve.wait_ge(inverse_ready, 1)
            dve.reciprocal(inverse[:], inverse[:]).then_inc(inverse_ready, 1)
            dve.wait_ge(inverse_ready, 2)
            dve.tensor_tensor(loop_ea[:], total[0:EF, 0:N], inverse[:], ALU.mult)

        @block.tensor
        def _(pe):
            pe.wait_ge(zeroed, 3)
            with pe.Fori(0, T // U) as i:
                t = i * U
                pe.wait_ge(parts_ready, i + 1)
                for u in range(U):
                    for part in range(2):
                        for a, b in PIECES:
                            ins = pe.matmul(total[:, a:b], parts[:, u, part, :], mem.dst_hot[:, bass.ds((t + u) * N + a, b - a)],
                                            start=False, stop=False, skip_group_check=True)
                ins.then_inc(added, 1)


def gat_scores(nc, mem, d, pfx, scores):
    with Phase(nc, "scores") as ph:
        left, right = ph.sb("left", [Q, U, F]), ph.sb("right", [Q, U, F])
        l_index, r_index = ph.sb("l_index", [Q, U], I32), ph.sb("r_index", [Q, U], I32)
        attr = ph.sb("attr", [EF, 2 * U * Q])
        w_e, att = ph.sb("w_e", [EF, F]), ph.sb("att", [P, F])
        ends = ph.sb("ends", [Q, 2, F])
        z, act_z, weighted = ph.sb("z", [Q, 2, F]), ph.sb("act_z", [Q, 2, F]), ph.sb("weighted", [Q, 2, F])
        from_edge = ph.ps("from_edge", [P, U, 512])
        load(nc, [(w_e[:], d[pfx + "_We"]), (att[:], d[pfx + "_att"].partition_broadcast(P))])
        attr_used, index_ready, from_edge_ready, ends_ready, z_ready, act_ready, weighted_ready, scored = (ph.sem(n) for n in (
            "attr_used", "index_ready", "from_edge_ready", "ends_ready", "z_ready", "act_ready", "weighted_ready", "scored"))
        attr_loaded, gathers = ph.sem("attr_loaded"), ph.sem("gathers")
        left_in = [ph.sem(f"left_in{u}") for u in range(U)]
        right_in = [ph.sem(f"right_in{u}") for u in range(U)]
        block = ph.block()

        @block.sync
        def _(sp):
            with sp.Fori(0, T // U) as i:
                sp.wait_ge(attr_used, i + 1)
                sp.dma_start(attr[:, 0:U * Q], d["small_attr_t"][:, bass.ds(i * (U * Q), U * Q)]).then_inc(attr_loaded, 16)

        @block.gpsimd
        def _(pool):
            with pool.Fori(0, T // U) as i:
                t = i * U
                for u in range(U):
                    pool.wait_ge(ends_ready, t + u + 1)
                    pool.tensor_copy(l_index[:, u:u + 1], mem.src[:, bass.ds(t + u, 1)]).then_inc(index_ready, 1)
                    pool.wait_ge(index_ready, 2 * t + (2 * u + 1))
                    pool.tensor_copy(r_index[:, u:u + 1], mem.dst[:, bass.ds(t + u, 1)]).then_inc(index_ready, 1)
                    pool.wait_ge(index_ready, 2 * t + (2 * u + 2))
                    pool.sem_inc(gathers, 1)
                    pool.indirect_dma_start(left[:, u, :], None, mem.table,
                                            bass.IndirectOffsetOnAxis(ap=l_index[:, u:u + 1], axis=0)).then_inc(left_in[u], 16)
                    pool.indirect_dma_start(right[:, u, :], None, mem.table_r,
                                            bass.IndirectOffsetOnAxis(ap=r_index[:, u:u + 1], axis=0)).then_inc(right_in[u], 16)

        @block.tensor
        def _(pe):
            pe.sem_inc(attr_used, 1)
            pe.sem_inc(ends_ready, U)
            pe.sem_inc(z_ready, U)
            with pe.Fori(0, T // U) as i:
                t = i * U
                pe.wait_ge(attr_loaded, i * 16 + 16)
                for u in range(U):
                    pe.wait_ge(z_ready, t + u + 1)
                    ins = pe.matmul(from_edge[0:Q, u, 0:F], attr[:, u * Q:(u + 1) * Q], w_e[:], start=True, stop=True)
                    ins.then_inc(from_edge_ready, 1)
                pe.wait_ge(from_edge_ready, t + U)
                pe.sem_inc(attr_used, 1)

        @block.vector
        def _(dve):
            with dve.Fori(0, T // U) as i:
                t = i * U
                for u in range(U):
                    n = t + u + 1
                    b = u % 2
                    dve.wait_ge(left_in[u], i * 16 + 16)
                    dve.wait_ge(right_in[u], i * 16 + 16)
                    dve.tensor_tensor(ends[:, b, :], left[:, u, :], right[:, u, :], ALU.add).then_inc(ends_ready, 1)
                    dve.wait_ge(ends_ready, t + (u + U + 1))
                    dve.wait_ge(from_edge_ready, n)
                    dve.tensor_tensor(z[:, b, :], ends[:, b, :], from_edge[0:Q, u, 0:F], ALU.add).then_inc(z_ready, 1)
                    dve.wait_ge(z_ready, t + (u + U + 1))
                    dve.scalar_tensor_tensor(out=act_z[:, b, :], in0=z[:, b, :], scalar=0.2, in1=z[:, b, :],
                                             op0=ALU.mult, op1=ALU.max).then_inc(act_ready, 1)
                    dve.wait_ge(act_ready, n)
                    dve.tensor_tensor(weighted[:, b, :], act_z[:, b, :], att[0:Q, :], ALU.mult).then_inc(weighted_ready, 1)
                    dve.wait_ge(weighted_ready, n)
                    dve.tensor_reduce(scores[:, bass.ds((t + u) * HEADS, HEADS)], weighted[:, b, :].rearrange("p (h e) -> p h e", h=HEADS),
                                      AX, ALU.add).then_inc(scored, 1)


def run_maxima(nc, mem, d, scores, top):
    NEG = -1e30
    G = U * Q
    with Phase(nc, "maxima") as ph:
        next_dst, last = ph.sb("next_dst", [Q, T], I32), ph.sb("last", [Q, T])
        dst_row, prev_row = ph.sb("dst_row", [HEADS, G], I32), ph.sb("prev_row", [HEADS, G], I32)
        begin = ph.sb("begin", [HEADS, G])
        own = ph.sb("own", [Q, U * HEADS])
        running = ph.sb("running", [HEADS, G])
        ends, parts = ph.sb("ends", [Q, U, HEADS]), ph.sb("parts", [Q, U, 72], F16)
        flags = ph.sb("flags", [Q, U, HEADS])
        runs, some = ph.sb("runs", [HEADS, N]), ph.sb("some", [HEADS, N])
        identity = ph.sb("identity", [P, P])
        turned, back, total = ph.ps("turned", [HEADS, 1024]), ph.ps("back", [Q, 512]), ph.ps("total", [72, 1024])
        load(nc, [(next_dst[:], d["dst_next"]), (identity[:], d["identity"][:, 0, 0:P])])
        (zeroed, last_ready, rows_loaded, rows_used, own_ready, turned_ready, begin_ready, scanned, back_ready, flags_ready,
         ends_ready, hi_ready, parts_ready, added, total_ready) = (ph.sem(n) for n in (
            "zeroed", "last_ready", "rows_loaded", "rows_used", "own_ready", "turned_ready", "begin_ready", "scanned", "back_ready",
            "flags_ready", "ends_ready", "hi_ready", "parts_ready", "added", "total_ready"))
        turns = ph.sem("turns")
        block = ph.block()
        at = lambda u: 512 if u == U - 1 else u * Q

        @block.sync
        def _(sp):
            with sp.Fori(0, T // U) as i:
                sp.wait_ge(rows_used, i + 1)
                for to, of in ((dst_row, d["dst_row"]), (prev_row, d["prev_row"])):
                    sp.dma_start(to[:], of[:, bass.ds(i * G, G)].partition_broadcast(HEADS)).then_inc(rows_loaded, 16)

        @block.scalar
        def _(act):
            act.sem_inc(turned_ready, 1)
            with act.Fori(0, T // U) as i:
                act.wait_ge(turned_ready, i + 1)
                act.activation(own[:], scores[:, bass.ds(i * (U * HEADS), U * HEADS)], ACT.Copy).then_inc(own_ready, 1)

        @block.tensor
        def _(pe):
            pe.wait_ge(zeroed, 3)
            with pe.Fori(0, T // U) as i:
                t = i * U
                pe.wait_ge(own_ready, i + 1)
                pe.wait_ge(scanned, i + 1)
                for u in range(U):
                    ins = pe.transpose(turned[:, at(u):at(u) + Q], own[:, u * HEADS:(u + 1) * HEADS], identity[0:Q, 0:Q])
                ins.then_inc(turned_ready, 1)
                pe.wait_ge(scanned, i + 2)
                pe.sem_inc(turns, 1)
                for u in range(U):
                    ins = pe.transpose(back[:, u * HEADS:(u + 1) * HEADS], running[:, u * Q:(u + 1) * Q], identity[0:HEADS, 0:HEADS])
                ins.then_inc(back_ready, 1)
                pe.wait_ge(parts_ready, i + 1)
                for u in range(U):
                    for a, b in PIECES:
                        ins = pe.matmul(total[:, a:b], parts[:, u, :], mem.dst_hot[:, bass.ds((t + u) * N + a, b - a)],
                                        start=False, stop=False, skip_group_check=True)
                ins.then_inc(added, 1)

        @block.vector
        def _(dve):
            dve.memset(total[:], 0.0).then_inc(zeroed, 1)
            dve.memset(parts[:], 0.0).then_inc(zeroed, 1)
            dve.memset(running[:, G - 1:G], NEG).then_inc(zeroed, 1)
            dve.tensor_tensor(last[:], mem.dst[:], next_dst[:], ALU.not_equal).then_inc(last_ready, 1)
            dve.wait_ge(last_ready, 1)
            dve.wait_ge(zeroed, 3)
            dve.sem_inc(rows_used, 1)
            dve.sem_inc(scanned, 1)
            dve.sem_inc(added, 1)
            with dve.Fori(0, T // U) as i:
                dve.wait_ge(rows_loaded, i * 32 + 32)
                dve.tensor_tensor(begin[:], dst_row[:], prev_row[:], ALU.not_equal).then_inc(rows_used, 1)
                dve.wait_ge(rows_used, i + 2)
                dve.tensor_scalar(begin[:], begin[:], NEG, None, ALU.mult).then_inc(begin_ready, 1)
                dve.wait_ge(begin_ready, 2 * i + 1)
                dve.wait_ge(turned_ready, i + 2)
                dve.tensor_tensor_scan(running[:, 0:4 * Q], begin[:, 0:4 * Q], turned[:, 0:4 * Q], running[:, G - 1:G],
                                       ALU.add, ALU.max).then_inc(begin_ready, 1)
                dve.wait_ge(begin_ready, 2 * i + 2)
                dve.tensor_tensor_scan(running[:, 4 * Q:G], begin[:, 4 * Q:G], turned[:, 512:512 + Q], running[:, 4 * Q - 1:4 * Q],
                                       ALU.add, ALU.max).then_inc(scanned, 1)
                dve.wait_ge(added, i + 1)
                dve.tensor_copy(flags[:], last[:, bass.ds(i * U, U)].rearrange("p (u one) -> p u one", one=1).to_broadcast((Q, U, HEADS))
                                ).then_inc(flags_ready, 1)
                dve.wait_ge(flags_ready, i + 1)
                dve.wait_ge(back_ready, i + 1)
                dve.tensor_tensor(ends[:], back[:, 0:U * HEADS].rearrange("p (u h) -> p u h", u=U), flags[:], ALU.mult).then_inc(ends_ready, 1)
                dve.tensor_copy(parts[:, :, 64:64 + HEADS], flags[:])
                dve.wait_ge(ends_ready, i + 1)
                dve.tensor_copy(parts[:, :, 0:HEADS], ends[:]).then_inc(hi_ready, 1)
                dve.wait_ge(hi_ready, i + 1)
                dve.tensor_tensor(parts[:, :, 32:32 + HEADS], ends[:], parts[:, :, 0:HEADS], ALU.subtract).then_inc(parts_ready, 1)
            dve.wait_ge(added, T // U + 1)
            dve.tensor_copy(top[:], total[32:32 + HEADS, 0:N]).then_inc(total_ready, 1)
            dve.tensor_scalar(runs[:], total[64:64 + HEADS, 0:N], 1.0, None, ALU.max).then_inc(total_ready, 1)
            dve.tensor_scalar(some[:], total[64:64 + HEADS, 0:N], 0.0, NEG, ALU.is_equal, ALU.mult).then_inc(total_ready, 1)
            dve.wait_ge(total_ready, 3)
            dve.tensor_tensor(top[:], total[0:HEADS, 0:N], top[:], ALU.add).then_inc(total_ready, 1)
            dve.reciprocal(runs[:], runs[:]).then_inc(total_ready, 1)
            dve.wait_ge(total_ready, 5)
            dve.tensor_tensor(top[:], top[:], runs[:], ALU.mult).then_inc(total_ready, 1)
            dve.wait_ge(total_ready, 6)
            dve.tensor_tensor(top[:], top[:], some[:], ALU.add)


def gat_loops(nc, mem, d, pfx, x, w_l, w_r, w_e, loop_ea, top, loop_exp):
    with Phase(nc, "selfs") as ph:
        z = ph.ps("z", [P, 2, 1024])
        loop_score, rows = ph.ps("loop_score", [HEADS, 1024]), ph.ps("rows", [Q, NC, HEADS])
        z_sb, act_z = ph.sb("z_sb", [P, KF, N]), ph.sb("act_z", [P, KF, N])
        att = ph.sb("att", [P, KF, HEADS])
        nodes = ph.sb("nodes", [Q, NC, HEADS])
        identity = ph.sb("identity", [P, P])
        load(nc, [(att[:], d[pfx + "_att_cols"]), (identity[:], d["identity"][:, 0, 0:P])])
        z_ready, z_out, act_ready, score_ready, top_ready, below, rows_ready, nodes_ready, stored = (ph.sem(n) for n in (
            "z_ready", "z_out", "act_ready", "score_ready", "top_ready", "below", "rows_ready", "nodes_ready", "stored"))
        block = ph.block()

        @block.tensor
        def _(pe):
            for m in range(KF):
                cols = slice(m * P, (m + 1) * P)
                for a, b in PIECES:
                    for k in range(KF):
                        for w in (w_l, w_r):
                            pe.matmul(z[:, m, a:b], w[:, k, cols], x[:, k, a:b], start=(k == 0 and w is w_l), stop=False)
                    ins = pe.matmul(z[:, m, a:b], w_e[:, cols], loop_ea[:, a:b], start=False, stop=True)
                ins.then_inc(z_ready, 1)
            pe.wait_ge(act_ready, KF)
            for a, b in PIECES:
                for k in range(KF):
                    ins = pe.matmul(loop_score[:, a:b], att[:, k, :], act_z[:, k, a:b], start=(k == 0), stop=(k == KF - 1))
            ins.then_inc(score_ready, 1)
            pe.wait_ge(top_ready, 1)
            for c in range(NC):
                ins = pe.transpose(rows[:, c, :], top[:, c * Q:(c + 1) * Q], identity[0:HEADS, 0:HEADS])
            ins.then_inc(rows_ready, 1)

        @block.scalar
        def _(act):
            for m in range(KF):
                act.wait_ge(z_ready, m + 1)
                act.activation(z_sb[:, m, :], z[:, m, 0:N], ACT.Copy).then_inc(z_out, 1)
            act.wait_ge(below, 1)
            act.activation(loop_exp[:], loop_exp[:], ACT.Exp)

        @block.vector
        def _(dve):
            for m in range(KF):
                dve.wait_ge(z_out, m + 1)
                dve.scalar_tensor_tensor(out=act_z[:, m, :], in0=z_sb[:, m, :], scalar=0.2, in1=z_sb[:, m, :],
                                         op0=ALU.mult, op1=ALU.max).then_inc(act_ready, 1)
            dve.wait_ge(score_ready, 1)
            dve.tensor_tensor(top[:], loop_score[:, 0:N], top[:], ALU.max).then_inc(top_ready, 1)
            dve.wait_ge(top_ready, 1)
            dve.tensor_tensor(loop_exp[:], loop_score[:, 0:N], top[:], ALU.subtract).then_inc(below, 1)
            dve.wait_ge(rows_ready, 1)
            dve.tensor_copy(nodes[:], rows[:]).then_inc(nodes_ready, 1)

        @block.sync
        def _(sp):
            sp.wait_ge(nodes_ready, 1)
            sp.dma_start(mem.table_top.rearrange("(c p) h -> p c h", p=Q), nodes[:]).then_inc(stored, 16)
            sp.wait_ge(stored, 16)


def gat_messages(nc, mem, d, scores, num, den):
    with Phase(nc, "mess") as ph:
        rows, top = ph.sb("rows", [Q, U, F]), ph.sb("top", [Q, U, HEADS])
        s_index, d_index = ph.sb("s_index", [Q, U], I32), ph.sb("d_index", [Q, U], I32)
        below, weight = ph.sb("below", [Q, U, HEADS]), ph.sb("weight", [Q, U, HEADS])
        W = F + HEADS
        message, parts = ph.sb("message", [Q, U, W]), ph.sb("parts", [Q, U, 2, W], F16)
        low, high, low_den = ph.ps("low", [P, KF, 512]), ph.ps("high", [P, 512]), ph.ps("low_den", [HEADS, 512])
        REST = N - 512
        (zeroed, index_ready, below_ready, weight_ready, scaled, message_ready, hi_ready, parts_ready, added) = (ph.sem(n) for n in (
            "zeroed", "index_ready", "below_ready", "weight_ready", "scaled", "message_ready", "hi_ready", "parts_ready", "added"))
        gathers = ph.sem("gathers")
        rows_in = [ph.sem(f"rows_in{u}") for u in range(U)]
        top_in = [ph.sem(f"top_in{u}") for u in range(U)]
        block = ph.block()

        @block.gpsimd
        def _(pool):
            with pool.Fori(0, T // U) as i:
                t = i * U
                for u in range(U):
                    pool.wait_ge(scaled, t + u + 1)
                    pool.tensor_copy(s_index[:, u:u + 1], mem.src[:, bass.ds(t + u, 1)]).then_inc(index_ready, 1)
                    pool.wait_ge(index_ready, 2 * t + (2 * u + 1))
                    pool.tensor_copy(d_index[:, u:u + 1], mem.dst[:, bass.ds(t + u, 1)]).then_inc(index_ready, 1)
                    pool.wait_ge(index_ready, 2 * t + (2 * u + 2))
                    pool.sem_inc(gathers, 1)
                    pool.indirect_dma_start(top[:, u, :], None, mem.table_top,
                                            bass.IndirectOffsetOnAxis(ap=d_index[:, u:u + 1], axis=0)).then_inc(top_in[u], 16)
                    pool.indirect_dma_start(rows[:, u, :], None, mem.table,
                                            bass.IndirectOffsetOnAxis(ap=s_index[:, u:u + 1], axis=0)).then_inc(rows_in[u], 16)

        @block.vector
        def _(dve):
            for p in (low, high, low_den):
                dve.memset(p[:], 0.0).then_inc(zeroed, 1)
            dve.sem_inc(scaled, U)
            dve.sem_inc(added, U)
            with dve.Fori(0, T // U) as i:
                t = i * U
                for u in range(U):
                    n = t + u + 1
                    dve.wait_ge(top_in[u], i * 16 + 16)
                    dve.wait_ge(added, n)
                    dve.tensor_tensor(below[:, u, :], scores[:, bass.ds((t + u) * HEADS, HEADS)], top[:, u, :], ALU.subtract
                                      ).then_inc(below_ready, 1)
                    dve.wait_ge(rows_in[u], i * 16 + 16)
                    dve.wait_ge(weight_ready, n)
                    dve.tensor_tensor(message[:, u, 0:F].rearrange("p (h e) -> p h e", h=HEADS),
                                      rows[:, u, :].rearrange("p (h e) -> p h e", h=HEADS),
                                      weight[:, u, :].rearrange("p (h one) -> p h one", one=1).to_broadcast((Q, HEADS, HD)), ALU.mult
                                      ).then_inc(scaled, 1)
                    dve.tensor_copy(message[:, u, F:W], weight[:, u, :]).then_inc(message_ready, 1)
                    dve.wait_ge(hi_ready, n)
                    dve.tensor_tensor(parts[:, u, 1, :], message[:, u, :], parts[:, u, 0, :], ALU.subtract).then_inc(parts_ready, 1)

        @block.scalar
        def _(act):
            with act.Fori(0, T // U) as i:
                t = i * U
                for u in range(U):
                    n = t + u + 1
                    act.wait_ge(below_ready, n)
                    act.activation(weight[:, u, :], below[:, u, :], ACT.Exp).then_inc(weight_ready, 1)
                    act.wait_ge(scaled, t + (u + U + 1))
                    act.wait_ge(message_ready, n)
                    act.activation(parts[:, u, 0, :], message[:, u, :], ACT.Copy).then_inc(hi_ready, 1)
            act.wait_ge(added, T + U)
            act.activation(num[:, :, 0:512], low[:], ACT.Copy)
            act.activation(num[:, :, 512:N], high[:, 0:KF * REST].rearrange("p (k n) -> p k n", k=KF), ACT.Copy)
            act.activation(den[:, 0:512], low_den[:], ACT.Copy)
            act.activation(den[:, 512:N], high[0:HEADS, KF * REST:(KF + 1) * REST], ACT.Copy)

        @block.tensor
        def _(pe):
            pe.wait_ge(zeroed, 3)
            with pe.Fori(0, T // U) as i:
                t = i * U
                for u in range(U):
                    pe.wait_ge(parts_ready, t + u + 1)
                    for part in range(2):
                        for k in range(KF + 1):
                            w = parts[:, u, part, k * P:min((k + 1) * P, W)]
                            m = P if k < KF else HEADS
                            pe.matmul(low[:, k, :] if k < KF else low_den[:], w, mem.dst_hot[:, bass.ds((t + u) * N, 512)],
                                      start=False, stop=False, skip_group_check=True)
                            ins = pe.matmul(high[0:m, k * REST:(k + 1) * REST], w, mem.dst_hot[:, bass.ds((t + u) * N + 512, REST)],
                                            start=False, stop=False, skip_group_check=True)
                    ins.then_inc(added, 1)


def gat_finish(nc, mem, d, xl, loop_exp, num, den, bias, out):
    with Phase(nc, "finish") as ph:
        spread = ph.sb("spread", [HEADS, F])
        load(nc, [(spread[:], d["head_rows"])])
        wide, inverse = ph.ps("wide", [P, KF, 1024]), ph.ps("inverse", [P, KF, 1024])
        den_ready, wide_ready, inverse_ready, scaled = (ph.sem(n) for n in ("den_ready", "wide_ready", "inverse_ready", "scaled"))
        block = ph.block()

        @block.tensor
        def _(pe):
            for k in range(KF):
                for a, b in PIECES:
                    ins = pe.matmul(wide[:, k, a:b], spread[:, k * P:(k + 1) * P], loop_exp[:, a:b], start=True, stop=True)
            ins.then_inc(wide_ready, 1)
            pe.wait_ge(den_ready, 2)
            for k in range(KF):
                for a, b in PIECES:
                    ins = pe.matmul(inverse[:, k, a:b], spread[:, k * P:(k + 1) * P], den[:, a:b], start=True, stop=True)
            ins.then_inc(inverse_ready, 1)

        @block.vector
        def _(dve):
            dve.tensor_tensor(den[:], den[:], loop_exp[:], ALU.add).then_inc(den_ready, 1)
            dve.wait_ge(den_ready, 1)
            dve.reciprocal(den[:], den[:]).then_inc(den_ready, 1)
            dve.wait_ge(wide_ready, 1)
            for k in range(KF):
                dve.tensor_tensor(out[:, k, :], wide[:, k, 0:N], xl[:, k, :], ALU.mult).then_inc(scaled, 1)
            for k in range(KF):
                dve.wait_ge(scaled, k + 1)
                dve.tensor_tensor(out[:, k, :], out[:, k, :], num[:, k, :], ALU.add).then_inc(scaled, 1)
            dve.wait_ge(inverse_ready, 1)
            for k in range(KF):
                dve.wait_ge(scaled, KF + k + 1)
                dve.tensor_tensor(out[:, k, :], out[:, k, :], inverse[:, k, 0:N], ALU.mult).then_inc(scaled, 1)
            for k in range(KF):
                dve.wait_ge(scaled, 2 * KF + k + 1)
                dve.tensor_scalar(out[:, k, :], out[:, k, :], bias[:, k:k + 1], None, ALU.add).then_inc(scaled, 1)


def batch_norm_step(nc, mem, y, gain, shift, x, out):
    with Phase(nc, "bnstep") as ph:
        mean, total, scale = ph.sb("mean", [P, KF]), ph.sb("total", [P, KF]), ph.sb("scale", [P, KF])
        squares = ph.sb("squares", [P, KF, N])
        summed, centred, squared, var_ready, std_ready, chain = (ph.sem(n) for n in (
            "summed", "centred", "squared", "var_ready", "std_ready", "chain"))
        block = ph.block()

        @block.scalar
        def _(act):
            for k in range(KF):
                act.wait_ge(centred, k + 1)
                act.activation(squares[:, k, :], y[:, k, :], ACT.Square).then_inc(squared, 1)
            act.wait_ge(var_ready, 1)
            act.activation(scale[:], total[:], ACT.Sqrt, bias=mem.eps[:, 0:1], scale=1.0 / N).then_inc(std_ready, 1)

        @block.vector
        def _(dve):
            count = [0]

            def link(ins):
                count[0] += 1
                ins.then_inc(chain, 1)
                dve.wait_ge(chain, count[0])

            link(dve.tensor_reduce(mean[:], y[:], AX, ALU.add))
            link(dve.tensor_scalar(mean[:], mean[:], 1.0 / N, None, ALU.mult))
            for k in range(KF):
                dve.tensor_scalar(y[:, k, :], y[:, k, :], mean[:, k:k + 1], None, ALU.subtract).then_inc(centred, 1)
            dve.wait_ge(squared, KF)
            dve.tensor_reduce(total[:], squares[:], AX, ALU.add).then_inc(var_ready, 1)
            dve.wait_ge(std_ready, 1)
            link(dve.reciprocal(scale[:], scale[:]))
            link(dve.tensor_tensor(scale[:], scale[:], gain, ALU.mult))
            for k in range(KF):
                link(dve.tensor_scalar(y[:, k, :], y[:, k, :], scale[:, k:k + 1], shift[:, k:k + 1], ALU.mult, ALU.add))
                link(dve.scalar_tensor_tensor(out=squares[:, k, :], in0=y[:, k, :], scalar=0.01, in1=y[:, k, :],
                                              op0=ALU.mult, op1=ALU.max))
                link(dve.tensor_tensor(out[:, k, :], x[:, k, :], squares[:, k, :], ALU.add))


def gat(nc, mem, d, pfx, x, loop_ea, out):
    with Phase(nc, pfx) as g:
        scores = g.sb("scores", [Q, T * HEADS])
        top, loop_exp = g.sb("top", [HEADS, N]), g.sb("loop_exp", [HEADS, N])
        num, den, xl = g.sb("num", [P, KF, N]), g.sb("den", [HEADS, N]), g.sb("xl", [P, KF, N])
        w_l, w_r, w_e = g.sb("w_l", [P, KF, F]), g.sb("w_r", [P, KF, F]), g.sb("w_e", [EF, F])
        load(nc, [(w_l[:], d[pfx + "_Wl"]), (w_r[:], d[pfx + "_Wr"]), (w_e[:], d[pfx + "_We"])])
        with Phase(nc, "tables") as g2:
            nodes = g2.sb("nodes", [Q, NC, F])
            for w, table in ((w_l, mem.table), (w_r, mem.table_r)):
                node_major(nc, x, w, nodes, F)
                write_table(nc, nodes, table)
        gat_scores(nc, mem, d, pfx, scores)
        run_maxima(nc, mem, d, scores, top)
        gat_loops(nc, mem, d, pfx, x, w_l, w_r, w_e, loop_ea, top, loop_exp)
        dense(nc, x, w_l, xl, KF, KF, ACT.Identity)
        gat_messages(nc, mem, d, scores, num, den)
        gat_finish(nc, mem, d, xl, loop_exp, num, den, vec(mem, f"L3_gnn_{pfx}_b"), out)


def layer_gat(nc, mem, d):
    with Phase(nc, "l3") as g:
        h, y = g.sb("h", [P, KF, N]), g.sb("y", [P, KF, N])
        with Phase(nc, "gats") as g2:
            loop_ea = g2.sb("loop_ea", [EF, N])
            loop_attributes(nc, mem, d, loop_ea)
            gat(nc, mem, d, "g1", mem.x, loop_ea, y)
            batch_norm_step(nc, mem, y, vec(mem, 'L3_gnn_n1_g'), vec(mem, 'L3_gnn_n1_b'), mem.x, h)
            recycle(nc)
            gat(nc, mem, d, "g2", h, loop_ea, y)
            batch_norm_step(nc, mem, y, vec(mem, 'L3_gnn_n2_g'), vec(mem, 'L3_gnn_n2_b'), h, h)
        recycle(nc)
        with Phase(nc, "ff") as g2:
            w1, w2 = g2.sb("w1", [P, KF, 4 * F]), g2.sb("w2", [P, 4 * KF, F])
            hidden = g2.sb("hidden", [P, 4 * KF, N])
            load(nc, [(w1[:], d["ff_w1"]), (w2[:], d["ff_w2"])])
            dense(nc, h, w1, hidden, KF, 4 * KF, ACT.Relu, vec(mem, 'L3_gnn_ff_b1'))
            dense(nc, hidden, w2, y, 4 * KF, KF, ACT.Identity, vec(mem, 'L3_gnn_ff_b2'))
        batch_norm_step(nc, mem, y, vec(mem, 'L3_gnn_n3_g'), vec(mem, 'L3_gnn_n3_b'), h, h)
        add_into(nc, mem.x, mem.x, h)
    layer_norm(nc, mem, mem.x, mem.x)


def layer_recurrent(nc, mem, d):
    with Phase(nc, "l0") as g:
        mem.xe_parts = g.sb("xe_parts", [P, STEPS + U, 2], F16)
        mem.h_all = g.sb("h_all", [P, KF, STEPS])
        gcn_input(nc, mem, d)
        lstms(nc, mem, d)
        residual_scaled(nc, mem.x, mem.h_all, mem.x, 1.0 / H_SCALE, at=LAG)
    layer_norm(nc, mem, mem.x, mem.x)


def build(nc, d, out, layers=(0, 1, 2, 3)):
    Phase.used.clear()
    with Phase(nc, "mem") as top:
        mem = Memory()
        mem.src, mem.dst = top.sb("src", [Q, T], I32), top.sb("dst", [Q, T], I32)
        mem.averager, mem.vecs, mem.eps = top.sb("averager", [P, P]), top.sb("vecs", [P, N_VEC]), top.sb("eps", [P, 1])
        mem.dst_hot = top.sb("dst_hot", [Q, T * N], F16)
        mem.counts = top.sb("counts", [Q, NC, N])
        mem.x = top.sb("x", [P, KF, N])
        mem.table, mem.table_r = (nc.dram_tensor(n, (N, F), F32).ap() for n in ("table", "table_r"))
        mem.table_top = nc.dram_tensor("table_top", (N, HEADS), F32).ap()
        setup(nc, mem, d)
        for n, layer in enumerate((layer_recurrent, layer_gin, layer_attention, layer_gat)):
            if n in layers:
                layer(nc, mem, d)
                recycle(nc)
        store(nc, mem, d, out)


def store(nc, mem, d, out):
    with Phase(nc, "store") as ph:
        nodes = ph.sb("nodes", [Q, NC, F])
        identity = ph.sb("identity", [P, KF, F])
        load(nc, [(identity[:], d["identity"])])
        node_major(nc, mem.x, identity, nodes, F)
        with Phase(nc, "out") as p2:
            stored = p2.sem("stored")
            block = p2.block()

            @block.sync
            def _(sp):
                sp.dma_start(out.rearrange("(c p) f -> p c f", p=Q), nodes[:]).then_inc(stored, 16)
                sp.wait_ge(stored, 16)



def lay_out(inputs):
    import numpy as np

    x = {k: np.asarray(v) for k, v in inputs.items()}
    blocks = lambda w: np.ascontiguousarray(w.reshape(-1, P, w.shape[-1]).transpose(1, 0, 2))
    a = {}
    a["x"] = blocks(x["x"].T)
    a["x_table"] = x["x"]
    a["dst_row"] = x["dst"].reshape(1, E)
    a["prev_row"] = np.concatenate([[-1], x["dst"][:-1]]).astype(np.int32).reshape(1, E)
    a["dst_next"] = np.ascontiguousarray(np.concatenate([x["dst"][1:], [-1]]).astype(np.int32).reshape(T, Q).T)
    a["src"] = np.ascontiguousarray(x["src"].reshape(T, Q).T)
    a["dst"] = np.ascontiguousarray(x["dst"].reshape(T, Q).T)
    a["averager"] = np.full((P, P), 1.0 / F, np.float32)
    a["identity"] = blocks(np.eye(F, dtype=np.float32))
    a["vecs"] = np.concatenate([x[v].reshape(-1, P).T for v in VECS], axis=1)
    a["w_gcn"] = blocks(x["L0_gnn_W_gcn"].T)
    a["w_enc"] = np.zeros((P, KF, P), np.float32)
    a["w_enc"][:, :, 64:104] = blocks(x["L0_gnn_Wih_e"].T)
    a["b_enc"] = np.zeros((P, 2), np.float32)
    a["b_enc"][64:104, 0] = x["L0_gnn_bih_e"]
    a["b_enc"][64:104, 1] = x["L0_gnn_bhh_e"]
    a["w_rec"] = blocks(x["L0_gnn_Whh_d"].T)
    w_in = np.zeros((P, 12, P), np.float32)
    w_in2 = np.zeros((P, 12, P), np.float32)
    for gate in range(4):
        for j in range(KF):
            m = slice(gate * F + j * P, gate * F + (j + 1) * P)
            for r in (0, 32):
                w_in[r:r + HE, 3 * gate + j, :] = x["L0_gnn_Wih_d"][m].T
            for r in (104, 105):
                w_in[r, 3 * gate + j, :] = x["L0_gnn_bih_d"][m]
                w_in2[r, 3 * gate + j, :] = x["L0_gnn_bhh_d"][m]
        for c in (0, 32):
            for r in (0, 32):
                w_in[r:r + HE, 3 * gate + 2, c:c + HE] = x["L0_gnn_Whh_e"][gate * HE:(gate + 1) * HE].T
            for j in range(HE):
                w_in[64 + gate * HE + j, 3 * gate + 2, c + j] = H_SCALE
    a["w_in"], a["w_in2"] = w_in, w_in2
    rows = np.zeros((P, 2), np.float32)
    rows[0:32, 0] = rows[64:105, 0] = 1.0
    rows[32:64, 1] = rows[105, 1] = 1.0
    a["part_rows"] = rows
    a["edge_attr"] = np.ascontiguousarray(x["edge_attr_256"].reshape(T, Q, F).transpose(1, 0, 2)).reshape(Q, T * F)
    a["gin_w1"], a["gin_w2"] = blocks(x["L1_gnn_W1"].T), blocks(x["L1_gnn_W2"].T)
    for w in ("q", "k", "v"):
        a["att_w" + w] = blocks(x["L2_gnn_W" + w])
    a["att_wo"], a["att_w1"], a["att_w2"] = (blocks(x["L2_gnn_" + n]) for n in ("Wo_w", "ffn_w1", "ffn_w2"))
    small = x["edge_attr_32"]
    a["small_attr"] = np.ascontiguousarray(small.reshape(T, Q, EF).transpose(1, 0, 2)).reshape(Q, T * EF)
    a["small_attr_t"] = small.T
    for g in ("g1", "g2"):
        att = x[f"L3_gnn_{g}_att"]
        a[g + "_Wl"], a[g + "_Wr"], a[g + "_We"] = blocks(x[f"L3_gnn_{g}_Wl"]), blocks(x[f"L3_gnn_{g}_Wr"]), x[f"L3_gnn_{g}_We"]
        a[g + "_att"] = att.reshape(1, F)
        cols = np.zeros((HEADS, HD, HEADS), np.float32)
        for h in range(HEADS):
            cols[h, :, h] = att[h]
        a[g + "_att_cols"] = blocks(cols.reshape(F, HEADS))
    a["ff_w1"], a["ff_w2"] = blocks(x["L3_gnn_ff_W1"]), blocks(x["L3_gnn_ff_W2"])
    a["head_rows"] = np.repeat(np.eye(HEADS, dtype=np.float32), HD, axis=1)
    a["minus_head"] = np.zeros((4, HD, HEADS, Q), np.float32)
    for h in range(HEADS):
        a["minus_head"][:, h, h, :] = -1.0
    a["minus_head"] = a["minus_head"].reshape(P, HEADS, Q)
    return {k: np.ascontiguousarray(v) for k, v in a.items()}


def kernel(**inputs):
    import numpy as np
    import concourse.bacc as bacc
    from concourse.bass_utils import run_bass_kernel_spmd

    nc = bacc.Bacc("TRN2", target_bir_lowering=False, num_devices=1)
    arrays = lay_out(inputs)
    d = {k: nc.dram_tensor(k, a.shape, mybir.dt.from_np(a.dtype), kind="ExternalInput").ap() for k, a in arrays.items()}
    out = nc.dram_tensor("out", (N, F), F32, kind="ExternalOutput").ap()
    build(nc, d, out)
    r = run_bass_kernel_spmd(nc, [arrays], core_ids=[0])
    return r.results[0]["out"]
```

```python
from contextlib import ExitStack

import concourse.bass as bass
from concourse import mybir

F32 = mybir.dt.float32
F16 = mybir.dt.float16
BF16 = mybir.dt.bfloat16
I32 = mybir.dt.int32
ALU = mybir.AluOpType
ACT = mybir.ActivationFunctionType
AX = mybir.AxisListType.X

P = 128
N = 625
Q = 125
NC = N // Q
E = 10625
T = E // Q
F = 256
KF = F // P
EF = 32
HE = 10
HEADS, HD = 8, 32
EPS = 1e-5
PIECES = ((0, 512), (512, N))
U = 5

H_SCALE = 2.0 ** 7
W_SCALE = 2.0 ** 7
G_SCALE = H_SCALE * W_SCALE
XE_MAX = 60000.0
UL = 6
STEPS = 630
LAG = 2
XE_HI = list(range(64, 104))
XE_LO = list(range(104, P)) + list(range(20, 32)) + list(range(52, 56))
ONES = (56, 57)

VECS = ['L0_gnn_b_gcn', 'L1_gnn_b1', 'L1_gnn_b2', 'L1_gnn_bn1_gamma', 'L1_gnn_bn1_beta', 'L1_gnn_bn1_mean',
        'L1_gnn_bn1_var', 'L1_gnn_bn2_gamma', 'L1_gnn_bn2_beta', 'L1_gnn_bn2_mean', 'L1_gnn_bn2_var',
        'L2_gnn_Wo_b', 'L2_gnn_ln1_g', 'L2_gnn_ln1_b', 'L2_gnn_ln2_g', 'L2_gnn_ln2_b', 'L2_gnn_ffn_b1',
        'L2_gnn_ffn_b2', 'L3_gnn_g1_b', 'L3_gnn_g2_b', 'L3_gnn_n1_g', 'L3_gnn_n1_b', 'L3_gnn_n2_g',
        'L3_gnn_n2_b', 'L3_gnn_n3_g', 'L3_gnn_n3_b', 'L3_gnn_ff_b1', 'L3_gnn_ff_b2']
VEC_BLOCKS = {name: {'L2_gnn_ffn_b1': 4, 'L3_gnn_ff_b1': 8}.get(name, 2) for name in VECS}
VEC_AT = {name: sum(VEC_BLOCKS[v] for v in VECS[:i]) for i, name in enumerate(VECS)}
N_VEC = sum(VEC_BLOCKS.values())


class Memory:
    pass


class Phase:

    used = []

    def __init__(self, nc, name):
        self.nc, self.name, self.ctx = nc, f"{name}{nc.next_id()}", ExitStack()

    def __enter__(self):
        self.ctx.__enter__()
        return self

    def __exit__(self, *exc):
        return self.ctx.__exit__(*exc)

    def sb(self, name, shape, dt=F32):
        return self.ctx.enter_context(self.nc.sbuf_tensor(f"{self.name}_{name}", shape, dt))

    def ps(self, name, shape):
        return self.ctx.enter_context(self.nc.psum_tensor(f"{self.name}_{name}", shape, F32))

    def sem(self, name):
        handle = self.nc.alloc_semaphore(f"{self.name}_{name}")
        Phase.used.append(handle)
        return handle

    def block(self):
        return self.ctx.enter_context(self.nc.Block())


def recycle(nc):
    nc.all_engine_barrier()
    nc.clear_and_free_semaphores(list(Phase.used))
    nc.all_engine_barrier()
    Phase.used.clear()


def vec(mem, name):
    at = VEC_AT[name]
    return mem.vecs[:, at:at + VEC_BLOCKS[name]]


def load(nc, pairs):
    with Phase(nc, "load") as ph:
        loaded = ph.sem("loaded")
        block = ph.block()

        @block.sync
        def _(sp):
            for to, of in pairs[0::2]:
                sp.dma_start(to, of).then_inc(loaded, 16)
            sp.wait_ge(loaded, 16 * len(pairs))

        @block.scalar
        def _(act):
            for to, of in pairs[1::2]:
                act.dma_start(to, of).then_inc(loaded, 16)


def dense(nc, x, w, out, k_blocks, m_blocks, func, bias=None, scale=1.0):
    with Phase(nc, "dense") as ph:
        product = ph.ps("product", [P, 2, 1024])
        product_ready, evacuated = ph.sem("product_ready"), ph.sem("evacuated")
        block = ph.block()

        @block.tensor
        def _(pe):
            for m in range(m_blocks):
                if m >= 2:
                    pe.wait_ge(evacuated, m - 1)
                for a, b in PIECES:
                    for k in range(k_blocks):
                        last = pe.matmul(product[:, m % 2, a:b], w[:, k, m * P:(m + 1) * P], x[:, k, a:b],
                                         start=(k == 0), stop=(k == k_blocks - 1))
                last.then_inc(product_ready, 1)

        @block.scalar
        def _(act):
            for m in range(m_blocks):
                act.wait_ge(product_ready, m + 1)
                act.activation(out[:, m, 0:N], product[:, m % 2, 0:N], func, scale=scale,
                               bias=0.0 if bias is None else bias[:, m:m + 1]).then_inc(evacuated, 1)


def node_major(nc, x, w, out, cols):
    with Phase(nc, "nodes") as ph:
        product = ph.ps("product", [P, 2, 512])
        product_ready, evacuated = ph.sem("product_ready"), ph.sem("evacuated")
        block = ph.block()

        @block.tensor
        def _(pe):
            for c in range(NC):
                if c >= 2:
                    pe.wait_ge(evacuated, c - 1)
                for k in range(KF):
                    last = pe.matmul(product[0:Q, c % 2, 0:cols], x[:, k, c * Q:(c + 1) * Q], w[:, k, 0:cols],
                                     start=(k == 0), stop=(k == KF - 1))
                last.then_inc(product_ready, 1)

        @block.vector
        def _(dve):
            for c in range(NC):
                dve.wait_ge(product_ready, c + 1)
                dve.tensor_copy(out[:, c, 0:cols], product[0:Q, c % 2, 0:cols]).then_inc(evacuated, 1)


def layer_norm(nc, mem, x, out, gain=None, shift=None):
    with Phase(nc, "ln") as ph:
        mean, var = ph.ps("mean", [P, 1024]), ph.ps("var", [P, 1024])
        centred, squares = ph.sb("centred", [P, KF, N]), ph.sb("squares", [P, KF, N])
        rstd = ph.sb("rstd", [P, N])
        mean_ready, centred_ready, squares_ready = ph.sem("mean_ready"), ph.sem("centred_ready"), ph.sem("squares_ready")
        var_ready, std_ready, rstd_ready, normed = ph.sem("var_ready"), ph.sem("std_ready"), ph.sem("rstd_ready"), ph.sem("normed")
        block = ph.block()

        @block.tensor
        def _(pe):
            for a, b in PIECES:
                for k in range(KF):
                    last = pe.matmul(mean[:, a:b], mem.averager[:], x[:, k, a:b], start=(k == 0), stop=(k == KF - 1))
            last.then_inc(mean_ready, 1)
            pe.wait_ge(squares_ready, KF)
            for a, b in PIECES:
                for k in range(KF):
                    last = pe.matmul(var[:, a:b], mem.averager[:], squares[:, k, a:b], start=(k == 0), stop=(k == KF - 1))
            last.then_inc(var_ready, 1)

        @block.scalar
        def _(act):
            for k in range(KF):
                act.wait_ge(centred_ready, k + 1)
                act.activation(squares[:, k, :], centred[:, k, :], ACT.Square).then_inc(squares_ready, 1)
            act.wait_ge(var_ready, 1)
            act.activation(rstd[:], var[:, 0:N], ACT.Sqrt, bias=mem.eps[:, 0:1]).then_inc(std_ready, 1)

        @block.vector
        def _(dve):
            dve.wait_ge(mean_ready, 1)
            for k in range(KF):
                dve.tensor_tensor(centred[:, k, :], x[:, k, :], mean[:, 0:N], ALU.subtract).then_inc(centred_ready, 1)
            dve.wait_ge(std_ready, 1)
            dve.reciprocal(rstd[:], rstd[:]).then_inc(rstd_ready, 1)
            dve.wait_ge(rstd_ready, 1)
            dve.wait_ge(centred_ready, KF)
            for k in range(KF):
                dve.tensor_tensor(out[:, k, :], centred[:, k, :], rstd[:], ALU.mult).then_inc(normed, 1)
            if gain is not None:
                for k in range(KF):
                    dve.wait_ge(normed, k + 1)
                    dve.tensor_scalar(out[:, k, :], out[:, k, :], gain[:, k:k + 1], shift[:, k:k + 1], ALU.mult, ALU.add)


def setup(nc, mem, d):
    load(nc, [(mem.src[:], d["src"]), (mem.dst[:], d["dst"]), (mem.averager[:], d["averager"]), (mem.vecs[:], d["vecs"]),
              (mem.x[:], d["x"])])
    with Phase(nc, "count") as ph:
        node_i = ph.sb("node_i", [P, N], I32)
        node = ph.sb("node", [P, N], F16)
        src_f, dst_f = ph.sb("src_f", [P, T]), ph.sb("dst_f", [P, T])
        src_hot = ph.sb("src_hot", [P, U, N], F16)
        low = [ph.ps(f"low{c}", [P, 512]) for c in range(NC)]
        high = ph.ps("high", [P, 2, 512])
        REST = N - 512
        iota_ready, node_ready, index_ready = ph.sem("iota_ready"), ph.sem("node_ready"), ph.sem("index_ready")
        hot_ready, counted, zeroed = ph.sem("hot_ready"), ph.sem("counted"), ph.sem("zeroed")
        block = ph.block()

        def rest(c):
            return high[0:Q, c // 4, (c % 4) * REST:(c % 4 + 1) * REST]

        @block.gpsimd
        def _(pool):
            pool.iota(node_i[:], pattern=[[1, N]], base=0, channel_multiplier=0).then_inc(iota_ready, 1)

        @block.vector
        def _(dve):
            dve.memset(mem.eps[:], EPS)
            for c in range(NC):
                dve.memset(low[c][:], 0.0).then_inc(zeroed, 1)
            dve.memset(high[:], 0.0).then_inc(zeroed, 1)
            dve.tensor_copy(src_f[0:Q, :], mem.src[:]).then_inc(index_ready, 1)
            dve.tensor_copy(dst_f[0:Q, :], mem.dst[:]).then_inc(index_ready, 1)
            dve.wait_ge(iota_ready, 1)
            dve.tensor_copy(node[:], node_i[:]).then_inc(node_ready, 1)
            dve.wait_ge(node_ready, 1)
            dve.wait_ge(index_ready, 2)
            with dve.Fori(0, T // U) as i:
                t = i * U
                for u in range(U):
                    dve.wait_ge(counted, t + u + 1)
                    dve.tensor_scalar(src_hot[0:Q, u, :], node[0:Q, :], src_f[0:Q, bass.ds(t + u, 1)], None,
                                      ALU.is_equal)
                    dve.tensor_scalar(mem.dst_hot[:, bass.ds(t * N + u * N, N)], node[0:Q, :],
                                      dst_f[0:Q, bass.ds(t + u, 1)], None, ALU.is_equal).then_inc(hot_ready, 1)

        @block.tensor
        def _(pe):
            pe.sem_inc(counted, U)
            pe.wait_ge(zeroed, NC + 1)
            with pe.Fori(0, T // U) as i:
                t = i * U
                for u in range(U):
                    pe.wait_ge(hot_ready, t + u + 1)
                    for c in range(NC):
                        rows = src_hot[0:Q, u, c * Q:(c + 1) * Q]
                        pe.matmul(low[c][0:Q, :], rows, mem.dst_hot[:, bass.ds(t * N + u * N, 512)],
                                  start=False, stop=False, skip_group_check=True)
                        last = pe.matmul(rest(c), rows, mem.dst_hot[:, bass.ds(t * N + (u * N + 512), REST)],
                                         start=False, stop=False, skip_group_check=True)
                    last.then_inc(counted, 1)

        @block.scalar
        def _(act):
            act.wait_ge(counted, T + U)
            for c in range(NC):
                act.activation(mem.counts[:, c, 0:512], low[c][0:Q, :], ACT.Copy)
                act.activation(mem.counts[:, c, 512:N], rest(c), ACT.Copy)


def edge_sums(nc, mem, d, agg):
    with Phase(nc, "sums") as ph:
        rows = ph.sb("rows", [Q, U, F])
        index = ph.sb("index", [Q, U], I32)
        index_ready, gathers = ph.sem("index_ready"), ph.sem("gathers")
        prev_row, dst_row = ph.sb("prev_row", [P, U * Q], I32), ph.sb("dst_row", [P, U * Q], I32)
        keep = ph.sb("keep", [P, U * Q])
        last = ph.sb("last", [Q, T])
        next_dst = ph.sb("next_dst", [Q, T], I32)
        sums = ph.sb("sums", [P, U, KF, Q])
        remainder = ph.sb("remainder", [Q, U, F])
        parts = ph.sb("parts", [Q, U, 3, F], BF16)
        identity = ph.sb("identity", [P, P])
        turned, back = ph.ps("turned", [P, 3, 512]), ph.ps("back", [P, 2, 512])
        low, high = ph.ps("low", [P, KF, 512]), ph.ps("high", [P, 512])
        REST = N - 512
        turned_bank = (0, 1, 0, 1, 2)
        back_bank = (0, 1, 0, 1, 1)
        load(nc, [(next_dst[:], d["dst_next"]), (identity[:], d["identity"][:, 0, 0:P])])
        zeroed, last_ready, rows_loaded, keep_ready, keep_used = (ph.sem(n) for n in (
            "zeroed", "last_ready", "rows_loaded", "keep_ready", "keep_used"))
        gathered = [ph.sem(f"gathered{u}") for u in range(U)]
        turned_ready, summed, back_ready = (ph.sem(n) for n in ("turned_ready", "summed", "back_ready"))
        hi_ready, rest_ready, mid_ready, parts_ready, added = (ph.sem(n) for n in ("hi_ready", "rest_ready", "mid_ready", "parts_ready", "added"))
        block = ph.block()

        def both(u):
            return back[0:Q, back_bank[u], 0:F]

        @block.sync
        def _(sp):
            with sp.Fori(0, T // U) as i:
                sp.wait_ge(keep_used, i + 1)
                for to, of in ((dst_row, d["dst_row"]), (prev_row, d["prev_row"])):
                    sp.dma_start(to[:], of[:, bass.ds(i * (U * Q), U * Q)].partition_broadcast(P)).then_inc(rows_loaded, 16)

        @block.gpsimd
        def _(pool):
            with pool.Fori(0, T // U) as i:
                t = i * U
                for u in range(U):
                    pool.wait_ge(turned_ready, t + u + 1)
                    pool.tensor_copy(index[:, u:u + 1], mem.src[:, bass.ds(t + u, 1)]).then_inc(index_ready, 1)
                    pool.wait_ge(index_ready, t + u + 1)
                    pool.sem_inc(gathers, 1)
                    pool.indirect_dma_start(rows[:, u, :], None, d["x_table"],
                                            bass.IndirectOffsetOnAxis(ap=index[:, u:u + 1], axis=0)
                                            ).then_inc(gathered[u], 16)

        @block.tensor
        def _(pe):
            def turn(tile, u, i):
                pe.wait_ge(gathered[u], i * 16 + 16)
                pe.wait_ge(summed, tile + 1)
                for k in range(KF):
                    ins = pe.transpose(turned[:, turned_bank[u], k * Q:(k + 1) * Q], rows[:, u, k * P:(k + 1) * P], identity[0:Q, 0:Q])
                ins.then_inc(turned_ready, 1)

            def turn_back(tile, u):
                pe.wait_ge(summed, tile + 3)
                pe.wait_ge(rest_ready, tile + (2 if u == U - 1 else 1))
                for k in range(KF):
                    ins = pe.transpose(back[0:Q, back_bank[u], k * P:(k + 1) * P], sums[:, u, k, :], identity[:])
                ins.then_inc(back_ready, 1)

            def add(tile, u):
                pe.wait_ge(parts_ready, tile + 1)
                for part in range(3):
                    for k in range(KF):
                        w = parts[:, u, part, k * P:(k + 1) * P]
                        pe.matmul(low[:, k, :], w, mem.dst_hot[:, bass.ds(tile * N, 512)],
                                  start=False, stop=False, skip_group_check=True)
                        ins = pe.matmul(high[:, k * REST:(k + 1) * REST], w, mem.dst_hot[:, bass.ds(tile * N + 512, REST)],
                                        start=False, stop=False, skip_group_check=True)
                ins.then_inc(added, 1)

            pe.sem_inc(turned_ready, U)
            pe.wait_ge(zeroed, 3)
            for u in range(U):
                turn(u, u, 0)
                if u >= 1:
                    turn_back(u - 1, u - 1)
                if u >= 3:
                    add(u - 3, u - 3)
            with pe.Fori(1, T // U) as i:
                t = i * U
                for u in range(U):
                    turn(t + u, u, i)
                    turn_back(t + (u - 1), (u - 1) % U)
                    add(t + (u - 3), (u - 3) % U)
            turn_back(T - 1, U - 1)
            for tile in range(T - 3, T):
                add(tile, tile % U)

        @block.vector
        def _(dve):
            def compare(i):
                dve.wait_ge(rows_loaded, i * 32 + 32)
                dve.wait_ge(summed, i * U + 2)
                dve.tensor_tensor(keep[:], dst_row[:], prev_row[:], ALU.is_equal).then_inc(keep_used, 1)
                dve.wait_ge(keep_used, i + 2)

            def scan(tile, u):
                dve.wait_ge(turned_ready, tile + (U + 1))
                dve.wait_ge(summed, tile + 2)
                for k in range(KF):
                    ins = dve.tensor_tensor_scan(sums[:, u, k, :], keep[:, u * Q:(u + 1) * Q], turned[:, turned_bank[u], k * Q:(k + 1) * Q],
                                                 sums[:, (u - 1) % U, k, Q - 1:Q], ALU.mult, ALU.add)
                ins.then_inc(summed, 1)

            def split_rest(tile, u):
                dve.wait_ge(hi_ready, tile + 1)
                dve.scalar_tensor_tensor(out=remainder[:, u, :], in0=both(u), scalar=last[:, bass.ds(tile, 1)],
                                         in1=parts[:, u, 0, :], op0=ALU.mult, op1=ALU.subtract).then_inc(rest_ready, 1)

            def split_lo(tile, u):
                dve.wait_ge(mid_ready, tile + 1)
                dve.tensor_tensor(parts[:, u, 2, :], remainder[:, u, :], parts[:, u, 1, :], ALU.subtract).then_inc(parts_ready, 1)

            dve.memset(low[:], 0.0).then_inc(zeroed, 1)
            dve.memset(high[:], 0.0).then_inc(zeroed, 1)
            dve.memset(sums[:, U - 1, :, :], 0.0).then_inc(zeroed, 1)
            dve.tensor_tensor(last[:], mem.dst[:], next_dst[:], ALU.not_equal).then_inc(last_ready, 1)
            dve.sem_inc(keep_used, 1)
            dve.sem_inc(summed, 2)
            dve.sem_inc(rest_ready, 2)
            dve.sem_inc(added, U)
            dve.wait_ge(zeroed, 3)
            dve.wait_ge(last_ready, 1)
            compare(0)
            for u in range(U):
                scan(u, u)
                if u >= 1:
                    split_rest(u - 1, u - 1)
                if u >= 2:
                    split_lo(u - 2, u - 2)
            with dve.Fori(1, T // U) as i:
                t = i * U
                compare(i)
                for u in range(U):
                    scan(t + u, u)
                    split_rest(t + (u - 1), (u - 1) % U)
                    split_lo(t + (u - 2), (u - 2) % U)
            split_rest(T - 1, U - 1)
            split_lo(T - 2, U - 2)
            split_lo(T - 1, U - 1)

        @block.scalar
        def _(act):
            def split_hi(tile, u):
                act.wait_ge(back_ready, tile + 1)
                act.wait_ge(added, tile + 1)
                act.activation(parts[:, u, 0, :], both(u), ACT.Copy, scale=last[:, bass.ds(tile, 1)]).then_inc(hi_ready, 1)

            def split_mid(tile, u):
                act.wait_ge(rest_ready, tile + 3)
                act.activation(parts[:, u, 1, :], remainder[:, u, :], ACT.Copy).then_inc(mid_ready, 1)

            act.wait_ge(last_ready, 1)
            for u in range(U):
                split_hi(u, u)
                if u >= 1:
                    split_mid(u - 1, u - 1)
            with act.Fori(1, T // U) as i:
                t = i * U
                for u in range(U):
                    split_hi(t + u, u)
                    split_mid(t + (u - 1), (u - 1) % U)
            split_mid(T - 1, U - 1)
            act.wait_ge(added, T + U)
            act.activation(agg[:, :, 0:512], low[:], ACT.Copy)
            act.activation(agg[:, :, 512:N], high[:, 0:KF * REST].rearrange("p (k n) -> p k n", k=KF), ACT.Copy)


def gcn_input(nc, mem, d):
    with Phase(nc, "gcn") as g:
        w_gcn, w_enc = g.sb("w_gcn", [P, KF, F]), g.sb("w_enc", [P, KF, P])
        b_enc, rows = g.sb("b_enc", [P, 2]), g.sb("rows", [P, 5])
        agg, hid = g.sb("agg", [P, KF, N]), g.sb("hid", [P, KF, N])
        xe = g.sb("xe", [P, N])
        load(nc, [(w_gcn[:], d["w_gcn"]), (w_enc[:], d["w_enc"]), (b_enc[:], d["b_enc"]), (rows[:], d["part_rows"])])
        edge_sums(nc, mem, d, agg)
        dense(nc, agg, w_gcn, hid, KF, KF, ACT.Relu, vec(mem, 'L0_gnn_b_gcn'))
        with Phase(nc, "xe") as ph:
            product = ph.ps("product", [P, 1024])
            hi, lo = ph.sb("hi", [P, N], F16), ph.sb("lo", [P, N], F16)
            product_ready, bias_ready, xe_ready, hi_ready, lo_ready, parts_ready = (ph.sem(n) for n in (
                "product_ready", "bias_ready", "xe_ready", "hi_ready", "lo_ready", "parts_ready"))
            block = ph.block()

            @block.tensor
            def _(pe):
                for a, b in PIECES:
                    for k in range(KF):
                        last = pe.matmul(product[:, a:b], w_enc[:, k, :], hid[:, k, a:b], start=(k == 0), stop=(k == KF - 1))
                last.then_inc(product_ready, 1)

            @block.vector
            def _(dve):
                dve.tensor_tensor(b_enc[:, 0:1], b_enc[:, 0:1], b_enc[:, 1:2], ALU.add).then_inc(bias_ready, 1)
                dve.memset(mem.xe_parts[:, N:], 0.0)
                dve.wait_ge(product_ready, 1)
                dve.wait_ge(bias_ready, 1)
                dve.tensor_scalar(xe[:], product[:, 0:N], b_enc[:, 0:1], XE_MAX, ALU.add, ALU.min).then_inc(xe_ready, 1)
                dve.wait_ge(xe_ready, 1)
                dve.tensor_scalar(xe[:], xe[:], -XE_MAX, None, ALU.max).then_inc(xe_ready, 1)
                dve.wait_ge(xe_ready, 2)
                dve.tensor_copy(hi[:], xe[:]).then_inc(hi_ready, 1)
                dve.wait_ge(hi_ready, 1)
                dve.tensor_tensor(lo[:], xe[:], hi[:], ALU.subtract).then_inc(lo_ready, 1)
                dve.wait_ge(lo_ready, 1)
                dve.tensor_scalar(lo[:], lo[:], rows[:, 2:3], None, ALU.mult).then_inc(lo_ready, 1)
                dve.wait_ge(lo_ready, 2)
                dve.scalar_tensor_tensor(out=mem.xe_parts[:, 0:N], in0=hi[:], scalar=rows[:, 3:4], in1=lo[:],
                                         op0=ALU.mult, op1=ALU.add).then_inc(parts_ready, 1)
                dve.wait_ge(parts_ready, 1)
                dve.tensor_scalar(mem.xe_parts[:, 0:1], mem.xe_parts[:, 0:1], rows[:, 4:5], None, ALU.mult)


def lstm_weights(nc, d, rec_parts, in_parts):
    with Phase(nc, "weights") as g:
        w_rec, w_in, w_in2 = g.sb("w_rec", [P, KF, 4 * F]), g.sb("w_in", [P, 12, P]), g.sb("w_in2", [P, 12, P])
        part = g.sb("part", [P, 12, P], F16)
        part2 = g.sb("part2", [P, 12, P], F16)
        rows = g.sb("rows", [P, 5])
        load(nc, [(w_rec[:], d["w_rec"]), (w_in[:], d["w_in"]), (w_in2[:], d["w_in2"]), (rows[:], d["part_rows"])])
        with Phase(nc, "parts") as ph:
            scaled, hi_ready, lo_ready = ph.sem("scaled"), ph.sem("hi_ready"), ph.sem("lo_ready")
            block = ph.block()

            @block.vector
            def _(dve):
                dve.tensor_tensor(w_in[:], w_in[:], w_in2[:], ALU.add).then_inc(scaled, 1)
                dve.wait_ge(scaled, 1)
                for lo, hi, s in ((0, 2, W_SCALE), (2, 3, 2 * W_SCALE), (3, 4, W_SCALE)):
                    dve.tensor_scalar(w_rec[:, :, lo * F:hi * F], w_rec[:, :, lo * F:hi * F], s, None, ALU.mult).then_inc(scaled, 1)
                    dve.tensor_scalar(w_in[:, 3 * lo:3 * hi, :], w_in[:, 3 * lo:3 * hi, :], s, None, ALU.mult).then_inc(scaled, 1)
                dve.wait_ge(scaled, 7)
                dve.tensor_copy(rec_parts[:, :, 0, :], w_rec[:]).then_inc(hi_ready, 1)
                dve.tensor_copy(part[:], w_in[:]).then_inc(hi_ready, 1)
                dve.wait_ge(hi_ready, 2)
                dve.tensor_tensor(rec_parts[:, :, 1, :], w_rec[:], rec_parts[:, :, 0, :], ALU.subtract)
                dve.tensor_tensor(part2[:], w_in[:], part[:], ALU.subtract).then_inc(lo_ready, 1)
                dve.wait_ge(lo_ready, 1)
                dve.tensor_scalar(part2[:], part2[:], rows[:, 1:2], None, ALU.mult).then_inc(lo_ready, 1)
                dve.wait_ge(lo_ready, 2)
                dve.scalar_tensor_tensor(out=in_parts[:].rearrange("p g m -> p (g m)"), in0=part[:].rearrange("p g m -> p (g m)"),
                                         scalar=rows[:, 0:1], in1=part2[:].rearrange("p g m -> p (g m)"),
                                         op0=ALU.mult, op1=ALU.add)


def lstms(nc, mem, d):
    with Phase(nc, "lstm") as ph:
        w_rec, w_in = ph.sb("w_rec", [P, KF, 2, 4 * F], F16), ph.sb("w_in", [P, 12, P], F16)
        lstm_weights(nc, d, w_rec, w_in)
        inputs = ph.sb("inputs", [P, UL], F16)
        h_hi, h_lo = ph.sb("h_hi", [P, 2, KF], F16), ph.sb("h_lo", [P, 2, KF], F16)
        acted = ph.sb("acted", [P, 4, 3])
        terms = ph.sb("terms", [P, 2, 3])
        acted_o = ph.sb("acted_o", [P, 3])
        o_scaled, tanh_c = ph.sb("o_scaled", [P, UL, 3]), ph.sb("tanh_c", [P, UL, 3])
        z_rows = ph.sb("z_rows", [P, 1], F16)
        ps_a, ps_b = ph.ps("ps_a", [P, 2, 512]), ph.ps("ps_b", [P, 2, 512])
        ps_oa, ps_ob = ph.ps("ps_oa", [P, 2, 512]), ph.ps("ps_ob", [P, 2, 512])
        cleared = ph.sem("cleared")
        a_ready, oa_ready, b_ready, ob_ready = (ph.sem(n) for n in ("a_ready", "oa_ready", "b_ready", "ob_ready"))
        a_acted, oa_acted, b_acted, ob_acted = (ph.sem(n) for n in ("a_acted", "oa_acted", "b_acted", "ob_acted"))
        a_terms, b_terms, oa_scaled, ob_scaled = (ph.sem(n) for n in ("a_terms", "b_terms", "oa_scaled", "ob_scaled"))
        a_cell, b_cell, a_tanh_c, b_tanh_c = (ph.sem(n) for n in ("a_cell", "b_cell", "a_tanh_c", "b_tanh_c"))
        a_hi, a_lo, b_hi, b_lo, z_hi, z_ready = (ph.sem(n) for n in ("a_hi", "a_lo", "b_hi", "b_lo", "z_hi", "z_ready"))
        h_kept, xe_filled = ph.sem("h_kept"), ph.sem("xe_filled")
        block = ph.block()
        HALF_A, HALF_B = slice(0, 1), slice(1, 3)

        @block.tensor
        def _(pe):
            pe.wait_ge(cleared, 5)
            with pe.Fori(0, STEPS // UL) as i:
                t = i * UL
                for u in range(UL):
                    a, b, oa, ob = (ps[:, u % 2, :] for ps in (ps_a, ps_b, ps_oa, ps_ob))
                    before = (u - 1) % 2

                    def gates(half, of):
                        if of == "ifg":
                            return [(gate, a[:, gate:gate + 1] if half == 0 else b[:, 2 * gate:2 * gate + 1]) for gate in range(3)]
                        return [(3, (oa if half == 0 else ob)[:, 0:1])]

                    def by_hi(half, of, k):
                        for gate, column in gates(half, of):
                            m = gate * F + half * P
                            for part in range(2):
                                ins = pe.matmul(column, w_rec[:, k, part, m:m + P], h_hi[:, before, k:k + 1],
                                                start=False, stop=False, skip_group_check=True)
                        return ins

                    def by_lo(half, of, k):
                        for gate, column in gates(half, of):
                            m = gate * F + half * P
                            ins = pe.matmul(column, w_rec[:, k, 0, m:m + P], h_lo[:, before, k:k + 1],
                                            start=False, stop=False, skip_group_check=True)
                        return ins

                    for half in range(2):
                        for of in ("ifg", "o"):
                            for gate, column in gates(half, of):
                                pe.matmul(column, w_in[:, 3 * gate + half, :], inputs[:, (u - 1) % UL:(u - 1) % UL + 1],
                                          start=gate in (0, 3), stop=False, skip_group_check=True)
                    pe.wait_ge(a_hi, t + u + 1)
                    by_hi(0, "ifg", 0)
                    by_hi(1, "ifg", 0)
                    pe.wait_ge(a_lo, t + u + 1)
                    by_lo(0, "ifg", 0)
                    pe.wait_ge(b_hi, t + u + 1)
                    by_hi(0, "ifg", 1)
                    by_hi(0, "o", 0)
                    by_lo(0, "o", 0)
                    pe.wait_ge(b_lo, t + u + 1)
                    by_lo(0, "ifg", 1).then_inc(a_ready, 1)
                    by_lo(1, "ifg", 0)
                    by_hi(0, "o", 1)
                    by_lo(0, "o", 1).then_inc(oa_ready, 1)
                    by_hi(1, "ifg", 1)
                    by_lo(1, "ifg", 1)
                    pe.wait_ge(z_ready, t + u + 1)
                    for gate in range(3):
                        ins = pe.matmul(b[:, 2 * gate + 1:2 * gate + 2], w_in[:, 3 * gate + 2, :], inputs[:, u:u + 1],
                                        start=False, stop=False, skip_group_check=True)
                    ins.then_inc(b_ready, 1)
                    for k in range(KF):
                        by_hi(1, "o", k)
                        by_lo(1, "o", k)
                    pe.matmul(ob[:, 1:2], w_in[:, 3 * 3 + 2, :], inputs[:, u:u + 1],
                              start=False, stop=False, skip_group_check=True).then_inc(ob_ready, 1)

        @block.scalar
        def _(act):
            with act.Fori(0, STEPS // UL) as i:
                t = i * UL
                for u in range(UL):
                    n = t + u + 1
                    act.wait_ge(a_ready, n)
                    act.activation(acted[:, 0:3, HALF_A], ps_a[:, u % 2, 0:3].rearrange("p (g c) -> p g c", g=3), ACT.Tanh, scale=0.5 / G_SCALE).then_inc(a_acted, 1)
                    act.wait_ge(oa_ready, n)
                    act.activation(acted_o[:, 0:1], ps_oa[:, u % 2, 0:1], ACT.Tanh, scale=0.5 / G_SCALE).then_inc(oa_acted, 1)
                    act.wait_ge(b_ready, n)
                    act.activation(acted[:, 0:3, HALF_B], ps_b[:, u % 2, 0:6].rearrange("p (g c) -> p g c", g=3), ACT.Tanh,
                                   scale=0.5 / G_SCALE).then_inc(b_acted, 1)
                    act.wait_ge(a_cell, n)
                    act.activation(tanh_c[:, u, HALF_A], acted[:, 3, HALF_A], ACT.Tanh, scale=0.5).then_inc(a_tanh_c, 1)
                    act.wait_ge(ob_ready, n)
                    act.activation(acted_o[:, HALF_B], ps_ob[:, u % 2, 0:2], ACT.Tanh, scale=0.5 / G_SCALE).then_inc(ob_acted, 1)
                    act.wait_ge(b_cell, n)
                    act.activation(tanh_c[:, u, HALF_B], acted[:, 3, HALF_B], ACT.Tanh, scale=0.5).then_inc(b_tanh_c, 1)

        @block.vector
        def _(dve):
            dve.memset(inputs[:], 0.0).then_inc(cleared, 1)
            dve.memset(h_hi[:], 0.0).then_inc(cleared, 1)
            dve.memset(h_lo[:], 0.0).then_inc(cleared, 1)
            dve.memset(acted[:, 3, :], 0.0).then_inc(cleared, 1)
            dve.wait_ge(cleared, 4)
            dve.tensor_copy(inputs[:, 0:UL - 1], mem.xe_parts[:, 0:UL - 1]).then_inc(cleared, 1)
            for ready in (a_hi, a_lo, b_hi, b_lo, z_ready):
                dve.sem_inc(ready, 1)
            dve.sem_inc(xe_filled, UL - 1)
            with dve.Fori(0, STEPS // UL) as i:
                t = i * UL
                for u in range(UL):
                    n = t + u + 1
                    even = u % 2

                    def terms_of(cols):
                        return dve.scalar_tensor_tensor(out=terms[:, :, cols], in0=acted[:, 0:2, cols], scalar=1.0,
                                                        in1=acted[:, 2:4, cols], op0=ALU.add, op1=ALU.mult)

                    def cell_of(cols):
                        return dve.scalar_tensor_tensor(out=acted[:, 3, cols], in0=terms[:, 1, cols], scalar=0.5,
                                                        in1=terms[:, 0, cols], op0=ALU.mult, op1=ALU.add)

                    def scale_o(cols):
                        return dve.tensor_scalar(o_scaled[:, u, cols], acted_o[:, cols], 1.0, H_SCALE / 2, ALU.add, ALU.mult)

                    def state(out, rows, j):
                        return dve.tensor_tensor(out, o_scaled[rows, u, j:j + 1], tanh_c[rows, u, j:j + 1], ALU.mult)

                    def state_lo(out, rows, j, hi):
                        return dve.scalar_tensor_tensor(out=out, in0=tanh_c[rows, u, j:j + 1], scalar=o_scaled[rows, u, j:j + 1],
                                                        in1=hi, op0=ALU.mult, op1=ALU.subtract)

                    ALL, Z, Z_LO = slice(0, P), slice(0, 2 * HE), slice(32, 32 + 2 * HE)
                    z_column = inputs[:, (u + 1) % UL:(u + 1) % UL + 1]
                    dve.wait_ge(a_acted, n)
                    terms_of(HALF_A).then_inc(a_terms, 1)
                    dve.wait_ge(a_terms, n)
                    cell_of(HALF_A).then_inc(a_cell, 1)
                    dve.wait_ge(oa_acted, n)
                    scale_o(HALF_A).then_inc(oa_scaled, 1)
                    dve.wait_ge(b_acted, n)
                    terms_of(HALF_B).then_inc(b_terms, 1)
                    dve.wait_ge(a_tanh_c, n)
                    dve.wait_ge(oa_scaled, n)
                    state(h_hi[:, even, 0:1], ALL, 0).then_inc(a_hi, 1)
                    dve.wait_ge(b_terms, n)
                    cell_of(HALF_B).then_inc(b_cell, 1)
                    dve.wait_ge(ob_acted, n)
                    scale_o(HALF_B).then_inc(ob_scaled, 1)
                    dve.wait_ge(a_hi, n + 1)
                    state_lo(h_lo[:, even, 0:1], ALL, 0, h_hi[:, even, 0:1]).then_inc(a_lo, 1)
                    dve.wait_ge(b_tanh_c, n)
                    dve.wait_ge(ob_scaled, n)
                    state(h_hi[:, even, 1:2], ALL, 1).then_inc(b_hi, 1)
                    state(z_rows[Z_LO, :], Z_LO, 2).then_inc(z_hi, 1)
                    dve.wait_ge(b_hi, n + 1)
                    state_lo(h_lo[:, even, 1:2], ALL, 1, h_hi[:, even, 1:2]).then_inc(b_lo, 1)
                    dve.wait_ge(xe_filled, n + 1)
                    state(z_column[Z, :], Z, 2)
                    dve.wait_ge(z_hi, n)
                    state_lo(z_column[Z_LO, :], Z_LO, 2, z_rows[Z_LO, :]).then_inc(z_ready, 1)

        @block.gpsimd
        def _(pool):
            pool.wait_ge(cleared, 5)
            with pool.Fori(0, STEPS // UL) as i:
                t = i * UL
                for u in range(UL):
                    pool.wait_ge(b_hi, t + u + 2)
                    pool.wait_ge(xe_filled, t + (u + UL - 1))
                    pool.tensor_tensor(mem.h_all[:, :, bass.ds(t + u, 1)].rearrange("p k one -> p (k one)"),
                                       o_scaled[:, u, 0:2], tanh_c[:, u, 0:2], ALU.mult).then_inc(h_kept, 1)
                    pool.wait_ge(h_kept, t + u + 1)
                    pool.tensor_copy(inputs[:, (u - 1) % UL:(u - 1) % UL + 1], mem.xe_parts[:, bass.ds(t + (u + UL - 1), 1)]
                                     ).then_inc(xe_filled, 1)


def residual_scaled(nc, x, y, out, scale, at=0):
    with Phase(nc, "res") as ph:
        block = ph.block()

        @block.vector
        def _(dve):
            for k in range(KF):
                dve.scalar_tensor_tensor(out=out[:, k, :], in0=y[:, k, at:at + N], scalar=scale, in1=x[:, k, :],
                                         op0=ALU.mult, op1=ALU.add)


def add_into(nc, out, x, y):
    with Phase(nc, "add") as ph:
        block = ph.block()

        @block.vector
        def _(dve):
            dve.tensor_tensor(out[:], x[:], y[:], ALU.add)


def write_table(nc, nodes, table):
    with Phase(nc, "table") as ph:
        stored = ph.sem("stored")
        block = ph.block()

        @block.sync
        def _(sp):
            sp.dma_start(table.rearrange("(c p) f -> p c f", p=Q), nodes[:]).then_inc(stored, 16)
            sp.wait_ge(stored, 16)


def batch_norm_fixed(nc, mem, x, out, pfx):
    mean, var, gamma, beta = (vec(mem, pfx + n) for n in ("_mean", "_var", "_gamma", "_beta"))
    with Phase(nc, "bn") as ph:
        scale = ph.sb("scale", [P, KF])
        std_ready, scale_ready, scaled = ph.sem("std_ready"), ph.sem("scale_ready"), ph.sem("scaled")
        block = ph.block()

        @block.scalar
        def _(act):
            act.activation(scale[:], var, ACT.Sqrt, bias=mem.eps[:, 0:1]).then_inc(std_ready, 1)

        @block.vector
        def _(dve):
            dve.wait_ge(std_ready, 1)
            dve.reciprocal(scale[:], scale[:]).then_inc(scale_ready, 1)
            dve.wait_ge(scale_ready, 1)
            dve.tensor_tensor(scale[:], scale[:], gamma, ALU.mult).then_inc(scale_ready, 1)
            dve.wait_ge(scale_ready, 2)
            for k in range(KF):
                dve.tensor_scalar(out[:, k, :], x[:, k, :], mean[:, k:k + 1], scale[:, k:k + 1], ALU.subtract,
                                  ALU.mult).then_inc(scaled, 1)
            for k in range(KF):
                dve.wait_ge(scaled, k + 1)
                dve.tensor_scalar(out[:, k, :], out[:, k, :], beta[:, k:k + 1], None, ALU.add)


def gin_messages(nc, mem, d, agg):
    with Phase(nc, "gin") as ph:
        rows, attr = ph.sb("rows", [Q, U, F]), ph.sb("attr", [Q, U, F])
        index = ph.sb("index", [Q, U], I32)
        message, parts = ph.sb("message", [Q, U, F]), ph.sb("parts", [Q, U, 2, F], F16)
        low, high = ph.ps("low", [P, KF, 512]), ph.ps("high", [P, 512])
        REST = N - 512
        zeroed, index_ready, message_ready, hi_ready, parts_ready, added = (ph.sem(n) for n in (
            "zeroed", "index_ready", "message_ready", "hi_ready", "parts_ready", "added"))
        gathers = ph.sem("gathers")
        gathered = [ph.sem(f"gathered{u}") for u in range(U)]
        loaded = [ph.sem(f"loaded{u}") for u in range(U)]
        block = ph.block()

        @block.sync
        def _(sp):
            with sp.Fori(0, T // U) as i:
                t = i * U
                for u in range(U):
                    sp.wait_ge(message_ready, t + u + 1)
                    sp.dma_start(attr[:, u, :], d["edge_attr"][:, bass.ds((t + u) * F, F)]).then_inc(loaded[u], 16)

        @block.gpsimd
        def _(pool):
            with pool.Fori(0, T // U) as i:
                t = i * U
                for u in range(U):
                    pool.wait_ge(message_ready, t + u + 1)
                    pool.tensor_copy(index[:, u:u + 1], mem.src[:, bass.ds(t + u, 1)]).then_inc(index_ready, 1)
                    pool.wait_ge(index_ready, t + u + 1)
                    pool.sem_inc(gathers, 1)
                    pool.indirect_dma_start(rows[:, u, :], None, mem.table,
                                            bass.IndirectOffsetOnAxis(ap=index[:, u:u + 1], axis=0)).then_inc(gathered[u], 16)

        @block.vector
        def _(dve):
            dve.memset(low[:], 0.0).then_inc(zeroed, 1)
            dve.memset(high[:], 0.0).then_inc(zeroed, 1)
            dve.sem_inc(message_ready, U)
            dve.sem_inc(added, U)
            with dve.Fori(0, T // U) as i:
                t = i * U
                for u in range(U):
                    dve.wait_ge(gathered[u], i * 16 + 16)
                    dve.wait_ge(loaded[u], i * 16 + 16)
                    dve.wait_ge(added, t + u + 1)
                    dve.tensor_tensor(message[:, u, :], rows[:, u, :], attr[:, u, :], ALU.add).then_inc(message_ready, 1)
                    dve.wait_ge(hi_ready, t + u + 1)
                    dve.scalar_tensor_tensor(out=parts[:, u, 1, :], in0=message[:, u, :], scalar=0.0, in1=parts[:, u, 0, :],
                                             op0=ALU.max, op1=ALU.subtract).then_inc(parts_ready, 1)

        @block.scalar
        def _(act):
            with act.Fori(0, T // U) as i:
                t = i * U
                for u in range(U):
                    act.wait_ge(message_ready, t + u + (U + 1))
                    act.activation(parts[:, u, 0, :], message[:, u, :], ACT.Relu).then_inc(hi_ready, 1)
            act.wait_ge(added, T + U)
            act.activation(agg[:, :, 0:512], low[:], ACT.Copy)
            act.activation(agg[:, :, 512:N], high[:, 0:KF * REST].rearrange("p (k n) -> p k n", k=KF), ACT.Copy)

        @block.tensor
        def _(pe):
            pe.wait_ge(zeroed, 2)
            with pe.Fori(0, T // U) as i:
                t = i * U
                for u in range(U):
                    pe.wait_ge(parts_ready, t + u + 1)
                    for part in range(2):
                        for k in range(KF):
                            w = parts[:, u, part, k * P:(k + 1) * P]
                            pe.matmul(low[:, k, :], w, mem.dst_hot[:, bass.ds((t + u) * N, 512)],
                                      start=False, stop=False, skip_group_check=True)
                            ins = pe.matmul(high[:, k * REST:(k + 1) * REST], w, mem.dst_hot[:, bass.ds((t + u) * N + 512, REST)],
                                            start=False, stop=False, skip_group_check=True)
                    ins.then_inc(added, 1)


def layer_gin(nc, mem, d):
    with Phase(nc, "l1") as g:
        identity, w1, w2 = (g.sb(n, [P, KF, F]) for n in ("identity", "w1", "w2"))
        nodes = g.sb("nodes", [Q, NC, F])
        agg, f, f2 = (g.sb(n, [P, KF, N]) for n in ("agg", "f", "f2"))
        load(nc, [(identity[:], d["identity"]), (w1[:], d["gin_w1"]), (w2[:], d["gin_w2"])])
        node_major(nc, mem.x, identity, nodes, F)
        write_table(nc, nodes, mem.table)
        gin_messages(nc, mem, d, agg)
        residual_scaled(nc, agg, mem.x, agg, 2.0)
        batch_norm_fixed(nc, mem, agg, f, 'L1_gnn_bn1')
        dense(nc, f, w1, f2, KF, KF, ACT.Gelu, vec(mem, 'L1_gnn_b1'))
        dense(nc, f2, w2, f, KF, KF, ACT.Identity, vec(mem, 'L1_gnn_b2'))
        add_into(nc, agg, agg, f)
        batch_norm_fixed(nc, mem, agg, agg, 'L1_gnn_bn2')
        add_into(nc, mem.x, mem.x, agg)
    layer_norm(nc, mem, mem.x, mem.x)


def attention(nc, mem, d, q, k_, v, out):
    NEG = -1e30
    with Phase(nc, "att") as g:
        v_ones = g.sb("v_ones", [Q, NC, HEADS, 2 * HD])
        no_edge = g.sb("no_edge", [Q, NC, N])
        top = g.sb("top", [Q, NC, HEADS])
        top_rows = g.sb("top_rows", [P, N])
        minus_head = g.sb("minus_head", [P, HEADS, Q])
        identity = g.sb("identity", [P, P])
        load(nc, [(minus_head[:], d["minus_head"]), (identity[:], d["identity"][:, 0, 0:P])])
        with Phase(nc, "mask") as ph:
            turned = ph.ps("turned", [P, 2, 1024])
            turned_ready, evacuated = ph.sem("turned_ready"), ph.sem("evacuated")
            block = ph.block()

            @block.tensor
            def _(pe):
                for c in range(NC):
                    if c >= 2:
                        pe.wait_ge(evacuated, c - 1)
                    for s in range(NC):
                        at = (512 if s == NC - 1 else 0) + (0 if s == NC - 1 else s * Q)
                        ins = pe.transpose(turned[0:Q, c % 2, at:at + Q], mem.counts[:, s, c * Q:(c + 1) * Q], identity[0:Q, 0:Q])
                    ins.then_inc(turned_ready, 1)

            @block.vector
            def _(dve):
                dve.memset(v_ones[:, :, :, HD:2 * HD], 1.0)
                for c in range(NC):
                    dve.tensor_copy(v_ones[:, c, :, 0:HD], v[:, c, :].rearrange("p (h e) -> p h e", h=HEADS))
                for c in range(NC):
                    dve.wait_ge(turned_ready, c + 1)
                    for a, b, at in ((0, 4 * Q, 0), (4 * Q, N, 512)):
                        ins = dve.tensor_scalar(no_edge[:, c, a:b], turned[0:Q, c % 2, at:at + b - a], 0.0, NEG,
                                                ALU.is_equal, ALU.mult)
                    ins.then_inc(evacuated, 1)
        with Phase(nc, "top") as ph:
            scores = ph.ps("scores", [P, 3, 1024])
            rows = ph.ps("rows", [HEADS, 1024])
            scratch = ph.sb("scratch", [Q, 2, N])
            scores_ready, reduced, rows_ready = ph.sem("scores_ready"), ph.sem("reduced"), ph.sem("rows_ready")
            block = ph.block()

            @block.tensor
            def _(pe):
                n = 0
                for c in range(NC):
                    for h in range(HEADS):
                        if n >= 3:
                            pe.wait_ge(reduced, n - 2)
                        p = slice(HD * (h % 4), HD * (h % 4) + HD)
                        for a, b in PIECES:
                            ins = pe.matmul(scores[0:Q, n % 3, a:b], q[p, h // 4, c * Q:(c + 1) * Q], k_[p, h // 4, a:b],
                                            start=True, stop=True)
                        ins.then_inc(scores_ready, 1)
                        n += 1
                pe.wait_ge(reduced, n)
                for c in range(NC):
                    at = 512 if c == NC - 1 else c * Q
                    ins = pe.transpose(rows[:, at:at + Q], top[:, c, :], identity[0:Q, 0:Q])
                ins.then_inc(rows_ready, 1)

            @block.vector
            def _(dve):
                n = 0
                for c in range(NC):
                    for h in range(HEADS):
                        dve.wait_ge(scores_ready, n + 1)
                        if n >= 2:
                            dve.wait_ge(reduced, n - 1)
                        dve.tensor_tensor_reduce(out=scratch[:, n % 2, :], in0=scores[0:Q, n % 3, 0:N], in1=no_edge[:, c, :],
                                                 scale=1.0, scalar=0.0, op0=ALU.add, op1=ALU.max,
                                                 accum_out=top[:, c, h:h + 1]).then_inc(reduced, 1)
                        n += 1
                dve.wait_ge(rows_ready, 1)
                for j in range(0, P, HD):
                    dve.tensor_copy(top_rows[j:j + HEADS, 0:4 * Q], rows[:, 0:4 * Q])
                    dve.tensor_copy(top_rows[j:j + HEADS, 4 * Q:N], rows[:, 512:512 + Q])
        with Phase(nc, "mix") as ph:
            scores = ph.ps("scores", [P, 2, 1024])
            mixed = ph.ps("mixed", [2 * HD, 2, 1024])
            low, weight = ph.sb("low", [Q, 2, N]), ph.sb("weight", [Q, 2, N])
            inverse = ph.sb("inverse", [HD, N])
            scores_ready, low_ready, exp_ready, weight_ready, mixed_ready, head_done = (ph.sem(n) for n in (
                "scores_ready", "low_ready", "exp_ready", "weight_ready", "mixed_ready", "head_done"))
            inverse_ready = ph.sem("inverse_ready")
            block = ph.block()
            todo = [(h, s) for h in range(HEADS) for s in range(NC)]
            rows_of = lambda h: slice(HD * (h % 4), HD * (h % 4) + HEADS)

            @block.tensor
            def _(pe):
                def mix(n):
                    h, s = todo[n]
                    pe.wait_ge(weight_ready, n + 1)
                    if s == 0 and h >= 2:
                        pe.wait_ge(head_done, h - 1)
                    for a, b in PIECES:
                        ins = pe.matmul(mixed[:, h % 2, a:b], v_ones[:, s, h, :], weight[:, n % 2, a:b],
                                        start=(s == 0), stop=(s == NC - 1))
                    ins.then_inc(mixed_ready, 1)

                for n, (h, s) in enumerate(todo):
                    if n >= 2:
                        pe.wait_ge(low_ready, n - 1)
                    p = slice(HD * (h % 4), HD * (h % 4) + HD)
                    for a, b in PIECES:
                        pe.matmul(scores[0:Q, n % 2, a:b], k_[p, h // 4, s * Q:(s + 1) * Q], q[p, h // 4, a:b],
                                  start=True, stop=False)
                        ins = pe.matmul(scores[0:Q, n % 2, a:b], minus_head[rows_of(h), h, :], top_rows[rows_of(h), a:b],
                                        start=False, stop=True)
                    ins.then_inc(scores_ready, 1)
                    if n >= 1:
                        mix(n - 1)
                mix(len(todo) - 1)

            @block.scalar
            def _(act):
                for n in range(len(todo)):
                    act.wait_ge(low_ready, n + 1)
                    act.activation(low[:, n % 2, :], low[:, n % 2, :], ACT.Exp).then_inc(exp_ready, 1)

            @block.vector
            def _(dve):
                def finish(h):
                    dve.wait_ge(mixed_ready, NC * (h + 1))
                    dve.wait_ge(head_done, h)
                    dve.tensor_scalar(inverse[:], mixed[HD:2 * HD, h % 2, 0:N], 1e-8, None, ALU.add).then_inc(inverse_ready, 1)
                    dve.wait_ge(inverse_ready, 2 * h + 1)
                    dve.reciprocal(inverse[:], inverse[:]).then_inc(inverse_ready, 1)
                    dve.wait_ge(inverse_ready, 2 * h + 2)
                    dve.tensor_tensor(out[HD * (h % 4):HD * (h % 4) + HD, h // 4, :], mixed[0:HD, h % 2, 0:N], inverse[:],
                                      ALU.mult).then_inc(head_done, 1)

                for n, (h, s) in enumerate(todo):
                    dve.wait_ge(scores_ready, n + 1)
                    if n >= 2:
                        dve.wait_ge(weight_ready, n - 1)
                    dve.tensor_scalar(low[:, n % 2, :], scores[0:Q, n % 2, 0:N], 0.0, None, ALU.min).then_inc(low_ready, 1)
                    dve.wait_ge(exp_ready, n + 1)
                    if n >= 2:
                        dve.wait_ge(mixed_ready, n - 1)
                    dve.tensor_tensor(weight[:, n % 2, :], low[:, n % 2, :], mem.counts[:, s, :], ALU.mult).then_inc(weight_ready, 1)
                    if s == 1 and h >= 1:
                        finish(h - 1)
                finish(HEADS - 1)


def layer_attention(nc, mem, d):
    with Phase(nc, "l2") as g:
        wo = g.sb("wo", [P, KF, F])
        mixed, y = g.sb("mixed", [P, KF, N]), g.sb("y", [P, KF, N])
        with Phase(nc, "qkv") as g2:
            wq, wk, wv = (g2.sb(n, [P, KF, F]) for n in ("wq", "wk", "wv"))
            q, k_ = g2.sb("q", [P, KF, N]), g2.sb("k", [P, KF, N])
            v = g2.sb("v", [Q, NC, F])
            load(nc, [(wq[:], d["att_wq"]), (wk[:], d["att_wk"]), (wv[:], d["att_wv"]), (wo[:], d["att_wo"])])
            dense(nc, mem.x, wq, q, KF, KF, ACT.Identity, scale=HD ** -0.5)
            dense(nc, mem.x, wk, k_, KF, KF, ACT.Identity)
            node_major(nc, mem.x, wv, v, F)
            attention(nc, mem, d, q, k_, v, mixed)
        dense(nc, mixed, wo, y, KF, KF, ACT.Identity, vec(mem, 'L2_gnn_Wo_b'))
        add_into(nc, y, mem.x, y)
        layer_norm(nc, mem, y, y, vec(mem, 'L2_gnn_ln1_g'), vec(mem, 'L2_gnn_ln1_b'))
        with Phase(nc, "ffn") as g2:
            w1, w2 = g2.sb("w1", [P, KF, 2 * F]), g2.sb("w2", [P, 2 * KF, F])
            hidden = g2.sb("hidden", [P, 2 * KF, N])
            load(nc, [(w1[:], d["att_w1"]), (w2[:], d["att_w2"])])
            dense(nc, y, w1, hidden, KF, 2 * KF, ACT.Gelu, vec(mem, 'L2_gnn_ffn_b1'))
            dense(nc, hidden, w2, mixed, 2 * KF, KF, ACT.Identity, vec(mem, 'L2_gnn_ffn_b2'))
        add_into(nc, y, y, mixed)
        layer_norm(nc, mem, y, y, vec(mem, 'L2_gnn_ln2_g'), vec(mem, 'L2_gnn_ln2_b'))
        add_into(nc, mem.x, mem.x, y)
    layer_norm(nc, mem, mem.x, mem.x)


def loop_attributes(nc, mem, d, loop_ea):
    with Phase(nc, "loops") as ph:
        attr = ph.sb("attr", [Q, U, EF])
        parts = ph.sb("parts", [Q, U, 2, 2 * EF], F16)
        total = ph.ps("total", [2 * EF, 1024])
        inverse = ph.sb("inverse", [EF, N])
        zeroed, loaded, attr_used, hi_ready, parts_ready, added, inverse_ready = (ph.sem(n) for n in (
            "zeroed", "loaded", "attr_used", "hi_ready", "parts_ready", "added", "inverse_ready"))
        block = ph.block()

        @block.sync
        def _(sp):
            with sp.Fori(0, T // U) as i:
                sp.wait_ge(attr_used, i + 1)
                sp.dma_start(attr[:], d["small_attr"][:, bass.ds(i * (U * EF), U * EF)].rearrange("p (u f) -> p u f", u=U)
                             ).then_inc(loaded, 16)

        @block.vector
        def _(dve):
            dve.memset(total[:], 0.0).then_inc(zeroed, 1)
            dve.memset(parts[:, :, 0, EF:], 1.0).then_inc(zeroed, 1)
            dve.memset(parts[:, :, 1, EF:], 0.0).then_inc(zeroed, 1)
            dve.sem_inc(attr_used, 1)
            dve.sem_inc(added, 1)
            with dve.Fori(0, T // U) as i:
                dve.wait_ge(loaded, i * 16 + 16)
                dve.wait_ge(added, i + 1)
                dve.tensor_copy(parts[:, :, 0, 0:EF], attr[:]).then_inc(hi_ready, 1)
                dve.wait_ge(hi_ready, i + 1)
                dve.tensor_tensor(parts[:, :, 1, 0:EF], attr[:], parts[:, :, 0, 0:EF], ALU.subtract).then_inc(parts_ready, 1)
                dve.wait_ge(parts_ready, i + 1)
                dve.sem_inc(attr_used, 1)
            dve.wait_ge(added, T // U + 1)
            dve.tensor_scalar(inverse[:], total[EF:2 * EF, 0:N], 1.0, None, ALU.max).then_inc(inverse_ready, 1)
            dve.wait_ge(inverse_ready, 1)
            dve.reciprocal(inverse[:], inverse[:]).then_inc(inverse_ready, 1)
            dve.wait_ge(inverse_ready, 2)
            dve.tensor_tensor(loop_ea[:], total[0:EF, 0:N], inverse[:], ALU.mult)

        @block.tensor
        def _(pe):
            pe.wait_ge(zeroed, 3)
            with pe.Fori(0, T // U) as i:
                t = i * U
                pe.wait_ge(parts_ready, i + 1)
                for u in range(U):
                    for part in range(2):
                        for a, b in PIECES:
                            ins = pe.matmul(total[:, a:b], parts[:, u, part, :], mem.dst_hot[:, bass.ds((t + u) * N + a, b - a)],
                                            start=False, stop=False, skip_group_check=True)
                ins.then_inc(added, 1)


def gat_scores(nc, mem, d, pfx, scores):
    with Phase(nc, "scores") as ph:
        left, right = ph.sb("left", [Q, U, F]), ph.sb("right", [Q, U, F])
        l_index, r_index = ph.sb("l_index", [Q, U], I32), ph.sb("r_index", [Q, U], I32)
        attr = ph.sb("attr", [EF, 2 * U * Q])
        w_e, att = ph.sb("w_e", [EF, F]), ph.sb("att", [P, F])
        ends = ph.sb("ends", [Q, 2, F])
        z, act_z, weighted = ph.sb("z", [Q, 2, F]), ph.sb("act_z", [Q, 2, F]), ph.sb("weighted", [Q, 2, F])
        from_edge = ph.ps("from_edge", [P, U, 512])
        load(nc, [(w_e[:], d[pfx + "_We"]), (att[:], d[pfx + "_att"].partition_broadcast(P))])
        attr_used, index_ready, from_edge_ready, ends_ready, z_ready, act_ready, weighted_ready, scored = (ph.sem(n) for n in (
            "attr_used", "index_ready", "from_edge_ready", "ends_ready", "z_ready", "act_ready", "weighted_ready", "scored"))
        attr_loaded, gathers = ph.sem("attr_loaded"), ph.sem("gathers")
        left_in = [ph.sem(f"left_in{u}") for u in range(U)]
        right_in = [ph.sem(f"right_in{u}") for u in range(U)]
        block = ph.block()

        @block.sync
        def _(sp):
            with sp.Fori(0, T // U) as i:
                sp.wait_ge(attr_used, i + 1)
                sp.dma_start(attr[:, 0:U * Q], d["small_attr_t"][:, bass.ds(i * (U * Q), U * Q)]).then_inc(attr_loaded, 16)

        @block.gpsimd
        def _(pool):
            with pool.Fori(0, T // U) as i:
                t = i * U
                for u in range(U):
                    pool.wait_ge(ends_ready, t + u + 1)
                    pool.tensor_copy(l_index[:, u:u + 1], mem.src[:, bass.ds(t + u, 1)]).then_inc(index_ready, 1)
                    pool.wait_ge(index_ready, 2 * t + (2 * u + 1))
                    pool.tensor_copy(r_index[:, u:u + 1], mem.dst[:, bass.ds(t + u, 1)]).then_inc(index_ready, 1)
                    pool.wait_ge(index_ready, 2 * t + (2 * u + 2))
                    pool.sem_inc(gathers, 1)
                    pool.indirect_dma_start(left[:, u, :], None, mem.table,
                                            bass.IndirectOffsetOnAxis(ap=l_index[:, u:u + 1], axis=0)).then_inc(left_in[u], 16)
                    pool.indirect_dma_start(right[:, u, :], None, mem.table_r,
                                            bass.IndirectOffsetOnAxis(ap=r_index[:, u:u + 1], axis=0)).then_inc(right_in[u], 16)

        @block.tensor
        def _(pe):
            pe.sem_inc(attr_used, 1)
            pe.sem_inc(ends_ready, U)
            pe.sem_inc(z_ready, U)
            with pe.Fori(0, T // U) as i:
                t = i * U
                pe.wait_ge(attr_loaded, i * 16 + 16)
                for u in range(U):
                    pe.wait_ge(z_ready, t + u + 1)
                    ins = pe.matmul(from_edge[0:Q, u, 0:F], attr[:, u * Q:(u + 1) * Q], w_e[:], start=True, stop=True)
                    ins.then_inc(from_edge_ready, 1)
                pe.wait_ge(from_edge_ready, t + U)
                pe.sem_inc(attr_used, 1)

        @block.vector
        def _(dve):
            with dve.Fori(0, T // U) as i:
                t = i * U
                for u in range(U):
                    n = t + u + 1
                    b = u % 2
                    dve.wait_ge(left_in[u], i * 16 + 16)
                    dve.wait_ge(right_in[u], i * 16 + 16)
                    dve.tensor_tensor(ends[:, b, :], left[:, u, :], right[:, u, :], ALU.add).then_inc(ends_ready, 1)
                    dve.wait_ge(ends_ready, t + (u + U + 1))
                    dve.wait_ge(from_edge_ready, n)
                    dve.tensor_tensor(z[:, b, :], ends[:, b, :], from_edge[0:Q, u, 0:F], ALU.add).then_inc(z_ready, 1)
                    dve.wait_ge(z_ready, t + (u + U + 1))
                    dve.scalar_tensor_tensor(out=act_z[:, b, :], in0=z[:, b, :], scalar=0.2, in1=z[:, b, :],
                                             op0=ALU.mult, op1=ALU.max).then_inc(act_ready, 1)
                    dve.wait_ge(act_ready, n)
                    dve.tensor_tensor(weighted[:, b, :], act_z[:, b, :], att[0:Q, :], ALU.mult).then_inc(weighted_ready, 1)
                    dve.wait_ge(weighted_ready, n)
                    dve.tensor_reduce(scores[:, bass.ds((t + u) * HEADS, HEADS)], weighted[:, b, :].rearrange("p (h e) -> p h e", h=HEADS),
                                      AX, ALU.add).then_inc(scored, 1)


def run_maxima(nc, mem, d, scores, top):
    NEG = -1e30
    G = U * Q
    with Phase(nc, "maxima") as ph:
        next_dst, last = ph.sb("next_dst", [Q, T], I32), ph.sb("last", [Q, T])
        dst_row, prev_row = ph.sb("dst_row", [HEADS, G], I32), ph.sb("prev_row", [HEADS, G], I32)
        begin = ph.sb("begin", [HEADS, G])
        own = ph.sb("own", [Q, U * HEADS])
        running = ph.sb("running", [HEADS, G])
        ends, parts = ph.sb("ends", [Q, U, HEADS]), ph.sb("parts", [Q, U, 72], F16)
        flags = ph.sb("flags", [Q, U, HEADS])
        runs, some = ph.sb("runs", [HEADS, N]), ph.sb("some", [HEADS, N])
        identity = ph.sb("identity", [P, P])
        turned, back, total = ph.ps("turned", [HEADS, 1024]), ph.ps("back", [Q, 512]), ph.ps("total", [72, 1024])
        load(nc, [(next_dst[:], d["dst_next"]), (identity[:], d["identity"][:, 0, 0:P])])
        (zeroed, last_ready, rows_loaded, rows_used, own_ready, turned_ready, begin_ready, scanned, back_ready, flags_ready,
         ends_ready, hi_ready, parts_ready, added, total_ready) = (ph.sem(n) for n in (
            "zeroed", "last_ready", "rows_loaded", "rows_used", "own_ready", "turned_ready", "begin_ready", "scanned", "back_ready",
            "flags_ready", "ends_ready", "hi_ready", "parts_ready", "added", "total_ready"))
        turns = ph.sem("turns")
        block = ph.block()
        at = lambda u: 512 if u == U - 1 else u * Q

        @block.sync
        def _(sp):
            with sp.Fori(0, T // U) as i:
                sp.wait_ge(rows_used, i + 1)
                for to, of in ((dst_row, d["dst_row"]), (prev_row, d["prev_row"])):
                    sp.dma_start(to[:], of[:, bass.ds(i * G, G)].partition_broadcast(HEADS)).then_inc(rows_loaded, 16)

        @block.scalar
        def _(act):
            act.sem_inc(turned_ready, 1)
            with act.Fori(0, T // U) as i:
                act.wait_ge(turned_ready, i + 1)
                act.activation(own[:], scores[:, bass.ds(i * (U * HEADS), U * HEADS)], ACT.Copy).then_inc(own_ready, 1)

        @block.tensor
        def _(pe):
            pe.wait_ge(zeroed, 3)
            with pe.Fori(0, T // U) as i:
                t = i * U
                pe.wait_ge(own_ready, i + 1)
                pe.wait_ge(scanned, i + 1)
                for u in range(U):
                    ins = pe.transpose(turned[:, at(u):at(u) + Q], own[:, u * HEADS:(u + 1) * HEADS], identity[0:Q, 0:Q])
                ins.then_inc(turned_ready, 1)
                pe.wait_ge(scanned, i + 2)
                pe.sem_inc(turns, 1)
                for u in range(U):
                    ins = pe.transpose(back[:, u * HEADS:(u + 1) * HEADS], running[:, u * Q:(u + 1) * Q], identity[0:HEADS, 0:HEADS])
                ins.then_inc(back_ready, 1)
                pe.wait_ge(parts_ready, i + 1)
                for u in range(U):
                    for a, b in PIECES:
                        ins = pe.matmul(total[:, a:b], parts[:, u, :], mem.dst_hot[:, bass.ds((t + u) * N + a, b - a)],
                                        start=False, stop=False, skip_group_check=True)
                ins.then_inc(added, 1)

        @block.vector
        def _(dve):
            dve.memset(total[:], 0.0).then_inc(zeroed, 1)
            dve.memset(parts[:], 0.0).then_inc(zeroed, 1)
            dve.memset(running[:, G - 1:G], NEG).then_inc(zeroed, 1)
            dve.tensor_tensor(last[:], mem.dst[:], next_dst[:], ALU.not_equal).then_inc(last_ready, 1)
            dve.wait_ge(last_ready, 1)
            dve.wait_ge(zeroed, 3)
            dve.sem_inc(rows_used, 1)
            dve.sem_inc(scanned, 1)
            dve.sem_inc(added, 1)
            with dve.Fori(0, T // U) as i:
                dve.wait_ge(rows_loaded, i * 32 + 32)
                dve.tensor_tensor(begin[:], dst_row[:], prev_row[:], ALU.not_equal).then_inc(rows_used, 1)
                dve.wait_ge(rows_used, i + 2)
                dve.tensor_scalar(begin[:], begin[:], NEG, None, ALU.mult).then_inc(begin_ready, 1)
                dve.wait_ge(begin_ready, 2 * i + 1)
                dve.wait_ge(turned_ready, i + 2)
                dve.tensor_tensor_scan(running[:, 0:4 * Q], begin[:, 0:4 * Q], turned[:, 0:4 * Q], running[:, G - 1:G],
                                       ALU.add, ALU.max).then_inc(begin_ready, 1)
                dve.wait_ge(begin_ready, 2 * i + 2)
                dve.tensor_tensor_scan(running[:, 4 * Q:G], begin[:, 4 * Q:G], turned[:, 512:512 + Q], running[:, 4 * Q - 1:4 * Q],
                                       ALU.add, ALU.max).then_inc(scanned, 1)
                dve.wait_ge(added, i + 1)
                dve.tensor_copy(flags[:], last[:, bass.ds(i * U, U)].rearrange("p (u one) -> p u one", one=1).to_broadcast((Q, U, HEADS))
                                ).then_inc(flags_ready, 1)
                dve.wait_ge(flags_ready, i + 1)
                dve.wait_ge(back_ready, i + 1)
                dve.tensor_tensor(ends[:], back[:, 0:U * HEADS].rearrange("p (u h) -> p u h", u=U), flags[:], ALU.mult).then_inc(ends_ready, 1)
                dve.tensor_copy(parts[:, :, 64:64 + HEADS], flags[:])
                dve.wait_ge(ends_ready, i + 1)
                dve.tensor_copy(parts[:, :, 0:HEADS], ends[:]).then_inc(hi_ready, 1)
                dve.wait_ge(hi_ready, i + 1)
                dve.tensor_tensor(parts[:, :, 32:32 + HEADS], ends[:], parts[:, :, 0:HEADS], ALU.subtract).then_inc(parts_ready, 1)
            dve.wait_ge(added, T // U + 1)
            dve.tensor_copy(top[:], total[32:32 + HEADS, 0:N]).then_inc(total_ready, 1)
            dve.tensor_scalar(runs[:], total[64:64 + HEADS, 0:N], 1.0, None, ALU.max).then_inc(total_ready, 1)
            dve.tensor_scalar(some[:], total[64:64 + HEADS, 0:N], 0.0, NEG, ALU.is_equal, ALU.mult).then_inc(total_ready, 1)
            dve.wait_ge(total_ready, 3)
            dve.tensor_tensor(top[:], total[0:HEADS, 0:N], top[:], ALU.add).then_inc(total_ready, 1)
            dve.reciprocal(runs[:], runs[:]).then_inc(total_ready, 1)
            dve.wait_ge(total_ready, 5)
            dve.tensor_tensor(top[:], top[:], runs[:], ALU.mult).then_inc(total_ready, 1)
            dve.wait_ge(total_ready, 6)
            dve.tensor_tensor(top[:], top[:], some[:], ALU.add)


def gat_loops(nc, mem, d, pfx, x, w_l, w_r, w_e, loop_ea, top, loop_exp):
    with Phase(nc, "selfs") as ph:
        z = ph.ps("z", [P, 2, 1024])
        loop_score, rows = ph.ps("loop_score", [HEADS, 1024]), ph.ps("rows", [Q, NC, HEADS])
        z_sb, act_z = ph.sb("z_sb", [P, KF, N]), ph.sb("act_z", [P, KF, N])
        att = ph.sb("att", [P, KF, HEADS])
        nodes = ph.sb("nodes", [Q, NC, HEADS])
        identity = ph.sb("identity", [P, P])
        load(nc, [(att[:], d[pfx + "_att_cols"]), (identity[:], d["identity"][:, 0, 0:P])])
        z_ready, z_out, act_ready, score_ready, top_ready, below, rows_ready, nodes_ready, stored = (ph.sem(n) for n in (
            "z_ready", "z_out", "act_ready", "score_ready", "top_ready", "below", "rows_ready", "nodes_ready", "stored"))
        block = ph.block()

        @block.tensor
        def _(pe):
            for m in range(KF):
                cols = slice(m * P, (m + 1) * P)
                for a, b in PIECES:
                    for k in range(KF):
                        for w in (w_l, w_r):
                            pe.matmul(z[:, m, a:b], w[:, k, cols], x[:, k, a:b], start=(k == 0 and w is w_l), stop=False)
                    ins = pe.matmul(z[:, m, a:b], w_e[:, cols], loop_ea[:, a:b], start=False, stop=True)
                ins.then_inc(z_ready, 1)
            pe.wait_ge(act_ready, KF)
            for a, b in PIECES:
                for k in range(KF):
                    ins = pe.matmul(loop_score[:, a:b], att[:, k, :], act_z[:, k, a:b], start=(k == 0), stop=(k == KF - 1))
            ins.then_inc(score_ready, 1)
            pe.wait_ge(top_ready, 1)
            for c in range(NC):
                ins = pe.transpose(rows[:, c, :], top[:, c * Q:(c + 1) * Q], identity[0:HEADS, 0:HEADS])
            ins.then_inc(rows_ready, 1)

        @block.scalar
        def _(act):
            for m in range(KF):
                act.wait_ge(z_ready, m + 1)
                act.activation(z_sb[:, m, :], z[:, m, 0:N], ACT.Copy).then_inc(z_out, 1)
            act.wait_ge(below, 1)
            act.activation(loop_exp[:], loop_exp[:], ACT.Exp)

        @block.vector
        def _(dve):
            for m in range(KF):
                dve.wait_ge(z_out, m + 1)
                dve.scalar_tensor_tensor(out=act_z[:, m, :], in0=z_sb[:, m, :], scalar=0.2, in1=z_sb[:, m, :],
                                         op0=ALU.mult, op1=ALU.max).then_inc(act_ready, 1)
            dve.wait_ge(score_ready, 1)
            dve.tensor_tensor(top[:], loop_score[:, 0:N], top[:], ALU.max).then_inc(top_ready, 1)
            dve.wait_ge(top_ready, 1)
            dve.tensor_tensor(loop_exp[:], loop_score[:, 0:N], top[:], ALU.subtract).then_inc(below, 1)
            dve.wait_ge(rows_ready, 1)
            dve.tensor_copy(nodes[:], rows[:]).then_inc(nodes_ready, 1)

        @block.sync
        def _(sp):
            sp.wait_ge(nodes_ready, 1)
            sp.dma_start(mem.table_top.rearrange("(c p) h -> p c h", p=Q), nodes[:]).then_inc(stored, 16)
            sp.wait_ge(stored, 16)


def gat_messages(nc, mem, d, scores, num, den):
    with Phase(nc, "mess") as ph:
        rows, top = ph.sb("rows", [Q, U, F]), ph.sb("top", [Q, U, HEADS])
        s_index, d_index = ph.sb("s_index", [Q, U], I32), ph.sb("d_index", [Q, U], I32)
        below, weight = ph.sb("below", [Q, U, HEADS]), ph.sb("weight", [Q, U, HEADS])
        W = F + HEADS
        message, parts = ph.sb("message", [Q, U, W]), ph.sb("parts", [Q, U, 2, W], F16)
        low, high, low_den = ph.ps("low", [P, KF, 512]), ph.ps("high", [P, 512]), ph.ps("low_den", [HEADS, 512])
        REST = N - 512
        (zeroed, index_ready, below_ready, weight_ready, scaled, message_ready, hi_ready, parts_ready, added) = (ph.sem(n) for n in (
            "zeroed", "index_ready", "below_ready", "weight_ready", "scaled", "message_ready", "hi_ready", "parts_ready", "added"))
        gathers = ph.sem("gathers")
        rows_in = [ph.sem(f"rows_in{u}") for u in range(U)]
        top_in = [ph.sem(f"top_in{u}") for u in range(U)]
        block = ph.block()

        @block.gpsimd
        def _(pool):
            with pool.Fori(0, T // U) as i:
                t = i * U
                for u in range(U):
                    pool.wait_ge(scaled, t + u + 1)
                    pool.tensor_copy(s_index[:, u:u + 1], mem.src[:, bass.ds(t + u, 1)]).then_inc(index_ready, 1)
                    pool.wait_ge(index_ready, 2 * t + (2 * u + 1))
                    pool.tensor_copy(d_index[:, u:u + 1], mem.dst[:, bass.ds(t + u, 1)]).then_inc(index_ready, 1)
                    pool.wait_ge(index_ready, 2 * t + (2 * u + 2))
                    pool.sem_inc(gathers, 1)
                    pool.indirect_dma_start(top[:, u, :], None, mem.table_top,
                                            bass.IndirectOffsetOnAxis(ap=d_index[:, u:u + 1], axis=0)).then_inc(top_in[u], 16)
                    pool.indirect_dma_start(rows[:, u, :], None, mem.table,
                                            bass.IndirectOffsetOnAxis(ap=s_index[:, u:u + 1], axis=0)).then_inc(rows_in[u], 16)

        @block.vector
        def _(dve):
            for p in (low, high, low_den):
                dve.memset(p[:], 0.0).then_inc(zeroed, 1)
            dve.sem_inc(scaled, U)
            dve.sem_inc(added, U)
            with dve.Fori(0, T // U) as i:
                t = i * U
                for u in range(U):
                    n = t + u + 1
                    dve.wait_ge(top_in[u], i * 16 + 16)
                    dve.wait_ge(added, n)
                    dve.tensor_tensor(below[:, u, :], scores[:, bass.ds((t + u) * HEADS, HEADS)], top[:, u, :], ALU.subtract
                                      ).then_inc(below_ready, 1)
                    dve.wait_ge(rows_in[u], i * 16 + 16)
                    dve.wait_ge(weight_ready, n)
                    dve.tensor_tensor(message[:, u, 0:F].rearrange("p (h e) -> p h e", h=HEADS),
                                      rows[:, u, :].rearrange("p (h e) -> p h e", h=HEADS),
                                      weight[:, u, :].rearrange("p (h one) -> p h one", one=1).to_broadcast((Q, HEADS, HD)), ALU.mult
                                      ).then_inc(scaled, 1)
                    dve.tensor_copy(message[:, u, F:W], weight[:, u, :]).then_inc(message_ready, 1)
                    dve.wait_ge(hi_ready, n)
                    dve.tensor_tensor(parts[:, u, 1, :], message[:, u, :], parts[:, u, 0, :], ALU.subtract).then_inc(parts_ready, 1)

        @block.scalar
        def _(act):
            with act.Fori(0, T // U) as i:
                t = i * U
                for u in range(U):
                    n = t + u + 1
                    act.wait_ge(below_ready, n)
                    act.activation(weight[:, u, :], below[:, u, :], ACT.Exp).then_inc(weight_ready, 1)
                    act.wait_ge(scaled, t + (u + U + 1))
                    act.wait_ge(message_ready, n)
                    act.activation(parts[:, u, 0, :], message[:, u, :], ACT.Copy).then_inc(hi_ready, 1)
            act.wait_ge(added, T + U)
            act.activation(num[:, :, 0:512], low[:], ACT.Copy)
            act.activation(num[:, :, 512:N], high[:, 0:KF * REST].rearrange("p (k n) -> p k n", k=KF), ACT.Copy)
            act.activation(den[:, 0:512], low_den[:], ACT.Copy)
            act.activation(den[:, 512:N], high[0:HEADS, KF * REST:(KF + 1) * REST], ACT.Copy)

        @block.tensor
        def _(pe):
            pe.wait_ge(zeroed, 3)
            with pe.Fori(0, T // U) as i:
                t = i * U
                for u in range(U):
                    pe.wait_ge(parts_ready, t + u + 1)
                    for part in range(2):
                        for k in range(KF + 1):
                            w = parts[:, u, part, k * P:min((k + 1) * P, W)]
                            m = P if k < KF else HEADS
                            pe.matmul(low[:, k, :] if k < KF else low_den[:], w, mem.dst_hot[:, bass.ds((t + u) * N, 512)],
                                      start=False, stop=False, skip_group_check=True)
                            ins = pe.matmul(high[0:m, k * REST:(k + 1) * REST], w, mem.dst_hot[:, bass.ds((t + u) * N + 512, REST)],
                                            start=False, stop=False, skip_group_check=True)
                    ins.then_inc(added, 1)


def gat_finish(nc, mem, d, xl, loop_exp, num, den, bias, out):
    with Phase(nc, "finish") as ph:
        spread = ph.sb("spread", [HEADS, F])
        load(nc, [(spread[:], d["head_rows"])])
        wide, inverse = ph.ps("wide", [P, KF, 1024]), ph.ps("inverse", [P, KF, 1024])
        den_ready, wide_ready, inverse_ready, scaled = (ph.sem(n) for n in ("den_ready", "wide_ready", "inverse_ready", "scaled"))
        block = ph.block()

        @block.tensor
        def _(pe):
            for k in range(KF):
                for a, b in PIECES:
                    ins = pe.matmul(wide[:, k, a:b], spread[:, k * P:(k + 1) * P], loop_exp[:, a:b], start=True, stop=True)
            ins.then_inc(wide_ready, 1)
            pe.wait_ge(den_ready, 2)
            for k in range(KF):
                for a, b in PIECES:
                    ins = pe.matmul(inverse[:, k, a:b], spread[:, k * P:(k + 1) * P], den[:, a:b], start=True, stop=True)
            ins.then_inc(inverse_ready, 1)

        @block.vector
        def _(dve):
            dve.tensor_tensor(den[:], den[:], loop_exp[:], ALU.add).then_inc(den_ready, 1)
            dve.wait_ge(den_ready, 1)
            dve.reciprocal(den[:], den[:]).then_inc(den_ready, 1)
            dve.wait_ge(wide_ready, 1)
            for k in range(KF):
                dve.tensor_tensor(out[:, k, :], wide[:, k, 0:N], xl[:, k, :], ALU.mult).then_inc(scaled, 1)
            for k in range(KF):
                dve.wait_ge(scaled, k + 1)
                dve.tensor_tensor(out[:, k, :], out[:, k, :], num[:, k, :], ALU.add).then_inc(scaled, 1)
            dve.wait_ge(inverse_ready, 1)
            for k in range(KF):
                dve.wait_ge(scaled, KF + k + 1)
                dve.tensor_tensor(out[:, k, :], out[:, k, :], inverse[:, k, 0:N], ALU.mult).then_inc(scaled, 1)
            for k in range(KF):
                dve.wait_ge(scaled, 2 * KF + k + 1)
                dve.tensor_scalar(out[:, k, :], out[:, k, :], bias[:, k:k + 1], None, ALU.add).then_inc(scaled, 1)


def batch_norm_step(nc, mem, y, gain, shift, x, out):
    with Phase(nc, "bnstep") as ph:
        mean, total, scale = ph.sb("mean", [P, KF]), ph.sb("total", [P, KF]), ph.sb("scale", [P, KF])
        squares = ph.sb("squares", [P, KF, N])
        summed, centred, squared, var_ready, std_ready, chain = (ph.sem(n) for n in (
            "summed", "centred", "squared", "var_ready", "std_ready", "chain"))
        block = ph.block()

        @block.scalar
        def _(act):
            for k in range(KF):
                act.wait_ge(centred, k + 1)
                act.activation(squares[:, k, :], y[:, k, :], ACT.Square).then_inc(squared, 1)
            act.wait_ge(var_ready, 1)
            act.activation(scale[:], total[:], ACT.Sqrt, bias=mem.eps[:, 0:1], scale=1.0 / N).then_inc(std_ready, 1)

        @block.vector
        def _(dve):
            count = [0]

            def link(ins):
                count[0] += 1
                ins.then_inc(chain, 1)
                dve.wait_ge(chain, count[0])

            link(dve.tensor_reduce(mean[:], y[:], AX, ALU.add))
            link(dve.tensor_scalar(mean[:], mean[:], 1.0 / N, None, ALU.mult))
            for k in range(KF):
                dve.tensor_scalar(y[:, k, :], y[:, k, :], mean[:, k:k + 1], None, ALU.subtract).then_inc(centred, 1)
            dve.wait_ge(squared, KF)
            dve.tensor_reduce(total[:], squares[:], AX, ALU.add).then_inc(var_ready, 1)
            dve.wait_ge(std_ready, 1)
            link(dve.reciprocal(scale[:], scale[:]))
            link(dve.tensor_tensor(scale[:], scale[:], gain, ALU.mult))
            for k in range(KF):
                link(dve.tensor_scalar(y[:, k, :], y[:, k, :], scale[:, k:k + 1], shift[:, k:k + 1], ALU.mult, ALU.add))
                link(dve.scalar_tensor_tensor(out=squares[:, k, :], in0=y[:, k, :], scalar=0.01, in1=y[:, k, :],
                                              op0=ALU.mult, op1=ALU.max))
                link(dve.tensor_tensor(out[:, k, :], x[:, k, :], squares[:, k, :], ALU.add))


def gat(nc, mem, d, pfx, x, loop_ea, out):
    with Phase(nc, pfx) as g:
        scores = g.sb("scores", [Q, T * HEADS])
        top, loop_exp = g.sb("top", [HEADS, N]), g.sb("loop_exp", [HEADS, N])
        num, den, xl = g.sb("num", [P, KF, N]), g.sb("den", [HEADS, N]), g.sb("xl", [P, KF, N])
        w_l, w_r, w_e = g.sb("w_l", [P, KF, F]), g.sb("w_r", [P, KF, F]), g.sb("w_e", [EF, F])
        load(nc, [(w_l[:], d[pfx + "_Wl"]), (w_r[:], d[pfx + "_Wr"]), (w_e[:], d[pfx + "_We"])])
        with Phase(nc, "tables") as g2:
            nodes = g2.sb("nodes", [Q, NC, F])
            for w, table in ((w_l, mem.table), (w_r, mem.table_r)):
                node_major(nc, x, w, nodes, F)
                write_table(nc, nodes, table)
        gat_scores(nc, mem, d, pfx, scores)
        run_maxima(nc, mem, d, scores, top)
        gat_loops(nc, mem, d, pfx, x, w_l, w_r, w_e, loop_ea, top, loop_exp)
        dense(nc, x, w_l, xl, KF, KF, ACT.Identity)
        gat_messages(nc, mem, d, scores, num, den)
        gat_finish(nc, mem, d, xl, loop_exp, num, den, vec(mem, f"L3_gnn_{pfx}_b"), out)


def layer_gat(nc, mem, d):
    with Phase(nc, "l3") as g:
        h, y = g.sb("h", [P, KF, N]), g.sb("y", [P, KF, N])
        with Phase(nc, "gats") as g2:
            loop_ea = g2.sb("loop_ea", [EF, N])
            loop_attributes(nc, mem, d, loop_ea)
            gat(nc, mem, d, "g1", mem.x, loop_ea, y)
            batch_norm_step(nc, mem, y, vec(mem, 'L3_gnn_n1_g'), vec(mem, 'L3_gnn_n1_b'), mem.x, h)
            recycle(nc)
            gat(nc, mem, d, "g2", h, loop_ea, y)
            batch_norm_step(nc, mem, y, vec(mem, 'L3_gnn_n2_g'), vec(mem, 'L3_gnn_n2_b'), h, h)
        recycle(nc)
        with Phase(nc, "ff") as g2:
            w1, w2 = g2.sb("w1", [P, KF, 4 * F]), g2.sb("w2", [P, 4 * KF, F])
            hidden = g2.sb("hidden", [P, 4 * KF, N])
            load(nc, [(w1[:], d["ff_w1"]), (w2[:], d["ff_w2"])])
            dense(nc, h, w1, hidden, KF, 4 * KF, ACT.Relu, vec(mem, 'L3_gnn_ff_b1'))
            dense(nc, hidden, w2, y, 4 * KF, KF, ACT.Identity, vec(mem, 'L3_gnn_ff_b2'))
        batch_norm_step(nc, mem, y, vec(mem, 'L3_gnn_n3_g'), vec(mem, 'L3_gnn_n3_b'), h, h)
        add_into(nc, mem.x, mem.x, h)
    layer_norm(nc, mem, mem.x, mem.x)


def layer_recurrent(nc, mem, d):
    with Phase(nc, "l0") as g:
        mem.xe_parts = g.sb("xe_parts", [P, STEPS + UL], F16)
        mem.h_all = g.sb("h_all", [P, KF, STEPS])
        gcn_input(nc, mem, d)
        lstms(nc, mem, d)
        residual_scaled(nc, mem.x, mem.h_all, mem.x, 1.0 / H_SCALE, at=LAG)
    layer_norm(nc, mem, mem.x, mem.x)


def build(nc, d, out, layers=(0, 1, 2, 3)):
    Phase.used.clear()
    with Phase(nc, "mem") as top:
        mem = Memory()
        mem.src, mem.dst = top.sb("src", [Q, T], I32), top.sb("dst", [Q, T], I32)
        mem.averager, mem.vecs, mem.eps = top.sb("averager", [P, P]), top.sb("vecs", [P, N_VEC]), top.sb("eps", [P, 1])
        mem.dst_hot = top.sb("dst_hot", [Q, T * N], F16)
        mem.counts = top.sb("counts", [Q, NC, N])
        mem.x = top.sb("x", [P, KF, N])
        mem.table, mem.table_r = (nc.dram_tensor(n, (N, F), F32).ap() for n in ("table", "table_r"))
        mem.table_top = nc.dram_tensor("table_top", (N, HEADS), F32).ap()
        setup(nc, mem, d)
        for n, layer in enumerate((layer_recurrent, layer_gin, layer_attention, layer_gat)):
            if n in layers:
                layer(nc, mem, d)
                recycle(nc)
        store(nc, mem, d, out)


def store(nc, mem, d, out):
    with Phase(nc, "store") as ph:
        nodes = ph.sb("nodes", [Q, NC, F])
        identity = ph.sb("identity", [P, KF, F])
        load(nc, [(identity[:], d["identity"])])
        node_major(nc, mem.x, identity, nodes, F)
        with Phase(nc, "out") as p2:
            stored = p2.sem("stored")
            block = p2.block()

            @block.sync
            def _(sp):
                sp.dma_start(out.rearrange("(c p) f -> p c f", p=Q), nodes[:]).then_inc(stored, 16)
                sp.wait_ge(stored, 16)



def lay_out(inputs):
    import numpy as np

    x = {k: np.asarray(v) for k, v in inputs.items()}
    blocks = lambda w: np.ascontiguousarray(w.reshape(-1, P, w.shape[-1]).transpose(1, 0, 2))
    a = {}
    a["x"] = blocks(x["x"].T)
    a["x_table"] = x["x"]
    a["dst_row"] = x["dst"].reshape(1, E)
    a["prev_row"] = np.concatenate([[-1], x["dst"][:-1]]).astype(np.int32).reshape(1, E)
    a["dst_next"] = np.ascontiguousarray(np.concatenate([x["dst"][1:], [-1]]).astype(np.int32).reshape(T, Q).T)
    a["src"] = np.ascontiguousarray(x["src"].reshape(T, Q).T)
    a["dst"] = np.ascontiguousarray(x["dst"].reshape(T, Q).T)
    a["averager"] = np.full((P, P), 1.0 / F, np.float32)
    a["identity"] = blocks(np.eye(F, dtype=np.float32))
    a["vecs"] = np.concatenate([x[v].reshape(-1, P).T for v in VECS], axis=1)
    a["w_gcn"] = blocks(x["L0_gnn_W_gcn"].T)
    a["w_enc"], a["b_enc"] = np.zeros((P, KF, P), np.float32), np.zeros((P, 2), np.float32)
    for rows in (XE_HI, XE_LO):
        a["w_enc"][:, :, rows] = blocks(x["L0_gnn_Wih_e"].T)
        a["b_enc"][rows, 0], a["b_enc"][rows, 1] = x["L0_gnn_bih_e"], x["L0_gnn_bhh_e"]
    a["b_enc"][list(ONES), 0] = H_SCALE
    a["w_rec"] = blocks(x["L0_gnn_Whh_d"].T)
    w_in = np.zeros((P, 12, P), np.float32)
    w_in2 = np.zeros((P, 12, P), np.float32)
    copies = (0, HE, 32, 32 + HE)
    for gate in range(4):
        for j in range(KF):
            m = slice(gate * F + j * P, gate * F + (j + 1) * P)
            for r in copies:
                w_in[r:r + HE, 3 * gate + j, :] = x["L0_gnn_Wih_d"][m].T
            for r in ONES:
                w_in[r, 3 * gate + j, :] = x["L0_gnn_bih_d"][m]
                w_in2[r, 3 * gate + j, :] = x["L0_gnn_bhh_d"][m]
        for c in copies:
            for r in copies:
                w_in[r:r + HE, 3 * gate + 2, c:c + HE] = x["L0_gnn_Whh_e"][gate * HE:(gate + 1) * HE].T
            for rows in (XE_HI, XE_LO):
                for j in range(HE):
                    w_in[rows[gate * HE + j], 3 * gate + 2, c + j] = H_SCALE
    a["w_in"], a["w_in2"] = w_in, w_in2
    low_rows = [*range(HE, 2 * HE), *range(32 + HE, 32 + 2 * HE), ONES[1]]
    rows = np.zeros((P, 5), np.float32)
    rows[:, 0] = rows[:, 4] = 1.0
    rows[low_rows, 0], rows[low_rows, 1] = 0.0, 1.0
    rows[XE_LO, 2] = 1.0
    rows[XE_HI + list(ONES), 3] = 1.0
    rows[list(ONES), 4] = 0.0
    a["part_rows"] = rows
    a["edge_attr"] = np.ascontiguousarray(x["edge_attr_256"].reshape(T, Q, F).transpose(1, 0, 2)).reshape(Q, T * F)
    a["gin_w1"], a["gin_w2"] = blocks(x["L1_gnn_W1"].T), blocks(x["L1_gnn_W2"].T)
    for w in ("q", "k", "v"):
        a["att_w" + w] = blocks(x["L2_gnn_W" + w])
    a["att_wo"], a["att_w1"], a["att_w2"] = (blocks(x["L2_gnn_" + n]) for n in ("Wo_w", "ffn_w1", "ffn_w2"))
    small = x["edge_attr_32"]
    a["small_attr"] = np.ascontiguousarray(small.reshape(T, Q, EF).transpose(1, 0, 2)).reshape(Q, T * EF)
    a["small_attr_t"] = small.T
    for g in ("g1", "g2"):
        att = x[f"L3_gnn_{g}_att"]
        a[g + "_Wl"], a[g + "_Wr"], a[g + "_We"] = blocks(x[f"L3_gnn_{g}_Wl"]), blocks(x[f"L3_gnn_{g}_Wr"]), x[f"L3_gnn_{g}_We"]
        a[g + "_att"] = att.reshape(1, F)
        cols = np.zeros((HEADS, HD, HEADS), np.float32)
        for h in range(HEADS):
            cols[h, :, h] = att[h]
        a[g + "_att_cols"] = blocks(cols.reshape(F, HEADS))
    a["ff_w1"], a["ff_w2"] = blocks(x["L3_gnn_ff_W1"]), blocks(x["L3_gnn_ff_W2"])
    a["head_rows"] = np.repeat(np.eye(HEADS, dtype=np.float32), HD, axis=1)
    a["minus_head"] = np.zeros((4, HD, HEADS, Q), np.float32)
    for h in range(HEADS):
        a["minus_head"][:, h, h, :] = -1.0
    a["minus_head"] = a["minus_head"].reshape(P, HEADS, Q)
    return {k: np.ascontiguousarray(v) for k, v in a.items()}


def kernel(**inputs):
    import numpy as np
    import concourse.bacc as bacc
    from concourse.bass_utils import run_bass_kernel_spmd

    nc = bacc.Bacc("TRN2", target_bir_lowering=False, num_devices=1)
    arrays = lay_out(inputs)
    d = {k: nc.dram_tensor(k, a.shape, mybir.dt.from_np(a.dtype), kind="ExternalInput").ap() for k, a in arrays.items()}
    out = nc.dram_tensor("out", (N, F), F32, kind="ExternalOutput").ap()
    build(nc, d, out)
    r = run_bass_kernel_spmd(nc, [arrays], core_ids=[0])
    return r.results[0]["out"]
```

```python
from contextlib import ExitStack

import concourse.bass as bass
from concourse import mybir

F32 = mybir.dt.float32
F16 = mybir.dt.float16
BF16 = mybir.dt.bfloat16
I32 = mybir.dt.int32
ALU = mybir.AluOpType
ACT = mybir.ActivationFunctionType
AX = mybir.AxisListType.X

P = 128
N = 625
Q = 125
NC = N // Q
E = 10625
T = E // Q
F = 256
KF = F // P
EF = 32
HE = 10
HEADS, HD = 8, 32
EPS = 1e-5
PIECES = ((0, 512), (512, N))
U = 5

H_SCALE = 2.0 ** 7
W_SCALE = 2.0 ** 7
G_SCALE = H_SCALE * W_SCALE
XE_MAX = 60000.0
UL = 6
STEPS = 630
LAG = 2
XE_HI = list(range(64, 104))
XE_LO = list(range(104, P)) + list(range(20, 32)) + list(range(52, 56))
ONES = (56, 57)

VECS = ['L0_gnn_b_gcn', 'L1_gnn_b1', 'L1_gnn_b2', 'L1_gnn_bn1_gamma', 'L1_gnn_bn1_beta', 'L1_gnn_bn1_mean',
        'L1_gnn_bn1_var', 'L1_gnn_bn2_gamma', 'L1_gnn_bn2_beta', 'L1_gnn_bn2_mean', 'L1_gnn_bn2_var',
        'L2_gnn_Wo_b', 'L2_gnn_ln1_g', 'L2_gnn_ln1_b', 'L2_gnn_ln2_g', 'L2_gnn_ln2_b', 'L2_gnn_ffn_b1',
        'L2_gnn_ffn_b2', 'L3_gnn_g1_b', 'L3_gnn_g2_b', 'L3_gnn_n1_g', 'L3_gnn_n1_b', 'L3_gnn_n2_g',
        'L3_gnn_n2_b', 'L3_gnn_n3_g', 'L3_gnn_n3_b', 'L3_gnn_ff_b1', 'L3_gnn_ff_b2']
VEC_BLOCKS = {name: {'L2_gnn_ffn_b1': 4, 'L3_gnn_ff_b1': 8}.get(name, 2) for name in VECS}
VEC_AT = {name: sum(VEC_BLOCKS[v] for v in VECS[:i]) for i, name in enumerate(VECS)}
N_VEC = sum(VEC_BLOCKS.values())


class Memory:
    pass


class Phase:

    used = []

    def __init__(self, nc, name):
        self.nc, self.name, self.ctx = nc, f"{name}{nc.next_id()}", ExitStack()

    def __enter__(self):
        self.ctx.__enter__()
        return self

    def __exit__(self, *exc):
        return self.ctx.__exit__(*exc)

    def sb(self, name, shape, dt=F32):
        return self.ctx.enter_context(self.nc.sbuf_tensor(f"{self.name}_{name}", shape, dt))

    def ps(self, name, shape):
        return self.ctx.enter_context(self.nc.psum_tensor(f"{self.name}_{name}", shape, F32))

    def sem(self, name):
        handle = self.nc.alloc_semaphore(f"{self.name}_{name}")
        Phase.used.append(handle)
        return handle

    def block(self):
        return self.ctx.enter_context(self.nc.Block())


def recycle(nc):
    nc.all_engine_barrier()
    nc.clear_and_free_semaphores(list(Phase.used))
    nc.all_engine_barrier()
    Phase.used.clear()


def vec(mem, name):
    at = VEC_AT[name]
    return mem.vecs[:, at:at + VEC_BLOCKS[name]]


def start_load(nc, pairs):
    with Phase(nc, "load") as ph:
        loaded = ph.sem("loaded")
        block = ph.block()

        @block.sync
        def _(sp):
            for to, of in pairs[0::2]:
                sp.dma_start(to, of).then_inc(loaded, 16)

        @block.scalar
        def _(act):
            for to, of in pairs[1::2]:
                act.dma_start(to, of).then_inc(loaded, 16)

    return loaded, 16 * len(pairs)


def finish_load(nc, started):
    with Phase(nc, "loaded") as ph:
        loaded, count = started
        block = ph.block()

        @block.sync
        def _(sp):
            sp.wait_ge(loaded, count)


def load(nc, pairs):
    finish_load(nc, start_load(nc, pairs))


def dense(nc, x, w, out, k_blocks, m_blocks, func, bias=None, scale=1.0):
    with Phase(nc, "dense") as ph:
        product = ph.ps("product", [P, 2, 1024])
        product_ready, evacuated = ph.sem("product_ready"), ph.sem("evacuated")
        block = ph.block()

        @block.tensor
        def _(pe):
            for m in range(m_blocks):
                if m >= 2:
                    pe.wait_ge(evacuated, m - 1)
                for a, b in PIECES:
                    for k in range(k_blocks):
                        last = pe.matmul(product[:, m % 2, a:b], w[:, k, m * P:(m + 1) * P], x[:, k, a:b],
                                         start=(k == 0), stop=(k == k_blocks - 1))
                last.then_inc(product_ready, 1)

        @block.scalar
        def _(act):
            for m in range(m_blocks):
                act.wait_ge(product_ready, m + 1)
                act.activation(out[:, m, 0:N], product[:, m % 2, 0:N], func, scale=scale,
                               bias=0.0 if bias is None else bias[:, m:m + 1]).then_inc(evacuated, 1)


def node_major(nc, x, w, out, cols):
    with Phase(nc, "nodes") as ph:
        product = ph.ps("product", [P, 2, 512])
        product_ready, evacuated = ph.sem("product_ready"), ph.sem("evacuated")
        block = ph.block()

        @block.tensor
        def _(pe):
            for c in range(NC):
                if c >= 2:
                    pe.wait_ge(evacuated, c - 1)
                for k in range(KF):
                    last = pe.matmul(product[0:Q, c % 2, 0:cols], x[:, k, c * Q:(c + 1) * Q], w[:, k, 0:cols],
                                     start=(k == 0), stop=(k == KF - 1))
                last.then_inc(product_ready, 1)

        @block.vector
        def _(dve):
            for c in range(NC):
                dve.wait_ge(product_ready, c + 1)
                dve.tensor_copy(out[:, c, 0:cols], product[0:Q, c % 2, 0:cols]).then_inc(evacuated, 1)


def turn_nodes(nc, mem, x, out):
    with Phase(nc, "turn") as ph:
        rows = ph.ps("rows", [P, 3, 512])
        rows_ready, evacuated = ph.sem("rows_ready"), ph.sem("evacuated")
        block = ph.block()

        @block.tensor
        def _(pe):
            for c in range(NC):
                if c >= 3:
                    pe.wait_ge(evacuated, c - 2)
                for k in range(KF):
                    last = pe.transpose(rows[0:Q, c % 3, k * P:(k + 1) * P], x[:, k, c * Q:(c + 1) * Q], mem.identity[:])
                last.then_inc(rows_ready, 1)

        @block.vector
        def _(dve):
            for c in range(NC):
                dve.wait_ge(rows_ready, c + 1)
                dve.tensor_copy(out[:, c, :], rows[0:Q, c % 3, 0:F]).then_inc(evacuated, 1)


def layer_norm(nc, mem, x, out, gain=None, shift=None):
    with Phase(nc, "ln") as ph:
        mean, var = ph.ps("mean", [P, 1024]), ph.ps("var", [P, 1024])
        centred, squares = ph.sb("centred", [P, KF, N]), ph.sb("squares", [P, KF, N])
        rstd = ph.sb("rstd", [P, N])
        mean_ready, centred_ready, squares_ready = ph.sem("mean_ready"), ph.sem("centred_ready"), ph.sem("squares_ready")
        var_ready, std_ready, rstd_ready, normed = ph.sem("var_ready"), ph.sem("std_ready"), ph.sem("rstd_ready"), ph.sem("normed")
        block = ph.block()

        @block.tensor
        def _(pe):
            for a, b in PIECES:
                for k in range(KF):
                    last = pe.matmul(mean[:, a:b], mem.averager[:], x[:, k, a:b], start=(k == 0), stop=(k == KF - 1))
            last.then_inc(mean_ready, 1)
            pe.wait_ge(squares_ready, KF)
            for a, b in PIECES:
                for k in range(KF):
                    last = pe.matmul(var[:, a:b], mem.averager[:], squares[:, k, a:b], start=(k == 0), stop=(k == KF - 1))
            last.then_inc(var_ready, 1)

        @block.scalar
        def _(act):
            for k in range(KF):
                act.wait_ge(centred_ready, k + 1)
                act.activation(squares[:, k, :], centred[:, k, :], ACT.Square).then_inc(squares_ready, 1)
            act.wait_ge(var_ready, 1)
            act.activation(rstd[:], var[:, 0:N], ACT.Sqrt, bias=mem.eps[:, 0:1]).then_inc(std_ready, 1)

        @block.vector
        def _(dve):
            dve.wait_ge(mean_ready, 1)
            for k in range(KF):
                dve.tensor_tensor(centred[:, k, :], x[:, k, :], mean[:, 0:N], ALU.subtract).then_inc(centred_ready, 1)
            dve.wait_ge(std_ready, 1)
            dve.reciprocal(rstd[:], rstd[:]).then_inc(rstd_ready, 1)
            dve.wait_ge(rstd_ready, 1)
            dve.wait_ge(centred_ready, KF)
            for k in range(KF):
                dve.tensor_tensor(out[:, k, :], centred[:, k, :], rstd[:], ALU.mult).then_inc(normed, 1)
            if gain is not None:
                for k in range(KF):
                    dve.wait_ge(normed, k + 1)
                    dve.tensor_scalar(out[:, k, :], out[:, k, :], gain[:, k:k + 1], shift[:, k:k + 1], ALU.mult, ALU.add)


def setup(nc, mem, d):
    load(nc, [(mem.ends[:], d["ends"])])
    started = start_load(nc, [(mem.averager[:], d["averager"]), (mem.vecs[:], d["vecs"]), (mem.x[:], d["x"]),
                              (mem.next_dst[:], d["dst_next"]), (mem.identity[:], d["identity"]), (mem.spread[:], d["head_rows"])])
    with Phase(nc, "count") as ph:
        node_i = ph.sb("node_i", [P, N], I32)
        node = ph.sb("node", [P, N], F16)
        src_f, dst_f = ph.sb("src_f", [P, T]), ph.sb("dst_f", [P, T])
        src_hot = ph.sb("src_hot", [P, U, N], F16)
        low = [ph.ps(f"low{c}", [P, 512]) for c in range(NC)]
        high = ph.ps("high", [P, 2, 512])
        REST = N - 512
        iota_ready, node_ready, index_ready = ph.sem("iota_ready"), ph.sem("node_ready"), ph.sem("index_ready")
        hot_ready, counted, zeroed = ph.sem("hot_ready"), ph.sem("counted"), ph.sem("zeroed")
        block = ph.block()

        def rest(c):
            return high[0:Q, c // 4, (c % 4) * REST:(c % 4 + 1) * REST]

        @block.gpsimd
        def _(pool):
            pool.iota(node_i[:], pattern=[[1, N]], base=0, channel_multiplier=0).then_inc(iota_ready, 1)

        @block.vector
        def _(dve):
            dve.memset(mem.eps[:], EPS)
            for c in range(NC):
                dve.memset(low[c][:], 0.0).then_inc(zeroed, 1)
            dve.memset(high[:], 0.0).then_inc(zeroed, 1)
            dve.tensor_copy(src_f[0:Q, :], mem.ends[:, 0:T, 0]).then_inc(index_ready, 1)
            dve.tensor_copy(dst_f[0:Q, :], mem.ends[:, 0:T, 1]).then_inc(index_ready, 1)
            dve.wait_ge(iota_ready, 1)
            dve.tensor_copy(node[:], node_i[:]).then_inc(node_ready, 1)
            dve.wait_ge(node_ready, 1)
            dve.wait_ge(index_ready, 2)
            with dve.Fori(0, T // U) as i:
                t = i * U
                for u in range(U):
                    dve.wait_ge(counted, t + u + 1)
                    dve.tensor_scalar(src_hot[0:Q, u, :], node[0:Q, :], src_f[0:Q, bass.ds(t + u, 1)], None,
                                      ALU.is_equal)
                    dve.tensor_scalar(mem.dst_hot[:, bass.ds(t * N + u * N, N)], node[0:Q, :],
                                      dst_f[0:Q, bass.ds(t + u, 1)], None, ALU.is_equal).then_inc(hot_ready, 1)

        @block.tensor
        def _(pe):
            pe.sem_inc(counted, U)
            pe.wait_ge(zeroed, NC + 1)
            with pe.Fori(0, T // U) as i:
                t = i * U
                for u in range(U):
                    pe.wait_ge(hot_ready, t + u + 1)
                    for c in range(NC):
                        rows = src_hot[0:Q, u, c * Q:(c + 1) * Q]
                        pe.matmul(low[c][0:Q, :], rows, mem.dst_hot[:, bass.ds(t * N + u * N, 512)],
                                  start=False, stop=False, skip_group_check=True)
                        last = pe.matmul(rest(c), rows, mem.dst_hot[:, bass.ds(t * N + (u * N + 512), REST)],
                                         start=False, stop=False, skip_group_check=True)
                    last.then_inc(counted, 1)

        @block.scalar
        def _(act):
            act.wait_ge(counted, T + U)
            for c in range(NC):
                act.activation(mem.counts[:, c, 0:512], low[c][0:Q, :], ACT.Copy)
                act.activation(mem.counts[:, c, 512:N], rest(c), ACT.Copy)
    finish_load(nc, started)


def edge_sums(nc, mem, d, agg):
    with Phase(nc, "sums") as ph:
        rows = ph.sb("rows", [Q, U, F])
        index = ph.sb("index", [Q, U], I32)
        index_ready, gathers = ph.sem("index_ready"), ph.sem("gathers")
        prev_row, dst_row = ph.sb("prev_row", [P, U * Q], I32), ph.sb("dst_row", [P, U * Q], I32)
        keep = ph.sb("keep", [P, U * Q])
        last = ph.sb("last", [Q, T])
        sums = ph.sb("sums", [P, U, KF, Q])
        remainder = ph.sb("remainder", [Q, U, F])
        parts = ph.sb("parts", [Q, U, 3, F], BF16)
        identity = mem.identity
        turned, back = ph.ps("turned", [P, 3, 512]), ph.ps("back", [P, 2, 512])
        low, high = ph.ps("low", [P, KF, 512]), ph.ps("high", [P, 512])
        REST = N - 512
        turned_bank = (0, 1, 0, 1, 2)
        back_bank = (0, 1, 0, 1, 1)
        zeroed, last_ready, rows_loaded, keep_used = (ph.sem(n) for n in ("zeroed", "last_ready", "rows_loaded", "keep_used"))
        gathered = [ph.sem(f"gathered{u}") for u in range(U)]
        turned_ready, summed, back_ready = (ph.sem(n) for n in ("turned_ready", "summed", "back_ready"))
        hi_ready, rest_ready, mid_ready, parts_ready, added = (ph.sem(n) for n in ("hi_ready", "rest_ready", "mid_ready", "parts_ready", "added"))
        block = ph.block()

        def both(u):
            return back[0:Q, back_bank[u], 0:F]

        @block.sync
        def _(sp):
            with sp.Fori(0, T // U) as i:
                sp.wait_ge(keep_used, i + 1)
                for to, of in ((dst_row, d["dst_row"]), (prev_row, d["prev_row"])):
                    sp.dma_start(to[:], of[:, bass.ds(i * (U * Q), U * Q)].partition_broadcast(P)).then_inc(rows_loaded, 16)

        @block.gpsimd
        def _(pool):
            with pool.Fori(0, T // U) as i:
                t = i * U
                for u in range(U):
                    pool.wait_ge(turned_ready, t + u + 1)
                    pool.tensor_copy(index[:, u:u + 1], mem.ends[:, bass.ds(t + u, 1), 0]).then_inc(index_ready, 1)
                    pool.wait_ge(index_ready, t + u + 1)
                    pool.sem_inc(gathers, 1)
                    pool.indirect_dma_start(rows[:, u, :], None, d["x_table"],
                                            bass.IndirectOffsetOnAxis(ap=index[:, u:u + 1], axis=0)
                                            ).then_inc(gathered[u], 16)

        @block.tensor
        def _(pe):
            def turn(tile, u, i):
                pe.wait_ge(gathered[u], i * 16 + 16)
                pe.wait_ge(summed, tile + 1)
                for k in range(KF):
                    ins = pe.transpose(turned[:, turned_bank[u], k * Q:(k + 1) * Q], rows[:, u, k * P:(k + 1) * P], identity[0:Q, 0:Q])
                ins.then_inc(turned_ready, 1)

            def turn_back(tile, u):
                pe.wait_ge(summed, tile + 3)
                pe.wait_ge(rest_ready, tile + (2 if u == U - 1 else 1))
                for k in range(KF):
                    ins = pe.transpose(back[0:Q, back_bank[u], k * P:(k + 1) * P], sums[:, u, k, :], identity[:])
                ins.then_inc(back_ready, 1)

            def add(tile, u):
                pe.wait_ge(parts_ready, tile + 1)
                for part in range(3):
                    for k in range(KF):
                        w = parts[:, u, part, k * P:(k + 1) * P]
                        pe.matmul(low[:, k, :], w, mem.dst_hot[:, bass.ds(tile * N, 512)],
                                  start=False, stop=False, skip_group_check=True)
                        ins = pe.matmul(high[:, k * REST:(k + 1) * REST], w, mem.dst_hot[:, bass.ds(tile * N + 512, REST)],
                                        start=False, stop=False, skip_group_check=True)
                ins.then_inc(added, 1)

            pe.sem_inc(turned_ready, U)
            pe.wait_ge(zeroed, 3)
            for u in range(U):
                turn(u, u, 0)
                if u >= 1:
                    turn_back(u - 1, u - 1)
                if u >= 3:
                    add(u - 3, u - 3)
            with pe.Fori(1, T // U) as i:
                t = i * U
                for u in range(U):
                    turn(t + u, u, i)
                    turn_back(t + (u - 1), (u - 1) % U)
                    add(t + (u - 3), (u - 3) % U)
            turn_back(T - 1, U - 1)
            for tile in range(T - 3, T):
                add(tile, tile % U)

        @block.vector
        def _(dve):
            def compare(i):
                dve.wait_ge(rows_loaded, i * 32 + 32)
                dve.wait_ge(summed, i * U + 2)
                dve.tensor_tensor(keep[:], dst_row[:], prev_row[:], ALU.is_equal).then_inc(keep_used, 1)
                dve.wait_ge(keep_used, i + 2)

            def scan(tile, u):
                dve.wait_ge(turned_ready, tile + (U + 1))
                dve.wait_ge(summed, tile + 2)
                for k in range(KF):
                    ins = dve.tensor_tensor_scan(sums[:, u, k, :], keep[:, u * Q:(u + 1) * Q], turned[:, turned_bank[u], k * Q:(k + 1) * Q],
                                                 sums[:, (u - 1) % U, k, Q - 1:Q], ALU.mult, ALU.add)
                ins.then_inc(summed, 1)

            def split_rest(tile, u):
                dve.wait_ge(hi_ready, tile + 1)
                dve.scalar_tensor_tensor(out=remainder[:, u, :], in0=both(u), scalar=last[:, bass.ds(tile, 1)],
                                         in1=parts[:, u, 0, :], op0=ALU.mult, op1=ALU.subtract).then_inc(rest_ready, 1)

            def split_lo(tile, u):
                dve.wait_ge(mid_ready, tile + 1)
                dve.tensor_tensor(parts[:, u, 2, :], remainder[:, u, :], parts[:, u, 1, :], ALU.subtract).then_inc(parts_ready, 1)

            dve.memset(low[:], 0.0).then_inc(zeroed, 1)
            dve.memset(high[:], 0.0).then_inc(zeroed, 1)
            dve.memset(sums[:, U - 1, :, :], 0.0).then_inc(zeroed, 1)
            dve.tensor_tensor(last[:], mem.ends[:, 0:T, 1], mem.next_dst[:], ALU.not_equal).then_inc(last_ready, 1)
            dve.sem_inc(keep_used, 1)
            dve.sem_inc(summed, 2)
            dve.sem_inc(rest_ready, 2)
            dve.sem_inc(added, U)
            dve.wait_ge(zeroed, 3)
            dve.wait_ge(last_ready, 1)
            compare(0)
            for u in range(U):
                scan(u, u)
                if u >= 1:
                    split_rest(u - 1, u - 1)
                if u >= 2:
                    split_lo(u - 2, u - 2)
            with dve.Fori(1, T // U) as i:
                t = i * U
                compare(i)
                for u in range(U):
                    scan(t + u, u)
                    split_rest(t + (u - 1), (u - 1) % U)
                    split_lo(t + (u - 2), (u - 2) % U)
            split_rest(T - 1, U - 1)
            split_lo(T - 2, U - 2)
            split_lo(T - 1, U - 1)

        @block.scalar
        def _(act):
            def split_hi(tile, u):
                act.wait_ge(back_ready, tile + 1)
                act.wait_ge(added, tile + 1)
                act.activation(parts[:, u, 0, :], both(u), ACT.Copy, scale=last[:, bass.ds(tile, 1)]).then_inc(hi_ready, 1)

            def split_mid(tile, u):
                act.wait_ge(rest_ready, tile + 3)
                act.activation(parts[:, u, 1, :], remainder[:, u, :], ACT.Copy).then_inc(mid_ready, 1)

            act.wait_ge(last_ready, 1)
            for u in range(U):
                split_hi(u, u)
                if u >= 1:
                    split_mid(u - 1, u - 1)
            with act.Fori(1, T // U) as i:
                t = i * U
                for u in range(U):
                    split_hi(t + u, u)
                    split_mid(t + (u - 1), (u - 1) % U)
            split_mid(T - 1, U - 1)
            act.wait_ge(added, T + U)
            act.activation(agg[:, :, 0:512], low[:], ACT.Copy)
            act.activation(agg[:, :, 512:N], high[:, 0:KF * REST].rearrange("p (k n) -> p k n", k=KF), ACT.Copy)


def gcn_input(nc, mem, d):
    with Phase(nc, "gcn") as g:
        w_gcn, w_enc = g.sb("w_gcn", [P, KF, F]), g.sb("w_enc", [P, KF, P])
        b_enc, rows = g.sb("b_enc", [P, 2]), g.sb("rows", [P, 5])
        agg, hid = g.sb("agg", [P, KF, N]), g.sb("hid", [P, KF, N])
        xe = g.sb("xe", [P, N])
        started = start_load(nc, [(w_gcn[:], d["w_gcn"]), (w_enc[:], d["w_enc"]), (b_enc[:], d["b_enc"]), (rows[:], d["part_rows"])])
        edge_sums(nc, mem, d, agg)
        finish_load(nc, started)
        dense(nc, agg, w_gcn, hid, KF, KF, ACT.Relu, vec(mem, 'L0_gnn_b_gcn'))
        with Phase(nc, "xe") as ph:
            product = ph.ps("product", [P, 1024])
            hi, lo = ph.sb("hi", [P, N], F16), ph.sb("lo", [P, N], F16)
            product_ready, bias_ready, xe_ready, hi_ready, lo_ready, parts_ready = (ph.sem(n) for n in (
                "product_ready", "bias_ready", "xe_ready", "hi_ready", "lo_ready", "parts_ready"))
            block = ph.block()

            @block.tensor
            def _(pe):
                for a, b in PIECES:
                    for k in range(KF):
                        last = pe.matmul(product[:, a:b], w_enc[:, k, :], hid[:, k, a:b], start=(k == 0), stop=(k == KF - 1))
                last.then_inc(product_ready, 1)

            @block.vector
            def _(dve):
                dve.tensor_tensor(b_enc[:, 0:1], b_enc[:, 0:1], b_enc[:, 1:2], ALU.add).then_inc(bias_ready, 1)
                dve.memset(mem.xe_parts[:, N:], 0.0)
                dve.wait_ge(product_ready, 1)
                dve.wait_ge(bias_ready, 1)
                dve.tensor_scalar(xe[:], product[:, 0:N], b_enc[:, 0:1], XE_MAX, ALU.add, ALU.min).then_inc(xe_ready, 1)
                dve.wait_ge(xe_ready, 1)
                dve.tensor_scalar(xe[:], xe[:], -XE_MAX, None, ALU.max).then_inc(xe_ready, 1)
                dve.wait_ge(xe_ready, 2)
                dve.tensor_copy(hi[:], xe[:]).then_inc(hi_ready, 1)
                dve.wait_ge(hi_ready, 1)
                dve.tensor_tensor(lo[:], xe[:], hi[:], ALU.subtract).then_inc(lo_ready, 1)
                dve.wait_ge(lo_ready, 1)
                dve.tensor_scalar(lo[:], lo[:], rows[:, 2:3], None, ALU.mult).then_inc(lo_ready, 1)
                dve.wait_ge(lo_ready, 2)
                dve.scalar_tensor_tensor(out=mem.xe_parts[:, 0:N], in0=hi[:], scalar=rows[:, 3:4], in1=lo[:],
                                         op0=ALU.mult, op1=ALU.add).then_inc(parts_ready, 1)
                dve.wait_ge(parts_ready, 1)
                dve.tensor_scalar(mem.xe_parts[:, 0:1], mem.xe_parts[:, 0:1], rows[:, 4:5], None, ALU.mult)


def lstm_weights(nc, raw, rec_parts, in_parts):
    with Phase(nc, "weights") as g:
        w_rec, w_in, w_in2, rows = raw
        part = g.sb("part", [P, 12, P], F16)
        part2 = g.sb("part2", [P, 12, P], F16)
        with Phase(nc, "parts") as ph:
            scaled, hi_ready, lo_ready = ph.sem("scaled"), ph.sem("hi_ready"), ph.sem("lo_ready")
            block = ph.block()

            @block.vector
            def _(dve):
                dve.tensor_tensor(w_in[:], w_in[:], w_in2[:], ALU.add).then_inc(scaled, 1)
                dve.wait_ge(scaled, 1)
                for lo, hi, s in ((0, 2, W_SCALE), (2, 3, 2 * W_SCALE), (3, 4, W_SCALE)):
                    dve.tensor_scalar(w_rec[:, :, lo * F:hi * F], w_rec[:, :, lo * F:hi * F], s, None, ALU.mult).then_inc(scaled, 1)
                    dve.tensor_scalar(w_in[:, 3 * lo:3 * hi, :], w_in[:, 3 * lo:3 * hi, :], s, None, ALU.mult).then_inc(scaled, 1)
                dve.wait_ge(scaled, 7)
                dve.tensor_copy(rec_parts[:, :, 0, :], w_rec[:]).then_inc(hi_ready, 1)
                dve.tensor_copy(part[:], w_in[:]).then_inc(hi_ready, 1)
                dve.wait_ge(hi_ready, 2)
                dve.tensor_tensor(rec_parts[:, :, 1, :], w_rec[:], rec_parts[:, :, 0, :], ALU.subtract)
                dve.tensor_tensor(part2[:], w_in[:], part[:], ALU.subtract).then_inc(lo_ready, 1)
                dve.wait_ge(lo_ready, 1)
                dve.tensor_scalar(part2[:], part2[:], rows[:, 1:2], None, ALU.mult).then_inc(lo_ready, 1)
                dve.wait_ge(lo_ready, 2)
                dve.scalar_tensor_tensor(out=in_parts[:].rearrange("p g m -> p (g m)"), in0=part[:].rearrange("p g m -> p (g m)"),
                                         scalar=rows[:, 0:1], in1=part2[:].rearrange("p g m -> p (g m)"),
                                         op0=ALU.mult, op1=ALU.add)


def lstms(nc, mem, raw):
    with Phase(nc, "lstm") as ph:
        w_rec, w_in = ph.sb("w_rec", [P, KF, 2, 4 * F], F16), ph.sb("w_in", [P, 12, P], F16)
        lstm_weights(nc, raw, w_rec, w_in)
        inputs = ph.sb("inputs", [P, UL], F16)
        h_hi, h_lo = ph.sb("h_hi", [P, 2, KF], F16), ph.sb("h_lo", [P, 2, KF], F16)
        acted = ph.sb("acted", [P, 4, 3])
        terms = ph.sb("terms", [P, 2, 3])
        acted_o = ph.sb("acted_o", [P, 3])
        o_scaled, tanh_c = ph.sb("o_scaled", [P, UL, 3]), ph.sb("tanh_c", [P, UL, 3])
        z_rows = ph.sb("z_rows", [P, 1], F16)
        ps_a, ps_b = ph.ps("ps_a", [P, 2, 512]), ph.ps("ps_b", [P, 2, 512])
        ps_oa, ps_ob = ph.ps("ps_oa", [P, 2, 512]), ph.ps("ps_ob", [P, 2, 512])
        cleared = ph.sem("cleared")
        a_ready, oa_ready, b_ready, ob_ready = (ph.sem(n) for n in ("a_ready", "oa_ready", "b_ready", "ob_ready"))
        a_acted, oa_acted, b_acted, ob_acted = (ph.sem(n) for n in ("a_acted", "oa_acted", "b_acted", "ob_acted"))
        a_terms, b_terms, oa_scaled, ob_scaled = (ph.sem(n) for n in ("a_terms", "b_terms", "oa_scaled", "ob_scaled"))
        a_cell, b_cell, a_tanh_c, b_tanh_c = (ph.sem(n) for n in ("a_cell", "b_cell", "a_tanh_c", "b_tanh_c"))
        a_hi, a_lo, b_hi, b_lo, z_hi, z_ready = (ph.sem(n) for n in ("a_hi", "a_lo", "b_hi", "b_lo", "z_hi", "z_ready"))
        h_kept, xe_filled = ph.sem("h_kept"), ph.sem("xe_filled")
        block = ph.block()
        HALF_A, HALF_B = slice(0, 1), slice(1, 3)

        @block.tensor
        def _(pe):
            pe.wait_ge(cleared, 5)
            with pe.Fori(0, STEPS // UL) as i:
                t = i * UL
                for u in range(UL):
                    a, b, oa, ob = (ps[:, u % 2, :] for ps in (ps_a, ps_b, ps_oa, ps_ob))
                    before = (u - 1) % 2

                    def gates(half, of):
                        if of == "ifg":
                            return [(gate, a[:, gate:gate + 1] if half == 0 else b[:, 2 * gate:2 * gate + 1]) for gate in range(3)]
                        return [(3, (oa if half == 0 else ob)[:, 0:1])]

                    def by_hi(half, of, k):
                        for gate, column in gates(half, of):
                            m = gate * F + half * P
                            for part in range(2):
                                ins = pe.matmul(column, w_rec[:, k, part, m:m + P], h_hi[:, before, k:k + 1],
                                                start=False, stop=False, skip_group_check=True)
                        return ins

                    def by_lo(half, of, k):
                        for gate, column in gates(half, of):
                            m = gate * F + half * P
                            ins = pe.matmul(column, w_rec[:, k, 0, m:m + P], h_lo[:, before, k:k + 1],
                                            start=False, stop=False, skip_group_check=True)
                        return ins

                    for half in range(2):
                        for of in ("ifg", "o"):
                            for gate, column in gates(half, of):
                                pe.matmul(column, w_in[:, 3 * gate + half, :], inputs[:, (u - 1) % UL:(u - 1) % UL + 1],
                                          start=gate in (0, 3), stop=False, skip_group_check=True)
                    pe.wait_ge(a_hi, t + u + 1)
                    by_hi(0, "ifg", 0)
                    by_hi(1, "ifg", 0)
                    pe.wait_ge(a_lo, t + u + 1)
                    by_lo(0, "ifg", 0)
                    pe.wait_ge(b_hi, t + u + 1)
                    by_hi(0, "ifg", 1)
                    by_hi(0, "o", 0)
                    by_lo(0, "o", 0)
                    pe.wait_ge(b_lo, t + u + 1)
                    by_lo(0, "ifg", 1).then_inc(a_ready, 1)
                    by_lo(1, "ifg", 0)
                    by_hi(0, "o", 1)
                    by_lo(0, "o", 1).then_inc(oa_ready, 1)
                    by_hi(1, "ifg", 1)
                    by_lo(1, "ifg", 1)
                    pe.wait_ge(z_ready, t + u + 1)
                    for gate in range(3):
                        ins = pe.matmul(b[:, 2 * gate + 1:2 * gate + 2], w_in[:, 3 * gate + 2, :], inputs[:, u:u + 1],
                                        start=False, stop=False, skip_group_check=True)
                    ins.then_inc(b_ready, 1)
                    for k in range(KF):
                        by_hi(1, "o", k)
                        by_lo(1, "o", k)
                    pe.matmul(ob[:, 1:2], w_in[:, 3 * 3 + 2, :], inputs[:, u:u + 1],
                              start=False, stop=False, skip_group_check=True).then_inc(ob_ready, 1)

        @block.scalar
        def _(act):
            with act.Fori(0, STEPS // UL) as i:
                t = i * UL
                for u in range(UL):
                    n = t + u + 1
                    act.wait_ge(a_ready, n)
                    act.activation(acted[:, 0:3, HALF_A], ps_a[:, u % 2, 0:3].rearrange("p (g c) -> p g c", g=3), ACT.Tanh, scale=0.5 / G_SCALE).then_inc(a_acted, 1)
                    act.wait_ge(oa_ready, n)
                    act.activation(acted_o[:, 0:1], ps_oa[:, u % 2, 0:1], ACT.Tanh, scale=0.5 / G_SCALE).then_inc(oa_acted, 1)
                    act.wait_ge(b_ready, n)
                    act.activation(acted[:, 0:3, HALF_B], ps_b[:, u % 2, 0:6].rearrange("p (g c) -> p g c", g=3), ACT.Tanh,
                                   scale=0.5 / G_SCALE).then_inc(b_acted, 1)
                    act.wait_ge(a_cell, n)
                    act.activation(tanh_c[:, u, HALF_A], acted[:, 3, HALF_A], ACT.Tanh, scale=0.5).then_inc(a_tanh_c, 1)
                    act.wait_ge(ob_ready, n)
                    act.activation(acted_o[:, HALF_B], ps_ob[:, u % 2, 0:2], ACT.Tanh, scale=0.5 / G_SCALE).then_inc(ob_acted, 1)
                    act.wait_ge(b_cell, n)
                    act.activation(tanh_c[:, u, HALF_B], acted[:, 3, HALF_B], ACT.Tanh, scale=0.5).then_inc(b_tanh_c, 1)

        @block.vector
        def _(dve):
            dve.memset(inputs[:], 0.0).then_inc(cleared, 1)
            dve.memset(h_hi[:], 0.0).then_inc(cleared, 1)
            dve.memset(h_lo[:], 0.0).then_inc(cleared, 1)
            dve.memset(acted[:, 3, :], 0.0).then_inc(cleared, 1)
            dve.wait_ge(cleared, 4)
            dve.tensor_copy(inputs[:, 0:UL - 1], mem.xe_parts[:, 0:UL - 1]).then_inc(cleared, 1)
            for ready in (a_hi, a_lo, b_hi, b_lo, z_ready):
                dve.sem_inc(ready, 1)
            dve.sem_inc(xe_filled, UL - 1)
            with dve.Fori(0, STEPS // UL) as i:
                t = i * UL
                for u in range(UL):
                    n = t + u + 1
                    even = u % 2

                    def terms_of(cols):
                        return dve.scalar_tensor_tensor(out=terms[:, :, cols], in0=acted[:, 0:2, cols], scalar=1.0,
                                                        in1=acted[:, 2:4, cols], op0=ALU.add, op1=ALU.mult)

                    def cell_of(cols):
                        return dve.scalar_tensor_tensor(out=acted[:, 3, cols], in0=terms[:, 1, cols], scalar=0.5,
                                                        in1=terms[:, 0, cols], op0=ALU.mult, op1=ALU.add)

                    def scale_o(cols):
                        return dve.tensor_scalar(o_scaled[:, u, cols], acted_o[:, cols], 1.0, H_SCALE / 2, ALU.add, ALU.mult)

                    def state(out, rows, j):
                        return dve.tensor_tensor(out, o_scaled[rows, u, j:j + 1], tanh_c[rows, u, j:j + 1], ALU.mult)

                    def state_lo(out, rows, j, hi):
                        return dve.scalar_tensor_tensor(out=out, in0=tanh_c[rows, u, j:j + 1], scalar=o_scaled[rows, u, j:j + 1],
                                                        in1=hi, op0=ALU.mult, op1=ALU.subtract)

                    ALL, Z, Z_LO = slice(0, P), slice(0, 2 * HE), slice(32, 32 + 2 * HE)
                    z_column = inputs[:, (u + 1) % UL:(u + 1) % UL + 1]
                    dve.wait_ge(a_acted, n)
                    terms_of(HALF_A).then_inc(a_terms, 1)
                    dve.wait_ge(a_terms, n)
                    cell_of(HALF_A).then_inc(a_cell, 1)
                    dve.wait_ge(oa_acted, n)
                    scale_o(HALF_A).then_inc(oa_scaled, 1)
                    dve.wait_ge(b_acted, n)
                    terms_of(HALF_B).then_inc(b_terms, 1)
                    dve.wait_ge(a_tanh_c, n)
                    dve.wait_ge(oa_scaled, n)
                    state(h_hi[:, even, 0:1], ALL, 0).then_inc(a_hi, 1)
                    dve.wait_ge(b_terms, n)
                    cell_of(HALF_B).then_inc(b_cell, 1)
                    dve.wait_ge(ob_acted, n)
                    scale_o(HALF_B).then_inc(ob_scaled, 1)
                    dve.wait_ge(a_hi, n + 1)
                    state_lo(h_lo[:, even, 0:1], ALL, 0, h_hi[:, even, 0:1]).then_inc(a_lo, 1)
                    dve.wait_ge(b_tanh_c, n)
                    dve.wait_ge(ob_scaled, n)
                    state(h_hi[:, even, 1:2], ALL, 1).then_inc(b_hi, 1)
                    state(z_rows[Z_LO, :], Z_LO, 2).then_inc(z_hi, 1)
                    dve.wait_ge(b_hi, n + 1)
                    state_lo(h_lo[:, even, 1:2], ALL, 1, h_hi[:, even, 1:2]).then_inc(b_lo, 1)
                    dve.wait_ge(xe_filled, n + 1)
                    state(z_column[Z, :], Z, 2)
                    dve.wait_ge(z_hi, n)
                    state_lo(z_column[Z_LO, :], Z_LO, 2, z_rows[Z_LO, :]).then_inc(z_ready, 1)

        @block.gpsimd
        def _(pool):
            pool.wait_ge(cleared, 5)
            with pool.Fori(0, STEPS // UL) as i:
                t = i * UL
                for u in range(UL):
                    pool.wait_ge(b_hi, t + u + 2)
                    pool.wait_ge(xe_filled, t + (u + UL - 1))
                    pool.tensor_tensor(mem.h_all[:, :, bass.ds(t + u, 1)].rearrange("p k one -> p (k one)"),
                                       o_scaled[:, u, 0:2], tanh_c[:, u, 0:2], ALU.mult).then_inc(h_kept, 1)
                    pool.wait_ge(h_kept, t + u + 1)
                    pool.tensor_copy(inputs[:, (u - 1) % UL:(u - 1) % UL + 1], mem.xe_parts[:, bass.ds(t + (u + UL - 1), 1)]
                                     ).then_inc(xe_filled, 1)


def residual_scaled(nc, x, y, out, scale, at=0):
    with Phase(nc, "res") as ph:
        block = ph.block()

        @block.vector
        def _(dve):
            for k in range(KF):
                dve.scalar_tensor_tensor(out=out[:, k, :], in0=y[:, k, at:at + N], scalar=scale, in1=x[:, k, :],
                                         op0=ALU.mult, op1=ALU.add)


def add_into(nc, out, x, y):
    with Phase(nc, "add") as ph:
        block = ph.block()

        @block.vector
        def _(dve):
            dve.tensor_tensor(out[:], x[:], y[:], ALU.add)


def write_table(nc, nodes, table):
    with Phase(nc, "table") as ph:
        stored = ph.sem("stored")
        block = ph.block()

        @block.sync
        def _(sp):
            sp.dma_start(table.rearrange("(c p) f -> p c f", p=Q), nodes[:]).then_inc(stored, 16)
            sp.wait_ge(stored, 16)


def batch_norm_fixed(nc, mem, x, out, pfx):
    mean, var, gamma, beta = (vec(mem, pfx + n) for n in ("_mean", "_var", "_gamma", "_beta"))
    with Phase(nc, "bn") as ph:
        scale = ph.sb("scale", [P, KF])
        std_ready, scale_ready, scaled = ph.sem("std_ready"), ph.sem("scale_ready"), ph.sem("scaled")
        block = ph.block()

        @block.scalar
        def _(act):
            act.activation(scale[:], var, ACT.Sqrt, bias=mem.eps[:, 0:1]).then_inc(std_ready, 1)

        @block.vector
        def _(dve):
            dve.wait_ge(std_ready, 1)
            dve.reciprocal(scale[:], scale[:]).then_inc(scale_ready, 1)
            dve.wait_ge(scale_ready, 1)
            dve.tensor_tensor(scale[:], scale[:], gamma, ALU.mult).then_inc(scale_ready, 1)
            dve.wait_ge(scale_ready, 2)
            for k in range(KF):
                dve.tensor_scalar(out[:, k, :], x[:, k, :], mean[:, k:k + 1], scale[:, k:k + 1], ALU.subtract,
                                  ALU.mult).then_inc(scaled, 1)
            for k in range(KF):
                dve.wait_ge(scaled, k + 1)
                dve.tensor_scalar(out[:, k, :], out[:, k, :], beta[:, k:k + 1], None, ALU.add)


def gin_messages(nc, mem, d, agg):
    with Phase(nc, "gin") as ph:
        rows, attr = ph.sb("rows", [Q, U, F]), ph.sb("attr", [Q, U, F])
        index = ph.sb("index", [Q, U], I32)
        message, parts = ph.sb("message", [Q, U, F]), ph.sb("parts", [Q, U, 2, F], F16)
        low, high = ph.ps("low", [P, KF, 512]), ph.ps("high", [P, 512])
        REST = N - 512
        zeroed, index_ready, message_ready, hi_ready, parts_ready, added = (ph.sem(n) for n in (
            "zeroed", "index_ready", "message_ready", "hi_ready", "parts_ready", "added"))
        gathers = ph.sem("gathers")
        gathered = [ph.sem(f"gathered{u}") for u in range(U)]
        loaded = [ph.sem(f"loaded{u}") for u in range(U)]
        block = ph.block()

        @block.sync
        def _(sp):
            with sp.Fori(0, T // U) as i:
                t = i * U
                for u in range(U):
                    sp.wait_ge(message_ready, t + u + 1)
                    sp.dma_start(attr[:, u, :], d["edge_attr"][:, bass.ds((t + u) * F, F)]).then_inc(loaded[u], 16)

        @block.gpsimd
        def _(pool):
            with pool.Fori(0, T // U) as i:
                t = i * U
                for u in range(U):
                    pool.wait_ge(index_ready, t + u + 1)
                    pool.sem_inc(gathers, 1)
                    pool.indirect_dma_start(rows[:, u, :], None, mem.table,
                                            bass.IndirectOffsetOnAxis(ap=index[:, u:u + 1], axis=0)).then_inc(gathered[u], 16)

        @block.vector
        def _(dve):
            dve.memset(low[:], 0.0).then_inc(zeroed, 1)
            dve.memset(high[:], 0.0).then_inc(zeroed, 1)
            def next_index(tile, u):
                dve.tensor_copy(index[:, u:u + 1], mem.ends[:, bass.ds(tile, 1), 0]).then_inc(index_ready, 1)

            for u in range(U):
                next_index(u, u)
            dve.sem_inc(message_ready, U)
            dve.sem_inc(added, U)
            with dve.Fori(0, T // U) as i:
                t = i * U
                for u in range(U + 1):
                    if u < U:
                        dve.wait_ge(gathered[u], i * 16 + 16)
                        dve.wait_ge(loaded[u], i * 16 + 16)
                        dve.wait_ge(added, t + u + 1)
                        dve.tensor_tensor(message[:, u, :], rows[:, u, :], attr[:, u, :], ALU.add).then_inc(message_ready, 1)
                    if u >= 1:
                        dve.wait_ge(hi_ready, t + u)
                        dve.scalar_tensor_tensor(out=parts[:, u - 1, 1, :], in0=message[:, u - 1, :], scalar=0.0,
                                                 in1=parts[:, u - 1, 0, :], op0=ALU.max, op1=ALU.subtract).then_inc(parts_ready, 1)
                    if u < U:
                        dve.wait_ge(message_ready, t + (u + U + 1))
                        next_index(t + (u + U), u)

        @block.scalar
        def _(act):
            with act.Fori(0, T // U) as i:
                t = i * U
                for u in range(U):
                    act.wait_ge(message_ready, t + u + (U + 1))
                    act.activation(parts[:, u, 0, :], message[:, u, :], ACT.Relu).then_inc(hi_ready, 1)
            act.wait_ge(added, T + U)
            act.activation(agg[:, :, 0:512], low[:], ACT.Copy)
            act.activation(agg[:, :, 512:N], high[:, 0:KF * REST].rearrange("p (k n) -> p k n", k=KF), ACT.Copy)

        @block.tensor
        def _(pe):
            pe.wait_ge(zeroed, 2)
            with pe.Fori(0, T // U) as i:
                t = i * U
                for u in range(U):
                    pe.wait_ge(parts_ready, t + u + 1)
                    for part in range(2):
                        for k in range(KF):
                            w = parts[:, u, part, k * P:(k + 1) * P]
                            pe.matmul(low[:, k, :], w, mem.dst_hot[:, bass.ds((t + u) * N, 512)],
                                      start=False, stop=False, skip_group_check=True)
                            ins = pe.matmul(high[:, k * REST:(k + 1) * REST], w, mem.dst_hot[:, bass.ds((t + u) * N + 512, REST)],
                                            start=False, stop=False, skip_group_check=True)
                    ins.then_inc(added, 1)


def layer_gin(nc, mem, d):
    with Phase(nc, "l1") as g:
        w1, w2 = (g.sb(n, [P, KF, F]) for n in ("w1", "w2"))
        nodes = g.sb("nodes", [Q, NC, F])
        agg, f, f2 = (g.sb(n, [P, KF, N]) for n in ("agg", "f", "f2"))
        started = start_load(nc, [(w1[:], d["gin_w1"]), (w2[:], d["gin_w2"])])
        turn_nodes(nc, mem, mem.x, nodes)
        write_table(nc, nodes, mem.table)
        gin_messages(nc, mem, d, agg)
        finish_load(nc, started)
        residual_scaled(nc, agg, mem.x, agg, 2.0)
        batch_norm_fixed(nc, mem, agg, f, 'L1_gnn_bn1')
        dense(nc, f, w1, f2, KF, KF, ACT.Gelu, vec(mem, 'L1_gnn_b1'))
        dense(nc, f2, w2, f, KF, KF, ACT.Identity, vec(mem, 'L1_gnn_b2'))
        add_into(nc, agg, agg, f)
        batch_norm_fixed(nc, mem, agg, agg, 'L1_gnn_bn2')
        add_into(nc, mem.x, mem.x, agg)
    layer_norm(nc, mem, mem.x, mem.x)


def stack_heads(nc, selectors, x, parts_of_x, out, kinds):
    hi, lo = parts_of_x
    with Phase(nc, "stack") as ph:
        stacked = ph.ps("stacked", [P, 4, 1024])
        hi_ready, lo_ready, stacked_ready, evacuated = (ph.sem(n) for n in ("hi_ready", "lo_ready", "stacked_ready", "evacuated"))
        block = ph.block()

        @block.tensor
        def _(pe):
            for h in range(HEADS):
                if h % 4 == 0:
                    pe.wait_ge(lo_ready, h // 4 + 1)
                if h >= 4:
                    pe.wait_ge(evacuated, h - 3)
                p = slice(HD * (h % 4), HD * (h % 4) + HD)
                for a, b in PIECES:
                    pe.matmul(stacked[:, h % 4, a:b], selectors[p, kinds[0], :], hi[p, h // 4, a:b], start=True, stop=False)
                    ins = pe.matmul(stacked[:, h % 4, a:b], selectors[p, kinds[1], :], lo[p, h // 4, a:b], start=False, stop=True)
                ins.then_inc(stacked_ready, 1)

        @block.scalar
        def _(act):
            for k in range(KF):
                act.activation(hi[:, k, :], x[:, k, :], ACT.Copy).then_inc(hi_ready, 1)
            for h in range(HEADS):
                act.wait_ge(stacked_ready, h + 1)
                act.activation(out[:, h, :], stacked[:, h % 4, 0:N], ACT.Copy).then_inc(evacuated, 1)

        @block.vector
        def _(dve):
            for k in range(KF):
                dve.wait_ge(hi_ready, k + 1)
                dve.tensor_tensor(lo[:, k, :], x[:, k, :], hi[:, k, :], ALU.subtract).then_inc(lo_ready, 1)


def attention(nc, mem, d, q, k_, v, total, out):
    NEG = -1e30
    LEAST = -60000.0
    with Phase(nc, "att") as g:
        v_ones = g.sb("v_ones", [Q, NC, HEADS, 2, 2 * HD], F16)
        top_rows = g.sb("top_rows", [2 * HD, N], F16)
        q_heads, k_heads = g.sb("q_heads", [P, HEADS, N], F16), g.sb("k_heads", [P, HEADS, N], F16)
        minus_head = g.sb("minus_head", [2 * HD, HEADS, Q], F16)
        identity, spread = mem.identity, mem.spread
        eps_rows = g.sb("eps_rows", [HEADS, N])
        with Phase(nc, "maxima") as g1:
            no_edge = g1.sb("no_edge", [Q, NC, N])
            top = g1.sb("top", [Q, NC, HEADS])
            with Phase(nc, "stacks") as g2:
                selectors = g2.sb("selectors", [P, 4, P], F16)
                with Phase(nc, "constants") as g3:
                    minus, select = g3.sb("minus", [2 * HD, HEADS, Q]), g3.sb("select", [P, 4, P])
                    load(nc, [(minus[:], d["minus_head"]), (select[:], d["selectors"])])
                    with Phase(nc, "mask") as ph:
                        turned = ph.ps("turned", [P, 2, 1024])
                        turned_ready, evacuated, hi_ready = ph.sem("turned_ready"), ph.sem("evacuated"), ph.sem("hi_ready")
                        block = ph.block()

                        @block.tensor
                        def _(pe):
                            for c in range(NC):
                                if c >= 2:
                                    pe.wait_ge(evacuated, c - 1)
                                for s in range(NC):
                                    at = (512 if s == NC - 1 else 0) + (0 if s == NC - 1 else s * Q)
                                    ins = pe.transpose(turned[0:Q, c % 2, at:at + Q], mem.counts[:, s, c * Q:(c + 1) * Q], identity[0:Q, 0:Q])
                                ins.then_inc(turned_ready, 1)

                        @block.scalar
                        def _(act):
                            act.activation(selectors[:], select[:], ACT.Copy)
                            act.activation(minus_head[:], minus[:], ACT.Copy)
                            for c in range(NC):
                                act.activation(v_ones[:, c, :, 0, 0:HD], v[:, c, :].rearrange("p (h e) -> p h e", h=HEADS), ACT.Copy
                                               ).then_inc(hi_ready, 1)

                        @block.gpsimd
                        def _(pool):
                            pool.memset(v_ones[:, :, :, 0, HD:2 * HD], 1.0)
                            pool.memset(v_ones[:, :, :, 1, HD:2 * HD], 0.0)
                            pool.memset(top_rows[:], 0.0)

                        @block.vector
                        def _(dve):
                            for c in range(NC):
                                dve.wait_ge(turned_ready, c + 1)
                                for a, b, at in ((0, 4 * Q, 0), (4 * Q, N, 512)):
                                    ins = dve.tensor_scalar(no_edge[:, c, a:b], turned[0:Q, c % 2, at:at + b - a], 0.0, NEG,
                                                            ALU.is_equal, ALU.mult)
                                ins.then_inc(evacuated, 1)
                            for c in range(NC):
                                dve.wait_ge(hi_ready, c + 1)
                                dve.tensor_tensor(v_ones[:, c, :, 1, 0:HD], v[:, c, :].rearrange("p (h e) -> p h e", h=HEADS),
                                                  v_ones[:, c, :, 0, 0:HD], ALU.subtract)
                hi, lo = g2.sb("hi", [P, KF, N], F16), g2.sb("lo", [P, KF, N], F16)
                stack_heads(nc, selectors, q, (hi, lo), q_heads, (0, 1))
                stack_heads(nc, selectors, k_, (hi, lo), k_heads, (2, 3))
            with Phase(nc, "top") as ph:
                scores = ph.ps("scores", [P, 3, 1024])
                rows = ph.ps("rows", [HEADS, 1024])
                scratch = ph.sb("scratch", [Q, 2, N])
                scores_ready, reduced, rows_ready, hi_ready, below_ready, exp_ready = (ph.sem(n) for n in (
                    "scores_ready", "reduced", "rows_ready", "hi_ready", "below_ready", "exp_ready"))
                block = ph.block()

                @block.tensor
                def _(pe):
                    n = 0
                    for c in range(NC):
                        for h in range(HEADS):
                            if n >= 3:
                                pe.wait_ge(reduced, n - 2)
                            for a, b in PIECES:
                                ins = pe.matmul(scores[0:Q, n % 3, a:b], q_heads[:, h, c * Q:(c + 1) * Q], k_heads[:, h, a:b],
                                                start=True, stop=True)
                            ins.then_inc(scores_ready, 1)
                            n += 1
                    pe.wait_ge(reduced, n)
                    for c in range(NC):
                        at = 512 if c == NC - 1 else c * Q
                        ins = pe.transpose(rows[:, at:at + Q], top[:, c, :], identity[0:Q, 0:Q])
                    ins.then_inc(rows_ready, 1)

                @block.vector
                def _(dve):
                    n = 0
                    for c in range(NC):
                        for h in range(HEADS):
                            dve.wait_ge(scores_ready, n + 1)
                            if n >= 2:
                                dve.wait_ge(reduced, n - 1)
                            dve.tensor_tensor_reduce(out=scratch[:, n % 2, :], in0=scores[0:Q, n % 3, 0:N], in1=no_edge[:, c, :],
                                                     scale=1.0, scalar=LEAST, op0=ALU.add, op1=ALU.max,
                                                     accum_out=top[:, c, h:h + 1]).then_inc(reduced, 1)
                            n += 1
                    dve.wait_ge(rows_ready, 1)
                    halves = ((slice(0, 4 * Q), slice(0, 4 * Q)), (slice(4 * Q, N), slice(512, 512 + Q)))
                    for cols, of in halves:
                        dve.tensor_copy(top_rows[0:HEADS, cols], rows[:, of]).then_inc(hi_ready, 1)
                    for n, (cols, of) in enumerate(halves):
                        dve.wait_ge(hi_ready, n + 1)
                        dve.tensor_tensor(top_rows[HD:HD + HEADS, cols], rows[:, of], top_rows[0:HEADS, cols], ALU.subtract)
                        dve.tensor_scalar(eps_rows[:, cols], rows[:, of], -1.0, 0.0, ALU.mult, ALU.max).then_inc(below_ready, 1)
                    dve.wait_ge(below_ready, 2)
                    dve.tensor_scalar(eps_rows[:], eps_rows[:], 80.0, None, ALU.min).then_inc(below_ready, 1)
                    dve.wait_ge(exp_ready, 1)
                    dve.tensor_scalar(eps_rows[:], eps_rows[:], 1e-8, None, ALU.mult)

                @block.scalar
                def _(act):
                    act.wait_ge(below_ready, 3)
                    act.activation(eps_rows[:], eps_rows[:], ACT.Exp).then_inc(exp_ready, 1)
        with Phase(nc, "mix") as ph:
            scores = ph.ps("scores", [P, 2, 1024])
            mixed = ph.ps("mixed", [2 * HD, 2, 1024])
            exps, weight = ph.sb("exps", [Q, 2, N]), ph.sb("weight", [Q, 2, N])
            parts = ph.sb("parts", [Q, 3, 2, N], F16)
            scores_ready, exp_ready, weight_ready, hi_ready, parts_ready, mixed_ready = (ph.sem(n) for n in (
                "scores_ready", "exp_ready", "weight_ready", "hi_ready", "parts_ready", "mixed_ready"))
            values_out, total_ready, eps_ready, inverse_ready = (ph.sem(n) for n in ("values_out", "total_ready", "eps_ready", "inverse_ready"))
            block = ph.block()
            todo = [(h, s) for h in range(HEADS) for s in range(NC)]
            STEPS_MIX = len(todo)

            @block.tensor
            def _(pe):
                def mix(n):
                    h, s = todo[n]
                    pe.wait_ge(parts_ready, n + 1)
                    if s == 0 and h >= 2:
                        pe.wait_ge(values_out, h - 1)
                        pe.wait_ge(total_ready, h - 1)
                    for values, weights in ((0, 0), (1, 0), (0, 1)):
                        for a, b in PIECES:
                            ins = pe.matmul(mixed[:, h % 2, a:b], v_ones[:, s, h, values, :], parts[:, n % 3, weights, a:b],
                                            start=(s == 0 and values == weights == 0), stop=(s == NC - 1 and weights == 1))
                    ins.then_inc(mixed_ready, 1)

                for n, (h, s) in enumerate(todo):
                    if n >= 2:
                        pe.wait_ge(exp_ready, n - 1)
                    for a, b in PIECES:
                        pe.matmul(scores[0:Q, n % 2, a:b], k_heads[:, h, s * Q:(s + 1) * Q], q_heads[:, h, a:b],
                                  start=True, stop=False)
                        ins = pe.matmul(scores[0:Q, n % 2, a:b], minus_head[:, h, :], top_rows[:, a:b],
                                        start=False, stop=True)
                    ins.then_inc(scores_ready, 1)
                    if n >= 2:
                        mix(n - 2)
                mix(STEPS_MIX - 2)
                mix(STEPS_MIX - 1)
                pe.wait_ge(exp_ready, STEPS_MIX)
                for k in range(KF):
                    for a, b in PIECES:
                        ins = pe.matmul(scores[:, k, a:b], spread[:, k * P:(k + 1) * P], eps_rows[:, a:b], start=True, stop=True)
                ins.then_inc(eps_ready, 1)

            @block.scalar
            def _(act):
                def split_hi(n):
                    act.wait_ge(weight_ready, n + 1)
                    if n >= 3:
                        act.wait_ge(mixed_ready, n - 2)
                    act.activation(parts[:, n % 3, 0, :], weight[:, n % 2, :], ACT.Copy).then_inc(hi_ready, 1)

                def values(h):
                    act.wait_ge(mixed_ready, NC * (h + 1))
                    act.activation(out[HD * (h % 4):HD * (h % 4) + HD, h // 4, :], mixed[0:HD, h % 2, 0:N], ACT.Copy).then_inc(values_out, 1)

                for n, (h, s) in enumerate(todo):
                    act.wait_ge(scores_ready, n + 1)
                    if n >= 2:
                        act.wait_ge(weight_ready, n - 1)
                    act.activation(exps[:, n % 2, :], scores[0:Q, n % 2, 0:N], ACT.Exp).then_inc(exp_ready, 1)
                    if n >= 1:
                        split_hi(n - 1)
                    if s == 3 and h >= 1:
                        values(h - 1)
                split_hi(STEPS_MIX - 1)
                values(HEADS - 1)

            @block.vector
            def _(dve):
                def split_lo(n):
                    dve.wait_ge(hi_ready, n + 1)
                    dve.tensor_tensor(parts[:, n % 3, 1, :], weight[:, n % 2, :], parts[:, n % 3, 0, :], ALU.subtract).then_inc(parts_ready, 1)

                def totals(h):
                    dve.wait_ge(values_out, h + 1)
                    dve.tensor_copy(total[HD * (h % 4):HD * (h % 4) + HD, h // 4, :], mixed[HD:2 * HD, h % 2, 0:N]).then_inc(total_ready, 1)

                for n, (h, s) in enumerate(todo):
                    dve.wait_ge(exp_ready, n + 1)
                    if n >= 2:
                        dve.wait_ge(parts_ready, n - 1)
                    dve.scalar_tensor_tensor(out=weight[:, n % 2, :], in0=exps[:, n % 2, :], scalar=1.0, in1=mem.counts[:, s, :],
                                             op0=ALU.min, op1=ALU.mult).then_inc(weight_ready, 1)
                    if n >= 1:
                        split_lo(n - 1)
                    if s == 4 and h >= 1:
                        totals(h - 1)
                split_lo(STEPS_MIX - 1)
                totals(HEADS - 1)
                dve.wait_ge(total_ready, HEADS)
                dve.wait_ge(eps_ready, 1)
                for k in range(KF):
                    dve.tensor_tensor(total[:, k, :], total[:, k, :], scores[:, k, 0:N], ALU.add).then_inc(total_ready, 1)
                for k in range(KF):
                    dve.wait_ge(total_ready, HEADS + k + 1)
                    dve.reciprocal(total[:, k, :], total[:, k, :]).then_inc(inverse_ready, 1)
                for k in range(KF):
                    dve.wait_ge(inverse_ready, k + 1)
                    dve.tensor_tensor(out[:, k, :], out[:, k, :], total[:, k, :], ALU.mult)


def layer_attention(nc, mem, d):
    with Phase(nc, "l2") as g:
        wo = g.sb("wo", [P, KF, F])
        mixed, y = g.sb("mixed", [P, KF, N]), g.sb("y", [P, KF, N])
        with Phase(nc, "qkv") as g2:
            q, k_ = g2.sb("q", [P, KF, N]), g2.sb("k", [P, KF, N])
            v = g2.sb("v", [Q, NC, F])
            with Phase(nc, "project") as g3:
                wq, wk, wv = (g3.sb(n, [P, KF, F]) for n in ("wq", "wk", "wv"))
                load(nc, [(wq[:], d["att_wq"]), (wk[:], d["att_wk"]), (wv[:], d["att_wv"]), (wo[:], d["att_wo"])])
                dense(nc, mem.x, wq, q, KF, KF, ACT.Identity, scale=HD ** -0.5)
                dense(nc, mem.x, wk, k_, KF, KF, ACT.Identity)
                node_major(nc, mem.x, wv, v, F)
            attention(nc, mem, d, q, k_, v, y, mixed)
        with Phase(nc, "ffn") as g2:
            w1, w2 = g2.sb("w1", [P, KF, 2 * F]), g2.sb("w2", [P, 2 * KF, F])
            hidden = g2.sb("hidden", [P, 2 * KF, N])
            started = start_load(nc, [(w1[:], d["att_w1"]), (w2[:], d["att_w2"])])
            dense(nc, mixed, wo, y, KF, KF, ACT.Identity, vec(mem, 'L2_gnn_Wo_b'))
            add_into(nc, y, mem.x, y)
            layer_norm(nc, mem, y, y, vec(mem, 'L2_gnn_ln1_g'), vec(mem, 'L2_gnn_ln1_b'))
            finish_load(nc, started)
            dense(nc, y, w1, hidden, KF, 2 * KF, ACT.Gelu, vec(mem, 'L2_gnn_ffn_b1'))
            dense(nc, hidden, w2, mixed, 2 * KF, KF, ACT.Identity, vec(mem, 'L2_gnn_ffn_b2'))
        add_into(nc, y, y, mixed)
        layer_norm(nc, mem, y, y, vec(mem, 'L2_gnn_ln2_g'), vec(mem, 'L2_gnn_ln2_b'))
        add_into(nc, mem.x, mem.x, y)
    layer_norm(nc, mem, mem.x, mem.x)


def loop_attributes(nc, mem, d, loop_ea):
    with Phase(nc, "loops") as ph:
        attr = ph.sb("attr", [Q, T, EF])
        parts = ph.sb("parts", [Q, T, 3 * EF], F16)
        total = ph.ps("total", [3 * EF, 1024])
        inverse = ph.sb("inverse", [EF, N])
        load(nc, [(attr[:], d["small_attr"])])
        zeroed, hi_ready, parts_ready, added, inverse_ready, sum_ready = (ph.sem(n) for n in (
            "zeroed", "hi_ready", "parts_ready", "added", "inverse_ready", "sum_ready"))
        block = ph.block()

        @block.gpsimd
        def _(pool):
            pool.memset(parts[:, :, 2 * EF:], 1.0).then_inc(parts_ready, 1)

        @block.scalar
        def _(act):
            act.activation(parts[:, :, 0:EF], attr[:], ACT.Copy).then_inc(hi_ready, 1)

        @block.vector
        def _(dve):
            dve.memset(total[:], 0.0).then_inc(zeroed, 1)
            dve.wait_ge(hi_ready, 1)
            dve.tensor_tensor(parts[:, :, EF:2 * EF], attr[:], parts[:, :, 0:EF], ALU.subtract).then_inc(parts_ready, 1)
            dve.wait_ge(added, T // U)
            dve.tensor_scalar(inverse[:], total[2 * EF:3 * EF, 0:N], 1.0, None, ALU.max).then_inc(inverse_ready, 1)
            dve.tensor_copy(loop_ea[:], total[0:EF, 0:N]).then_inc(sum_ready, 1)
            dve.wait_ge(inverse_ready, 1)
            dve.reciprocal(inverse[:], inverse[:]).then_inc(inverse_ready, 1)
            dve.wait_ge(sum_ready, 1)
            dve.tensor_tensor(loop_ea[:], total[EF:2 * EF, 0:N], loop_ea[:], ALU.add).then_inc(sum_ready, 1)
            dve.wait_ge(inverse_ready, 2)
            dve.wait_ge(sum_ready, 2)
            dve.tensor_tensor(loop_ea[:], loop_ea[:], inverse[:], ALU.mult)

        @block.tensor
        def _(pe):
            pe.wait_ge(zeroed, 1)
            pe.wait_ge(parts_ready, 2)
            with pe.Fori(0, T // U) as i:
                t = i * U
                for u in range(U):
                    for a, b in PIECES:
                        ins = pe.matmul(total[:, a:b], parts[:, bass.ds(t + u, 1), :].rearrange("p one f -> p (one f)"),
                                        mem.dst_hot[:, bass.ds((t + u) * N + a, b - a)], start=False, stop=False, skip_group_check=True)
                ins.then_inc(added, 1)


def gat_scores(nc, mem, d, w_e, att, scores, top):
    NEG = -1e30
    G, GROUPS = U * Q, T // U
    with Phase(nc, "scores") as ph:
        left, right = ph.sb("left", [Q, U, F]), ph.sb("right", [Q, U, F])
        index = ph.sb("index", [Q, U, 2], I32)
        attr = ph.sb("attr", [EF, U, Q])
        fifth, act_z, weighted = (ph.sb(n, [Q, 3, F]) for n in ("fifth", "act_z", "weighted"))
        slot = (0, 1, 2, 0, 1)
        last = ph.sb("last", [Q, T])
        dst_row, prev_row = ph.sb("dst_row", [HEADS, G], I32), ph.sb("prev_row", [HEADS, G], I32)
        begin = ph.sb("begin", [HEADS, G])
        own = ph.sb("own", [Q, U * HEADS])
        running = ph.sb("running", [HEADS, G])
        run_ends, parts = ph.sb("run_ends", [Q, U, HEADS]), ph.sb("parts", [Q, U, 72], F16)
        flags = ph.sb("flags", [Q, U, HEADS])
        runs = ph.sb("runs", [HEADS, N])
        some = begin[:, 0:N]
        identity = mem.identity
        z = ph.ps("z", [P, 3, 512])
        turned, back, total = ph.ps("turned", [HEADS, 1024]), ph.ps("back", [Q, 512]), ph.ps("total", [72, 1024])
        index_ready, z_ready, fifth_ready, act_ready, weighted_ready, scored = (ph.sem(n) for n in (
            "index_ready", "z_ready", "fifth_ready", "act_ready", "weighted_ready", "scored"))
        gathers = ph.sem("gathers")
        left_in = [ph.sem(f"left_in{u}") for u in range(U)]
        right_in = [ph.sem(f"right_in{u}") for u in range(U)]
        attr_in = [ph.sem(f"attr_in{u}") for u in range(U)]
        (zeroed, last_ready, rows_loaded, rows_used, own_ready, turned_ready, begin_ready, scanned, back_ready, flags_ready,
         run_ends_ready, hi_ready, parts_ready, added, total_ready) = (ph.sem(n) for n in (
            "zeroed", "last_ready", "rows_loaded", "rows_used", "own_ready", "turned_ready", "begin_ready", "scanned", "back_ready",
            "flags_ready", "run_ends_ready", "hi_ready", "parts_ready", "added", "total_ready"))
        turns = ph.sem("turns")
        block = ph.block()
        at = lambda u: 512 if u == U - 1 else u * Q

        @block.sync
        def _(sp):
            with sp.Fori(0, GROUPS) as i:
                t = i * U
                for u in range(U):
                    sp.wait_ge(z_ready, t + u + 1)
                    sp.dma_start(attr[:, u, :], d["small_attr_t"][:, bass.ds((t + u) * Q, Q)]).then_inc(attr_in[u], 16)
                sp.wait_ge(rows_used, i + 1)
                for to, of in ((dst_row, d["dst_row"]), (prev_row, d["prev_row"])):
                    sp.dma_start(to[:], of[:, bass.ds(i * G, G)].partition_broadcast(HEADS)).then_inc(rows_loaded, 16)

        @block.gpsimd
        def _(pool):
            with pool.Fori(0, GROUPS) as i:
                t = i * U
                for u in range(U):
                    pool.wait_ge(index_ready, t + u + 1)
                    pool.sem_inc(gathers, 1)
                    pool.indirect_dma_start(left[:, u, :], None, mem.table,
                                            bass.IndirectOffsetOnAxis(ap=index[:, u, 0:1], axis=0)).then_inc(left_in[u], 16)
                    pool.indirect_dma_start(right[:, u, :], None, mem.table_r,
                                            bass.IndirectOffsetOnAxis(ap=index[:, u, 1:2], axis=0)).then_inc(right_in[u], 16)

        @block.tensor
        def _(pe):
            def sum_up(tile, u, i):
                pe.wait_ge(attr_in[u], i * 16 + 16)
                pe.wait_ge(act_ready, tile + 1)
                pe.matmul(z[0:Q, slot[u], 0:F], attr[:, u, :], w_e[:], start=True, stop=False)
                pe.wait_ge(left_in[u], i * 16 + 16)
                pe.matmul(z[0:Q, slot[u], 0:F], identity[0:Q, 0:Q], left[:, u, :], start=False, stop=False)
                pe.wait_ge(right_in[u], i * 16 + 16)
                pe.matmul(z[0:Q, slot[u], 0:F], identity[0:Q, 0:Q], right[:, u, :], start=False, stop=True).then_inc(z_ready, 1)

            def turn(i):
                pe.wait_ge(own_ready, i + 1)
                pe.wait_ge(scanned, i + 1)
                for u in range(U):
                    ins = pe.transpose(turned[:, at(u):at(u) + Q], own[:, u * HEADS:(u + 1) * HEADS], identity[0:Q, 0:Q])
                ins.then_inc(turned_ready, 1)

            def turn_back(i):
                pe.wait_ge(scanned, i + 2)
                pe.sem_inc(turns, 1)
                for u in range(U):
                    ins = pe.transpose(back[:, u * HEADS:(u + 1) * HEADS], running[:, u * Q:(u + 1) * Q], identity[0:HEADS, 0:HEADS])
                ins.then_inc(back_ready, 1)

            def add(i):
                pe.wait_ge(parts_ready, i + 1)
                for u in range(U):
                    for a, b in PIECES:
                        ins = pe.matmul(total[:, a:b], parts[:, u, :], mem.dst_hot[:, bass.ds((i * U + u) * N + a, b - a)],
                                        start=False, stop=False, skip_group_check=True)
                ins.then_inc(added, 1)

            pe.sem_inc(z_ready, U)
            pe.wait_ge(zeroed, 3)
            for u in range(U):
                sum_up(u, u, 0)
            def group(i, behind=True):
                t = i * U
                sum_up(t, 0, i)
                sum_up(t + 1, 1, i)
                if behind:
                    add(i - 2)
                sum_up(t + 2, 2, i)
                turn(i - 1)
                sum_up(t + 3, 3, i)
                turn_back(i - 1)
                sum_up(t + 4, 4, i)

            group(1, behind=False)
            with pe.Fori(2, GROUPS) as i:
                group(i)
            add(GROUPS - 2)
            turn(GROUPS - 1)
            turn_back(GROUPS - 1)
            add(GROUPS - 1)

        @block.scalar
        def _(act):
            def scale(tile, u):
                act.wait_ge(z_ready, tile + (U + 1))
                act.activation(fifth[:, slot[u], :], z[0:Q, slot[u], 0:F], ACT.Copy, scale=0.2).then_inc(fifth_ready, 1)

            def copy_scores(i):
                act.wait_ge(scored, i * U + (U + 2))
                act.wait_ge(turned_ready, i + 1)
                act.activation(own[:], scores[:, bass.ds(i * (U * HEADS), U * HEADS)], ACT.Copy).then_inc(own_ready, 1)

            for u in range(U):
                scale(u, u)
            with act.Fori(1, GROUPS) as i:
                for u in range(U):
                    scale(i * U + u, u)
                    if u == 1:
                        copy_scores(i - 1)
            copy_scores(GROUPS - 1)

        @block.vector
        def _(dve):
            def next_index(tile, u):
                dve.tensor_copy(index[:, u, :], mem.ends[:, bass.ds(tile, 1), :].rearrange("p one two -> p (one two)")).then_inc(index_ready, 1)

            def act_on(tile, u):
                dve.wait_ge(fifth_ready, tile + 1)
                dve.wait_ge(weighted_ready, tile + 1)
                dve.tensor_tensor(act_z[:, slot[u], :], z[0:Q, slot[u], 0:F], fifth[:, slot[u], :], ALU.max).then_inc(act_ready, 1)

            def weigh(tile, u):
                dve.wait_ge(act_ready, tile + 3)
                dve.wait_ge(scored, tile + 1)
                dve.tensor_tensor(weighted[:, slot[u], :], act_z[:, slot[u], :], att[0:Q, :], ALU.mult).then_inc(weighted_ready, 1)

            def score(tile, u):
                dve.wait_ge(weighted_ready, tile + 3)
                dve.tensor_reduce(scores[:, bass.ds(tile * HEADS, HEADS)], weighted[:, slot[u], :].rearrange("p (h e) -> p h e", h=HEADS),
                                  AX, ALU.add).then_inc(scored, 1)

            def tile_scores(tile, u, previous=2):
                if previous > 1:
                    score(tile - 2, (u - 2) % U)
                act_on(tile, u)
                next_index(tile + U, u)
                if previous > 0:
                    weigh(tile - 1, (u - 1) % U)

            def compare(i):
                dve.wait_ge(rows_loaded, i * 32 + 32)
                dve.wait_ge(scanned, i + 1)
                dve.tensor_tensor(begin[:], dst_row[:], prev_row[:], ALU.not_equal).then_inc(rows_used, 1)
                dve.tensor_copy(flags[:], last[:, bass.ds(i * U, U)].rearrange("p (u one) -> p u one", one=1).to_broadcast((Q, U, HEADS))
                                ).then_inc(flags_ready, 1)
                dve.wait_ge(rows_used, i + 2)
                dve.tensor_scalar(begin[:], begin[:], NEG, None, ALU.mult).then_inc(begin_ready, 1)

            def scan(i):
                dve.wait_ge(begin_ready, 2 * i + 1)
                dve.wait_ge(turned_ready, i + 2)
                dve.tensor_tensor_scan(running[:, 0:4 * Q], begin[:, 0:4 * Q], turned[:, 0:4 * Q], running[:, G - 1:G],
                                       ALU.add, ALU.max).then_inc(begin_ready, 1)
                dve.wait_ge(begin_ready, 2 * i + 2)
                dve.tensor_tensor_scan(running[:, 4 * Q:G], begin[:, 4 * Q:G], turned[:, 512:512 + Q], running[:, 4 * Q - 1:4 * Q],
                                       ALU.add, ALU.max).then_inc(scanned, 1)

            def split(i):
                dve.wait_ge(added, i + 1)
                dve.wait_ge(flags_ready, i + 1)
                dve.wait_ge(back_ready, i + 1)
                dve.tensor_tensor(run_ends[:], back[:, 0:U * HEADS].rearrange("p (u h) -> p u h", u=U), flags[:], ALU.mult).then_inc(run_ends_ready, 1)
                dve.tensor_copy(parts[:, :, 64:64 + HEADS], flags[:])
                dve.wait_ge(run_ends_ready, i + 1)
                dve.tensor_copy(parts[:, :, 0:HEADS], run_ends[:]).then_inc(hi_ready, 1)

            def split_lo(i):
                dve.wait_ge(hi_ready, i + 1)
                dve.tensor_tensor(parts[:, :, 32:32 + HEADS], run_ends[:], parts[:, :, 0:HEADS], ALU.subtract).then_inc(parts_ready, 1)

            dve.tensor_tensor(last[:], mem.ends[:, 0:T, 1], mem.next_dst[:], ALU.not_equal).then_inc(last_ready, 1)
            for u in range(U):
                next_index(u, u)
            dve.memset(total[:], 0.0).then_inc(zeroed, 1)
            dve.memset(parts[:], 0.0).then_inc(zeroed, 1)
            dve.memset(running[:, G - 1:G], NEG).then_inc(zeroed, 1)
            dve.sem_inc(turned_ready, 1)
            dve.sem_inc(rows_used, 1)
            dve.sem_inc(scanned, 1)
            dve.sem_inc(added, 1)
            for ready in (act_ready, weighted_ready, scored):
                dve.sem_inc(ready, 2)
            dve.wait_ge(last_ready, 1)
            dve.wait_ge(zeroed, 3)
            for u in range(U):
                tile_scores(u, u, previous=u)
            with dve.Fori(1, GROUPS) as i:
                t = i * U
                tile_scores(t, 0)
                compare(i - 1)
                tile_scores(t + 1, 1)
                tile_scores(t + 2, 2)
                scan(i - 1)
                tile_scores(t + 3, 3)
                split(i - 1)
                split_lo(i - 1)
                tile_scores(t + 4, 4)
            score(T - 2, U - 2)
            weigh(T - 1, U - 1)
            score(T - 1, U - 1)
            compare(GROUPS - 1)
            scan(GROUPS - 1)
            split(GROUPS - 1)
            split_lo(GROUPS - 1)
            dve.wait_ge(added, GROUPS + 1)
            dve.tensor_copy(top[:], total[32:32 + HEADS, 0:N]).then_inc(total_ready, 1)
            dve.tensor_scalar(runs[:], total[64:64 + HEADS, 0:N], 1.0, None, ALU.max).then_inc(total_ready, 1)
            dve.tensor_scalar(some, total[64:64 + HEADS, 0:N], 0.0, NEG, ALU.is_equal, ALU.mult).then_inc(total_ready, 1)
            dve.wait_ge(total_ready, 3)
            dve.tensor_tensor(top[:], total[0:HEADS, 0:N], top[:], ALU.add).then_inc(total_ready, 1)
            dve.reciprocal(runs[:], runs[:]).then_inc(total_ready, 1)
            dve.wait_ge(total_ready, 5)
            dve.tensor_tensor(top[:], top[:], runs[:], ALU.mult).then_inc(total_ready, 1)
            dve.wait_ge(total_ready, 6)
            dve.tensor_tensor(top[:], top[:], some, ALU.add)


def gat_loops(nc, mem, att, x, xl, w_r, w_e, loop_ea, top, top_parts, loop_exp):
    with Phase(nc, "selfs") as ph:
        z = ph.ps("z", [P, 2, 1024])
        loop_score, rows = ph.ps("loop_score", [HEADS, 1024]), ph.ps("rows", [Q, NC, HEADS])
        z_sb, act_z = ph.sb("z_sb", [P, KF, N]), ph.sb("act_z", [P, KF, N])
        identity = mem.identity
        z_ready, z_out, act_ready, score_ready, top_ready, below, rows_ready, hi_ready = (ph.sem(n) for n in (
            "z_ready", "z_out", "act_ready", "score_ready", "top_ready", "below", "rows_ready", "hi_ready"))
        block = ph.block()

        @block.tensor
        def _(pe):
            for m in range(KF):
                cols = slice(m * P, (m + 1) * P)
                for a, b in PIECES:
                    for k in range(KF):
                        pe.matmul(z[:, m, a:b], w_r[:, k, cols], x[:, k, a:b], start=(k == 0), stop=False)
                    ins = pe.matmul(z[:, m, a:b], w_e[:, cols], loop_ea[:, a:b], start=False, stop=True)
                ins.then_inc(z_ready, 1)
            pe.wait_ge(act_ready, KF)
            for a, b in PIECES:
                for k in range(KF):
                    ins = pe.matmul(loop_score[:, a:b], att[:, k, :], act_z[:, k, a:b], start=(k == 0), stop=(k == KF - 1))
            ins.then_inc(score_ready, 1)
            pe.wait_ge(top_ready, 1)
            for c in range(NC):
                ins = pe.transpose(rows[:, c, :], top[:, c * Q:(c + 1) * Q], identity[0:HEADS, 0:HEADS])
            ins.then_inc(rows_ready, 1)

        @block.scalar
        def _(act):
            act.wait_ge(below, 1)
            act.activation(loop_exp[:], loop_exp[:], ACT.Exp)

        @block.vector
        def _(dve):
            for m in range(KF):
                dve.wait_ge(z_ready, m + 1)
                dve.tensor_tensor(z_sb[:, m, :], z[:, m, 0:N], xl[:, m, :], ALU.add).then_inc(z_out, 1)
                dve.wait_ge(z_out, m + 1)
                dve.scalar_tensor_tensor(out=act_z[:, m, :], in0=z_sb[:, m, :], scalar=0.2, in1=z_sb[:, m, :],
                                         op0=ALU.mult, op1=ALU.max).then_inc(act_ready, 1)
            dve.wait_ge(score_ready, 1)
            dve.tensor_tensor(top[:], loop_score[:, 0:N], top[:], ALU.max).then_inc(top_ready, 1)
            dve.wait_ge(top_ready, 1)
            dve.tensor_tensor(loop_exp[:], loop_score[:, 0:N], top[:], ALU.subtract).then_inc(below, 1)
            dve.wait_ge(rows_ready, 1)
            dve.tensor_copy(top_parts[:, :, 0, :], rows[:]).then_inc(hi_ready, 1)
            dve.wait_ge(hi_ready, 1)
            dve.tensor_tensor(top_parts[:, :, 1, :], rows[:], top_parts[:, :, 0, :], ALU.subtract)


def gat_messages(nc, mem, scores, top_parts, num, den):
    with Phase(nc, "mess") as ph:
        rows = ph.sb("rows", [Q, U, F])
        index = ph.sb("index", [Q, U], I32)
        one = ph.sb("one", [Q, Q], F16)
        hot = ph.sb("hot", [Q, 3, NC, Q], F16)
        below_hi, below, weight = (ph.sb(n, [Q, U, HEADS]) for n in ("below_hi", "below", "weight"))
        weight_parts = ph.sb("weight_parts", [Q, U, HD + HEADS], F16)
        message, parts = ph.sb("message", [Q, U, F]), ph.sb("parts", [Q, U, 2, F], F16)
        low, high, low_den = ph.ps("low", [P, KF, 512]), ph.ps("high", [P, 512]), ph.ps("low_den", [HD + HEADS, 512])
        turned, top = ph.ps("turned", [Q, 1024]), ph.ps("top", [Q, 2 * HEADS])
        REST = N - 512
        slot = (0, 1, 2, 0, 1)
        (zeroed, one_ready, index_ready, hot_ready, hot_out, top_ready, below_ready, weight_ready) = (ph.sem(n) for n in (
            "zeroed", "one_ready", "index_ready", "hot_ready", "hot_out", "top_ready", "below_ready", "weight_ready"))
        scaled, hi_ready, weight_hi, weight_lo, parts_ready, added, den_out = (ph.sem(n) for n in (
            "scaled", "hi_ready", "weight_hi", "weight_lo", "parts_ready", "added", "den_out"))
        gathers, below_hi_ready = ph.sem("gathers"), ph.sem("below_hi_ready")
        rows_in = [ph.sem(f"rows_in{u}") for u in range(U)]
        block = ph.block()

        def groups(engine, group):
            group(0, True, False)
            with engine.Fori(1, T // U - 1) as i:
                group(i, False, False)
            group(T // U - 1, False, True)

        @block.gpsimd
        def _(pool):
            with pool.Fori(0, T // U) as i:
                t = i * U
                for u in range(U):
                    pool.wait_ge(index_ready, t + u + 1)
                    pool.sem_inc(gathers, 1)
                    pool.indirect_dma_start(rows[:, u, :], None, mem.table,
                                            bass.IndirectOffsetOnAxis(ap=index[:, u:u + 1], axis=0)).then_inc(rows_in[u], 16)

        @block.tensor
        def _(pe):
            def turn(tile):
                for c in range(NC):
                    at = 512 if c == NC - 1 else c * Q
                    ins = pe.matmul(turned[:, at:at + Q], mem.dst_hot[:, bass.ds(tile * N + c * Q, Q)], one[:], start=True, stop=True)
                ins.then_inc(hot_ready, 1)

            def spread(tile, u):
                pe.wait_ge(hot_out, tile + 1)
                for c in range(NC):
                    ins = pe.matmul(top[:], hot[:, slot[u], c, :], top_parts[:, c, :, :].rearrange("p two h -> p (two h)"),
                                    start=(c == 0), stop=(c == NC - 1))
                ins.then_inc(top_ready, 1)

            def add(tile, u):
                def add_to(low_sums, high_sums, w):
                    pe.matmul(low_sums, w, mem.dst_hot[:, bass.ds(tile * N, 512)], start=False, stop=False, skip_group_check=True)
                    return pe.matmul(high_sums, w, mem.dst_hot[:, bass.ds(tile * N + 512, REST)],
                                     start=False, stop=False, skip_group_check=True)

                pe.wait_ge(weight_lo, tile + 1)
                add_to(low_den[:], high[0:HD + HEADS, KF * REST:(KF + 1) * REST], weight_parts[:, u, :])
                pe.wait_ge(hi_ready, tile + 1)
                for part in range(2):
                    if part == 1:
                        pe.wait_ge(parts_ready, tile + 1)
                    for k in range(KF):
                        ins = add_to(low[:, k, :], high[:, k * REST:(k + 1) * REST], parts[:, u, part, k * P:(k + 1) * P])
                ins.then_inc(added, 1)

            def group(i, first, last):
                t = i * U
                for u in range(U):
                    if not (last and u + 1 >= U):
                        pe.wait_ge(below_ready, t + (u + 1))
                        spread(t + (u + 1), (u + 1) % U)
                    if not (last and u + 2 >= U):
                        turn(t + (u + 2))
                    if not (first and u == 0):
                        add(t + (u - 1), (u - 1) % U)

            pe.wait_ge(zeroed, 4)
            pe.wait_ge(one_ready, 1)
            turn(0)
            spread(0, 0)
            turn(1)
            groups(pe, group)
            add(T - 1, U - 1)

        @block.scalar
        def _(act):
            def copy_hot(tile, u):
                act.wait_ge(hot_ready, tile + 1)
                act.activation(hot[:, slot[u], 0:NC - 1, :], turned[:, 0:(NC - 1) * Q].rearrange("p (c e) -> p c e", c=NC - 1), ACT.Copy)
                act.activation(hot[:, slot[u], NC - 1, :], turned[:, 512:512 + Q], ACT.Copy).then_inc(hot_out, 1)

            def weigh(tile, u):
                act.wait_ge(below_ready, tile + 1)
                act.activation(weight[:, u, :], below[:, u, :], ACT.Exp).then_inc(weight_ready, 1)

            def group(i, first, last):
                t = i * U
                for u in range(U):
                    act.wait_ge(weight_ready, t + u + 1)
                    act.activation(weight_parts[:, u, 0:HEADS], weight[:, u, :], ACT.Copy).then_inc(weight_hi, 1)
                    act.wait_ge(scaled, t + (u + 1))
                    act.activation(parts[:, u, 0, :], message[:, u, :], ACT.Copy).then_inc(hi_ready, 1)
                    if not (last and u + 2 >= U):
                        copy_hot(t + (u + 2), (u + 2) % U)
                    if not (last and u + 1 >= U):
                        weigh(t + (u + 1), (u + 1) % U)

            act.activation(one[:], mem.identity[0:Q, 0:Q], ACT.Copy).then_inc(one_ready, 1)
            copy_hot(0, 0)
            weigh(0, 0)
            copy_hot(1, 1)
            groups(act, group)
            act.wait_ge(added, T + U)
            act.activation(num[:, :, 0:512], low[:], ACT.Copy)
            act.activation(num[:, :, 512:N], high[:, 0:KF * REST].rearrange("p (k n) -> p k n", k=KF), ACT.Copy).then_inc(den_out, 1)

        @block.vector
        def _(dve):
            def next_index(tile, u):
                dve.tensor_copy(index[:, u:u + 1], mem.ends[:, bass.ds(tile, 1), 0]).then_inc(index_ready, 1)

            def take_top(tile, u):
                dve.wait_ge(top_ready, tile + 1)
                dve.tensor_tensor(below_hi[:, u, :], scores[:, bass.ds(tile * HEADS, HEADS)], top[:, 0:HEADS], ALU.subtract
                                  ).then_inc(below_hi_ready, 1)
                dve.wait_ge(below_hi_ready, tile + 1)
                dve.tensor_tensor(below[:, u, :], below_hi[:, u, :], top[:, HEADS:2 * HEADS], ALU.subtract).then_inc(below_ready, 1)

            def group(i, first, last):
                t = i * U
                for u in range(U):
                    n = t + u + 1
                    dve.wait_ge(rows_in[u], i * 16 + 16)
                    dve.wait_ge(weight_ready, n)
                    dve.wait_ge(added, n)
                    dve.tensor_tensor(message[:, u, :].rearrange("p (h e) -> p h e", h=HEADS),
                                      rows[:, u, :].rearrange("p (h e) -> p h e", h=HEADS),
                                      weight[:, u, :].rearrange("p (h one) -> p h one", one=1).to_broadcast((Q, HEADS, HD)), ALU.mult
                                      ).then_inc(scaled, 1)
                    dve.wait_ge(weight_hi, n)
                    dve.tensor_tensor(weight_parts[:, u, HD:HD + HEADS], weight[:, u, :], weight_parts[:, u, 0:HEADS], ALU.subtract
                                      ).then_inc(weight_lo, 1)
                    if not (last and u + 1 >= U):
                        take_top(t + (u + 1), (u + 1) % U)
                    dve.wait_ge(scaled, n)
                    next_index(t + (u + U), u)
                    dve.wait_ge(hi_ready, n)
                    dve.tensor_tensor(parts[:, u, 1, :], message[:, u, :], parts[:, u, 0, :], ALU.subtract).then_inc(parts_ready, 1)

            for u in range(U):
                next_index(u, u)
            for p in (low, high, low_den, weight_parts):
                dve.memset(p[:], 0.0).then_inc(zeroed, 1)
            dve.sem_inc(added, U)
            take_top(0, 0)
            groups(dve, group)
            dve.wait_ge(added, T + U)
            dve.wait_ge(den_out, 1)
            dve.tensor_copy(den[:, 0:512], low_den[0:HEADS, :]).then_inc(den_out, 1)
            dve.tensor_copy(den[:, 512:N], high[0:HEADS, KF * REST:(KF + 1) * REST]).then_inc(den_out, 1)
            dve.wait_ge(den_out, 3)
            dve.tensor_tensor(den[:, 0:512], low_den[HD:HD + HEADS, :], den[:, 0:512], ALU.add)
            dve.tensor_tensor(den[:, 512:N], high[HD:HD + HEADS, KF * REST:(KF + 1) * REST], den[:, 512:N], ALU.add)


def gat_finish(nc, mem, d, xl, loop_exp, num, den, bias, out):
    with Phase(nc, "finish") as ph:
        spread = mem.spread
        wide, inverse = ph.ps("wide", [P, KF, 1024]), ph.ps("inverse", [P, KF, 1024])
        den_ready, wide_ready, inverse_ready, scaled = (ph.sem(n) for n in ("den_ready", "wide_ready", "inverse_ready", "scaled"))
        block = ph.block()

        @block.tensor
        def _(pe):
            for k in range(KF):
                for a, b in PIECES:
                    ins = pe.matmul(wide[:, k, a:b], spread[:, k * P:(k + 1) * P], loop_exp[:, a:b], start=True, stop=True)
            ins.then_inc(wide_ready, 1)
            pe.wait_ge(den_ready, 2)
            for k in range(KF):
                for a, b in PIECES:
                    ins = pe.matmul(inverse[:, k, a:b], spread[:, k * P:(k + 1) * P], den[:, a:b], start=True, stop=True)
            ins.then_inc(inverse_ready, 1)

        @block.vector
        def _(dve):
            dve.tensor_tensor(den[:], den[:], loop_exp[:], ALU.add).then_inc(den_ready, 1)
            dve.wait_ge(den_ready, 1)
            dve.reciprocal(den[:], den[:]).then_inc(den_ready, 1)
            dve.wait_ge(wide_ready, 1)
            for k in range(KF):
                dve.tensor_tensor(out[:, k, :], wide[:, k, 0:N], xl[:, k, :], ALU.mult).then_inc(scaled, 1)
            for k in range(KF):
                dve.wait_ge(scaled, k + 1)
                dve.tensor_tensor(out[:, k, :], out[:, k, :], num[:, k, :], ALU.add).then_inc(scaled, 1)
            dve.wait_ge(inverse_ready, 1)
            for k in range(KF):
                dve.wait_ge(scaled, KF + k + 1)
                dve.tensor_tensor(out[:, k, :], out[:, k, :], inverse[:, k, 0:N], ALU.mult).then_inc(scaled, 1)
            for k in range(KF):
                dve.wait_ge(scaled, 2 * KF + k + 1)
                dve.tensor_scalar(out[:, k, :], out[:, k, :], bias[:, k:k + 1], None, ALU.add).then_inc(scaled, 1)


def batch_norm_step(nc, mem, y, gain, shift, x, out):
    with Phase(nc, "bnstep") as ph:
        mean, total, scale = ph.sb("mean", [P, KF]), ph.sb("total", [P, KF]), ph.sb("scale", [P, KF])
        squares = ph.sb("squares", [P, KF, N])
        centred, squared, var_ready, std_ready, chain = (ph.sem(n) for n in (
            "centred", "squared", "var_ready", "std_ready", "chain"))
        block = ph.block()

        @block.scalar
        def _(act):
            for k in range(KF):
                act.wait_ge(centred, k + 1)
                act.activation(squares[:, k, :], y[:, k, :], ACT.Square).then_inc(squared, 1)
            act.wait_ge(var_ready, 1)
            act.activation(scale[:], total[:], ACT.Sqrt, bias=mem.eps[:, 0:1], scale=1.0 / N).then_inc(std_ready, 1)

        @block.vector
        def _(dve):
            count = [0]

            def link(ins):
                count[0] += 1
                ins.then_inc(chain, 1)
                dve.wait_ge(chain, count[0])

            link(dve.tensor_reduce(mean[:], y[:], AX, ALU.add))
            link(dve.tensor_scalar(mean[:], mean[:], 1.0 / N, None, ALU.mult))
            for k in range(KF):
                dve.tensor_scalar(y[:, k, :], y[:, k, :], mean[:, k:k + 1], None, ALU.subtract).then_inc(centred, 1)
            dve.wait_ge(squared, KF)
            dve.tensor_reduce(total[:], squares[:], AX, ALU.add).then_inc(var_ready, 1)
            dve.wait_ge(std_ready, 1)
            link(dve.reciprocal(scale[:], scale[:]))
            link(dve.tensor_tensor(scale[:], scale[:], gain, ALU.mult))
            for k in range(KF):
                link(dve.tensor_scalar(y[:, k, :], y[:, k, :], scale[:, k:k + 1], shift[:, k:k + 1], ALU.mult, ALU.add))
                link(dve.scalar_tensor_tensor(out=squares[:, k, :], in0=y[:, k, :], scalar=0.01, in1=y[:, k, :],
                                              op0=ALU.mult, op1=ALU.max))
                link(dve.tensor_tensor(out[:, k, :], x[:, k, :], squares[:, k, :], ALU.add))


def gat_weights(nc, d, g, pfx):
    weights = (g.sb("w_l", [P, KF, F]), g.sb("w_r", [P, KF, F]), g.sb("w_e", [EF, F]),
               g.sb("att", [P, F]),
               g.sb("att_cols", [P, KF, HEADS]))
    of = (d[pfx + "_Wl"], d[pfx + "_Wr"], d[pfx + "_We"], d[pfx + "_att"].partition_broadcast(P), d[pfx + "_att_cols"])
    return weights, start_load(nc, [(to[:], w) for to, w in zip(weights, of)])


def gat(nc, mem, d, weights, bias, x, loop_ea, out):
    with Phase(nc, "gat") as g:
        scores = g.sb("scores", [Q, T * HEADS])
        top, loop_exp = g.sb("top", [HEADS, N]), g.sb("loop_exp", [HEADS, N])
        w_l, w_r, w_e, att, att_cols = weights
        xl = g.sb("xl", [P, KF, N])
        with Phase(nc, "tables") as g2:
            nodes_l, nodes_r = g2.sb("nodes_l", [Q, NC, F]), g2.sb("nodes_r", [Q, NC, F])
            written = []
            for w, nodes, table in ((w_l, nodes_l, mem.table), (w_r, nodes_r, mem.table_r)):
                node_major(nc, x, w, nodes, F)
                written.append(start_load(nc, [(table.rearrange("(c p) f -> p c f", p=Q), nodes[:])]))
            dense(nc, x, w_l, xl, KF, KF, ACT.Identity)
            for started in written:
                finish_load(nc, started)
        gat_scores(nc, mem, d, w_e, att, scores, top)
        num, den = g.sb("num", [P, KF, N]), g.sb("den", [HEADS, N])
        top_parts = g.sb("top_parts", [Q, NC, 2, HEADS], F16)
        gat_loops(nc, mem, att_cols, x, xl, w_r, w_e, loop_ea, top, top_parts, loop_exp)
        gat_messages(nc, mem, scores, top_parts, num, den)
        gat_finish(nc, mem, d, xl, loop_exp, num, den, bias, out)


def layer_gat(nc, mem, d):
    with Phase(nc, "l3") as g:
        h, y = g.sb("h", [P, KF, N]), g.sb("y", [P, KF, N])
        w1, w2 = g.sb("w1", [P, KF, 4 * F]), g.sb("w2", [P, 4 * KF, F])
        with Phase(nc, "gats") as g2:
            loop_ea = g2.sb("loop_ea", [EF, N])
            with Phase(nc, "first") as g3:
                weights, started = gat_weights(nc, d, g3, "g1")
                loop_attributes(nc, mem, d, loop_ea)
                finish_load(nc, started)
                gat(nc, mem, d, weights, vec(mem, 'L3_gnn_g1_b'), mem.x, loop_ea, y)
            with Phase(nc, "second") as g3:
                weights, started = gat_weights(nc, d, g3, "g2")
                batch_norm_step(nc, mem, y, vec(mem, 'L3_gnn_n1_g'), vec(mem, 'L3_gnn_n1_b'), mem.x, h)
                finish_load(nc, started)
                recycle(nc)
                started = start_load(nc, [(w1[:], d["ff_w1"]), (w2[:], d["ff_w2"])])
                gat(nc, mem, d, weights, vec(mem, 'L3_gnn_g2_b'), h, loop_ea, y)
            finish_load(nc, started)
            batch_norm_step(nc, mem, y, vec(mem, 'L3_gnn_n2_g'), vec(mem, 'L3_gnn_n2_b'), h, h)
        recycle(nc)
        with Phase(nc, "ff") as g2:
            hidden = g2.sb("hidden", [P, 4 * KF, N])
            dense(nc, h, w1, hidden, KF, 4 * KF, ACT.Relu, vec(mem, 'L3_gnn_ff_b1'))
            dense(nc, hidden, w2, y, 4 * KF, KF, ACT.Identity, vec(mem, 'L3_gnn_ff_b2'))
        batch_norm_step(nc, mem, y, vec(mem, 'L3_gnn_n3_g'), vec(mem, 'L3_gnn_n3_b'), h, h)
        add_into(nc, mem.x, mem.x, h)
    layer_norm(nc, mem, mem.x, mem.x)


def layer_recurrent(nc, mem, d):
    with Phase(nc, "l0") as g:
        mem.xe_parts = g.sb("xe_parts", [P, STEPS + UL], F16)
        mem.h_all = g.sb("h_all", [P, KF, STEPS])
        raw = (g.sb("w_rec", [P, KF, 4 * F]), g.sb("w_in", [P, 12, P]), g.sb("w_in2", [P, 12, P]), g.sb("rows", [P, 5]))
        started = start_load(nc, [(to[:], d[of]) for to, of in zip(raw, ("w_rec", "w_in", "w_in2", "part_rows"))])
        gcn_input(nc, mem, d)
        finish_load(nc, started)
        lstms(nc, mem, raw)
        residual_scaled(nc, mem.x, mem.h_all, mem.x, 1.0 / H_SCALE, at=LAG)
    layer_norm(nc, mem, mem.x, mem.x)


def build(nc, d, out, layers=(0, 1, 2, 3)):
    Phase.used.clear()
    with Phase(nc, "mem") as top:
        mem = Memory()
        mem.ends = top.sb("ends", [Q, T + U, 2], I32)
        mem.next_dst = top.sb("next_dst", [Q, T], I32)
        mem.identity, mem.spread = top.sb("identity", [P, P]), top.sb("spread", [HEADS, F])
        mem.averager, mem.vecs, mem.eps = top.sb("averager", [P, P]), top.sb("vecs", [P, N_VEC]), top.sb("eps", [P, 1])
        mem.dst_hot = top.sb("dst_hot", [Q, T * N], F16)
        mem.counts = top.sb("counts", [Q, NC, N])
        mem.x = top.sb("x", [P, KF, N])
        mem.table, mem.table_r = (nc.dram_tensor(n, (N, F), F32).ap() for n in ("table", "table_r"))
        setup(nc, mem, d)
        for n, layer in enumerate((layer_recurrent, layer_gin, layer_attention, layer_gat)):
            if n in layers:
                layer(nc, mem, d)
                recycle(nc)
        store(nc, mem, d, out)


def store(nc, mem, d, out):
    with Phase(nc, "store") as ph:
        nodes = ph.sb("nodes", [Q, NC, F])
        turn_nodes(nc, mem, mem.x, nodes)
        with Phase(nc, "out") as p2:
            stored = p2.sem("stored")
            block = p2.block()

            @block.sync
            def _(sp):
                sp.dma_start(out.rearrange("(c p) f -> p c f", p=Q), nodes[:]).then_inc(stored, 16)
                sp.wait_ge(stored, 16)



def lay_out(inputs):
    import numpy as np

    x = {k: np.asarray(v) for k, v in inputs.items()}
    blocks = lambda w: np.ascontiguousarray(w.reshape(-1, P, w.shape[-1]).transpose(1, 0, 2))
    a = {}
    a["x"] = blocks(x["x"].T)
    a["x_table"] = x["x"]
    a["dst_row"] = x["dst"].reshape(1, E)
    a["prev_row"] = np.concatenate([[-1], x["dst"][:-1]]).astype(np.int32).reshape(1, E)
    a["dst_next"] = np.ascontiguousarray(np.concatenate([x["dst"][1:], [-1]]).astype(np.int32).reshape(T, Q).T)
    a["ends"] = np.zeros((Q, T + U, 2), np.int32)
    a["ends"][:, 0:T, 0], a["ends"][:, 0:T, 1] = x["src"].reshape(T, Q).T, x["dst"].reshape(T, Q).T
    a["averager"] = np.full((P, P), 1.0 / F, np.float32)
    a["identity"] = np.eye(P, dtype=np.float32)
    a["vecs"] = np.concatenate([x[v].reshape(-1, P).T for v in VECS], axis=1)
    a["w_gcn"] = blocks(x["L0_gnn_W_gcn"].T)
    a["w_enc"], a["b_enc"] = np.zeros((P, KF, P), np.float32), np.zeros((P, 2), np.float32)
    for rows in (XE_HI, XE_LO):
        a["w_enc"][:, :, rows] = blocks(x["L0_gnn_Wih_e"].T)
        a["b_enc"][rows, 0], a["b_enc"][rows, 1] = x["L0_gnn_bih_e"], x["L0_gnn_bhh_e"]
    a["b_enc"][list(ONES), 0] = H_SCALE
    a["w_rec"] = blocks(x["L0_gnn_Whh_d"].T)
    w_in = np.zeros((P, 12, P), np.float32)
    w_in2 = np.zeros((P, 12, P), np.float32)
    copies = (0, HE, 32, 32 + HE)
    for gate in range(4):
        for j in range(KF):
            m = slice(gate * F + j * P, gate * F + (j + 1) * P)
            for r in copies:
                w_in[r:r + HE, 3 * gate + j, :] = x["L0_gnn_Wih_d"][m].T
            for r in ONES:
                w_in[r, 3 * gate + j, :] = x["L0_gnn_bih_d"][m]
                w_in2[r, 3 * gate + j, :] = x["L0_gnn_bhh_d"][m]
        for c in copies:
            for r in copies:
                w_in[r:r + HE, 3 * gate + 2, c:c + HE] = x["L0_gnn_Whh_e"][gate * HE:(gate + 1) * HE].T
            for rows in (XE_HI, XE_LO):
                for j in range(HE):
                    w_in[rows[gate * HE + j], 3 * gate + 2, c + j] = H_SCALE
    a["w_in"], a["w_in2"] = w_in, w_in2
    low_rows = [*range(HE, 2 * HE), *range(32 + HE, 32 + 2 * HE), ONES[1]]
    rows = np.zeros((P, 5), np.float32)
    rows[:, 0] = rows[:, 4] = 1.0
    rows[low_rows, 0], rows[low_rows, 1] = 0.0, 1.0
    rows[XE_LO, 2] = 1.0
    rows[XE_HI + list(ONES), 3] = 1.0
    rows[list(ONES), 4] = 0.0
    a["part_rows"] = rows
    a["edge_attr"] = np.ascontiguousarray(x["edge_attr_256"].reshape(T, Q, F).transpose(1, 0, 2)).reshape(Q, T * F)
    a["gin_w1"], a["gin_w2"] = blocks(x["L1_gnn_W1"].T), blocks(x["L1_gnn_W2"].T)
    for w in ("q", "k", "v"):
        a["att_w" + w] = blocks(x["L2_gnn_W" + w])
    a["att_wo"], a["att_w1"], a["att_w2"] = (blocks(x["L2_gnn_" + n]) for n in ("Wo_w", "ffn_w1", "ffn_w2"))
    small = x["edge_attr_32"]
    a["small_attr"] = np.ascontiguousarray(small.reshape(T, Q, EF).transpose(1, 0, 2)).reshape(Q, T * EF)
    a["small_attr_t"] = small.T
    for g in ("g1", "g2"):
        att = x[f"L3_gnn_{g}_att"]
        a[g + "_Wl"], a[g + "_Wr"], a[g + "_We"] = blocks(x[f"L3_gnn_{g}_Wl"]), blocks(x[f"L3_gnn_{g}_Wr"]), x[f"L3_gnn_{g}_We"]
        a[g + "_att"] = att.reshape(1, F)
        cols = np.zeros((HEADS, HD, HEADS), np.float32)
        for h in range(HEADS):
            cols[h, :, h] = att[h]
        a[g + "_att_cols"] = blocks(cols.reshape(F, HEADS))
    a["ff_w1"], a["ff_w2"] = blocks(x["L3_gnn_ff_W1"]), blocks(x["L3_gnn_ff_W2"])
    a["head_rows"] = np.repeat(np.eye(HEADS, dtype=np.float32), HD, axis=1)
    a["minus_head"] = np.zeros((2, HD, HEADS, Q), np.float32)
    for h in range(HEADS):
        a["minus_head"][:, h, h, :] = -1.0
    a["minus_head"] = a["minus_head"].reshape(2 * HD, HEADS, Q)
    select = np.zeros((4, HD, 4, 4, HD), np.float32)
    for kind, groups in enumerate(((0, 1), (2, 3), (0, 2), (1, 3))):
        for group in groups:
            select[:, range(HD), kind, group, range(HD)] = 1.0
    a["selectors"] = select.reshape(P, 4, P)
    return {k: np.ascontiguousarray(v) for k, v in a.items()}


def kernel(**inputs):
    import numpy as np
    import concourse.bacc as bacc
    from concourse.bass_utils import run_bass_kernel_spmd

    nc = bacc.Bacc("TRN2", target_bir_lowering=False, num_devices=1)
    arrays = lay_out(inputs)
    d = {k: nc.dram_tensor(k, a.shape, mybir.dt.from_np(a.dtype), kind="ExternalInput").ap() for k, a in arrays.items()}
    out = nc.dram_tensor("out", (N, F), F32, kind="ExternalOutput").ap()
    build(nc, d, out)
    r = run_bass_kernel_spmd(nc, [arrays], core_ids=[0])
    return r.results[0]["out"]
```
